# Optimizing a Trainium2 kernel written in Bass

```python
import numpy as np
import jax
import jax.numpy as jnp

def _softmax(x, axis=-1):
    return jax.nn.softmax(x, axis=axis)

def _gelu(x):
    return jax.nn.gelu(x, approximate=True)

def _silu(x):
    return jax.nn.silu(x)

def _sigmoid(x):
    return jax.nn.sigmoid(x)

def _layernorm(x, axis=-1, eps=1e-05):
    m = jnp.mean(x, axis=axis, keepdims=True)
    v = jnp.var(x, axis=axis, keepdims=True)
    return (x - m) / jnp.sqrt(v + eps)

def _scatter_add(tgt, idx, src, axis=0):
    return tgt.at[idx].add(src)

def _segment_sum(src, seg, n):
    return jax.ops.segment_sum(src, seg, n)
kernel_name = 'mk_lm_tower_d2_tok_ids256_r4_e9d3c4'

def setup_inputs(seed: int=0):
    np.random.seed(seed)
    _w = jnp.asarray

    def _rec_inputs():
        import jax
        import jax.numpy as jnp
        _rk = jax.random.key(seed)
        x = jax.random.randint(jax.random.fold_in(_rk, 1), (32, 128), 0, 2048, jnp.int32)
        return x
    x = _rec_inputs()

    def _L0_tok_setup():
        import jax, jax.numpy as jnp
        import numpy as np
        D = 64
        NLEAF = 8
        N_INTERNAL = 7
        N_STRUCT = 2048
        COMP_V = 256
        OP_V = 64
        EPS = 1e-05

        def _layer_norm(x, gamma, beta):
            mu = jnp.mean(x, axis=-1, keepdims=True)
            var = jnp.mean(jnp.square(x - mu), axis=-1, keepdims=True)
            return (x - mu) * jax.lax.rsqrt(var + EPS) * gamma + beta
        key = jax.random.key(seed)
        ks = jax.random.split(key, 8)
        struct_indices = jax.random.randint(ks[0], (32, 512), 0, N_STRUCT)
        leaf_ids = jax.random.randint(ks[1], (N_STRUCT, NLEAF), 0, COMP_V).astype(jnp.int32)
        op_ids = jax.random.randint(ks[2], (N_STRUCT, N_INTERNAL), 0, OP_V).astype(jnp.int32)
        comp_emb = jax.random.normal(ks[3], (COMP_V, D), dtype=jnp.float32)
        op_emb = jax.random.normal(ks[4], (OP_V, D), dtype=jnp.float32)
        W_bin = jax.random.normal(ks[5], (3 * D, D), dtype=jnp.float32) / np.sqrt(3 * D)
        b_bin = jnp.zeros((D,), dtype=jnp.float32)
        gamma = jnp.ones((D,), dtype=jnp.float32)
        beta = jnp.zeros((D,), dtype=jnp.float32)
        return {'struct_indices': struct_indices, 'leaf_ids': leaf_ids, 'op_ids': op_ids, 'comp_emb': comp_emb, 'op_emb': op_emb, 'W_bin': W_bin, 'b_bin': b_bin, 'gamma': gamma, 'beta': beta}
    _L0_tok_all = _L0_tok_setup()
    _L0_tok_in = {k: v for k, v in _L0_tok_all.items() if k in ('leaf_ids', 'op_ids', 'comp_emb', 'op_emb', 'W_bin', 'b_bin', 'gamma', 'beta')}
    del _L0_tok_all

    def _L0_attn_setup():
        import jax, jax.numpy as jnp
        import numpy as np
        IN_C = 64
        HID_C = 64
        HEADS = 8
        SCALE = 1.0 / np.sqrt(HID_C / HEADS).astype(np.float32)
        key = jax.random.key(seed)
        k_v, k_q, k_k, k_w, k_o, k_b = jax.random.split(key, 6)
        B, S = (4, 512)
        lim_in = 1.0 / np.sqrt(IN_C)
        lim_out = 1.0 / np.sqrt(IN_C * HEADS)
        v = jax.random.normal(k_v, (B, S, IN_C), dtype=jnp.float32)
        WQ = jax.random.uniform(k_q, (IN_C, IN_C * HEADS), jnp.float32, -lim_in, lim_in)
        WK = jax.random.uniform(k_k, (IN_C, IN_C * HEADS), jnp.float32, -lim_in, lim_in)
        WV = jax.random.uniform(k_w, (IN_C, IN_C * HEADS), jnp.float32, -lim_in, lim_in)
        Wout = jax.random.uniform(k_o, (IN_C * HEADS, HID_C), jnp.float32, -lim_out, lim_out)
        bout = jax.random.uniform(k_b, (HID_C,), jnp.float32, -lim_out, lim_out)
        return {'v': v, 'WQ': WQ, 'WK': WK, 'WV': WV, 'Wout': Wout, 'bout': bout}
    _L0_attn_all = _L0_attn_setup()
    _L0_attn_in = {k: v for k, v in _L0_attn_all.items() if k in ('WQ', 'WK', 'WV', 'Wout', 'bout')}
    del _L0_attn_all

    def _L0_ffn_setup():
        import jax, jax.numpy as jnp
        import numpy as np
        DIM = 64
        HEADS = 8
        NUM_KEYS = 64
        NUM_KV = NUM_KEYS ** 2
        PK_TOPK = 16
        FINAL_TOPK = 16
        DIM_KEY = DIM // 2
        P = 2

        def _pk(x, Wq_pk, pk_keys):
            b, n, _ = x.shape
            q = (x @ Wq_pk).reshape(b, n, P, HEADS, DIM_KEY).transpose(2, 0, 1, 3, 4)
            sim = jnp.einsum('pbnhd,pkhd->pbnhk', q, pk_keys)
            scores, idx = jax.lax.top_k(sim, PK_TOPK)
            idx0 = idx[0]
            idx1 = idx[1] * NUM_KEYS
            index = (idx0[..., :, None] + idx1[..., None, :]).reshape(b, n, HEADS, PK_TOPK * PK_TOPK)
            score = (scores[0][..., :, None] + scores[1][..., None, :]).reshape(b, n, HEADS, PK_TOPK * PK_TOPK)
            final_scores, pk_idx = jax.lax.top_k(score, FINAL_TOPK)
            final_indices = jnp.take_along_axis(index, pk_idx, axis=-1)
            final_scores = jax.nn.softmax(final_scores, axis=-1)
            return (final_scores, final_indices)
        key = jax.random.key(seed)
        ks = jax.random.split(key, 7)
        b, n = (2, 256)
        std = 0.02
        x = jax.random.normal(ks[0], (b, n, DIM), dtype=jnp.float32)
        Wq_pk = jax.random.normal(ks[1], (DIM, P * HEADS * DIM_KEY), dtype=jnp.float32) * std
        pk_keys = jax.random.normal(ks[2], (P, NUM_KEYS, HEADS, DIM_KEY), dtype=jnp.float32) * std
        Wq = jax.random.normal(ks[3], (DIM, HEADS * DIM), dtype=jnp.float32) * std
        keys_table = jax.random.normal(ks[4], (NUM_KV * HEADS, DIM), dtype=jnp.float32) * std
        values_table = jax.random.normal(ks[5], (NUM_KV * HEADS, DIM), dtype=jnp.float32) * std
        Wo = jax.random.normal(ks[6], (DIM * HEADS, DIM), dtype=jnp.float32) * std
        return {'x': x, 'Wq_pk': Wq_pk, 'pk_keys': pk_keys, 'Wq': Wq, 'keys_table': keys_table, 'values_table': values_table, 'Wo': Wo}
    _L0_ffn_all = _L0_ffn_setup()
    _L0_ffn_in = {k: v for k, v in _L0_ffn_all.items() if k in ('Wq_pk', 'pk_keys', 'Wq', 'keys_table', 'values_table', 'Wo')}
    del _L0_ffn_all

    def _L1_attn_setup():
        import jax, jax.numpy as jnp
        import numpy as np
        B, T, C, HR = (8, 1024, 64, 4)
        N_LAYER, LAYER_ID = (12, 3)
        HID = HR * C

        def _fancy_decay_first():
            r01 = LAYER_ID / (N_LAYER - 1)
            h = np.arange(C, dtype=np.float32)
            decay = -5.0 + 8.0 * (h / (C - 1)) ** (0.7 + 1.3 * r01)
            zig = (np.arange(1, C + 1) % 3 - 1).astype(np.float32) * 0.5
            first = np.float32(np.log(0.3)) + zig
            return (jnp.asarray(decay, jnp.float32), jnp.asarray(first, jnp.float32))

        def _ln(x, g, b):
            m = jnp.mean(x, axis=-1, keepdims=True)
            v = jnp.var(x, axis=-1, keepdims=True)
            return (x - m) * jax.lax.rsqrt(v + 1e-05) * g + b

        def _wkv(w, u, k, v):
            Bb, Tt, Cc = k.shape
            kT = jnp.swapaxes(k, 0, 1)
            vT = jnp.swapaxes(v, 0, 1)

            def step(carry, kv):
                p, q, o = carry
                kt, vt = kv
                no = jnp.maximum(o, u + kt)
                A = jnp.exp(o - no)
                E = jnp.exp(u + kt - no)
                y = (A * p + E * vt) / (A * q + E)
                no2 = jnp.maximum(w + o, kt)
                A2 = jnp.exp(w + o - no2)
                E2 = jnp.exp(kt - no2)
                return ((A2 * p + E2 * vt, A2 * q + E2, no2), y)
            init = (jnp.zeros((Bb, Cc), k.dtype), jnp.zeros((Bb, Cc), k.dtype), jnp.full((Bb, Cc), -1e+38, k.dtype))
            _, yT = jax.lax.scan(step, init, (kT, vT))
            return jnp.swapaxes(yT, 0, 1)
        key = jax.random.key(seed)
        ks = jax.random.split(key, 12)
        s = 0.02
        decay, first = _fancy_decay_first()
        return {'x': jax.random.normal(ks[0], (B, T, C), jnp.float32), 'Wk': jax.random.normal(ks[1], (C, C), jnp.float32) * s, 'Wv': jax.random.normal(ks[2], (C, C), jnp.float32) * s, 'Wr': jax.random.normal(ks[3], (C, C), jnp.float32) * s, 'Wo': jax.random.normal(ks[4], (C, C), jnp.float32) * s, 'Wk_ffn': jax.random.normal(ks[5], (C, HID), jnp.float32) * s, 'Wv_ffn': jax.random.normal(ks[6], (HID, C), jnp.float32) * s, 'Wr_ffn': jax.random.normal(ks[7], (C, C), jnp.float32) * s, 'g1': 1.0 + 0.1 * jax.random.normal(ks[8], (C,), jnp.float32), 'b1': 0.1 * jax.random.normal(ks[9], (C,), jnp.float32), 'g2': 1.0 + 0.1 * jax.random.normal(ks[10], (C,), jnp.float32), 'b2': 0.1 * jax.random.normal(ks[11], (C,), jnp.float32), 'spatial_decay': decay, 'spatial_first': first}
    _L1_attn_all = _L1_attn_setup()
    _L1_attn_in = {k: v for k, v in _L1_attn_all.items() if k in ('Wk', 'Wv', 'Wr', 'Wo', 'Wk_ffn', 'Wv_ffn', 'Wr_ffn', 'g1', 'b1', 'g2', 'b2', 'spatial_decay', 'spatial_first')}
    del _L1_attn_all

    def _L1_ffn_setup():
        import math
        import jax, jax.numpy as jnp
        import numpy as np
        CAPACITY_FACTOR = 1.25
        key = jax.random.key(seed)
        ks = jax.random.split(key, 5)
        B, L, D, F, E = (8, 2048, 64, 256, 8)
        h = jax.random.normal(ks[0], (B, L, D), dtype=jnp.float32)
        gate_w = jax.random.normal(ks[1], (D, E), dtype=jnp.float32) * 0.02
        gate_b = jnp.zeros((E,), dtype=jnp.float32)
        w1 = jax.random.normal(ks[2], (E, D, F), dtype=jnp.float32) * (1.0 / math.sqrt(D))
        b1 = jnp.zeros((E, F), dtype=jnp.float32)
        w2 = jax.random.normal(ks[3], (E, F, D), dtype=jnp.float32) * (1.0 / math.sqrt(F))
        b2 = jnp.zeros((E, D), dtype=jnp.float32)
        return {'h': h, 'gate_w': gate_w, 'gate_b': gate_b, 'w1': w1, 'b1': b1, 'w2': w2, 'b2': b2}
    _L1_ffn_all = _L1_ffn_setup()
    _L1_ffn_in = {k: v for k, v in _L1_ffn_all.items() if k in ('gate_w', 'gate_b', 'w1', 'b1', 'w2', 'b2')}
    del _L1_ffn_all
    return {'x': x, 'L0_tok_leaf_ids': _L0_tok_in['leaf_ids'], 'L0_tok_op_ids': _L0_tok_in['op_ids'], 'L0_tok_comp_emb': _L0_tok_in['comp_emb'], 'L0_tok_op_emb': _L0_tok_in['op_emb'], 'L0_tok_W_bin': _L0_tok_in['W_bin'], 'L0_tok_b_bin': _L0_tok_in['b_bin'], 'L0_tok_gamma': _L0_tok_in['gamma'], 'L0_tok_beta': _L0_tok_in['beta'], 'L0_attn_WQ': _L0_attn_in['WQ'], 'L0_attn_WK': _L0_attn_in['WK'], 'L0_attn_WV': _L0_attn_in['WV'], 'L0_attn_Wout': _L0_attn_in['Wout'], 'L0_attn_bout': _L0_attn_in['bout'], 'L0_ffn_Wq_pk': _L0_ffn_in['Wq_pk'], 'L0_ffn_pk_keys': _L0_ffn_in['pk_keys'], 'L0_ffn_Wq': _L0_ffn_in['Wq'], 'L0_ffn_keys_table': _L0_ffn_in['keys_table'], 'L0_ffn_values_table': _L0_ffn_in['values_table'], 'L0_ffn_Wo': _L0_ffn_in['Wo'], 'L1_attn_Wk': _L1_attn_in['Wk'], 'L1_attn_Wv': _L1_attn_in['Wv'], 'L1_attn_Wr': _L1_attn_in['Wr'], 'L1_attn_Wo': _L1_attn_in['Wo'], 'L1_attn_Wk_ffn': _L1_attn_in['Wk_ffn'], 'L1_attn_Wv_ffn': _L1_attn_in['Wv_ffn'], 'L1_attn_Wr_ffn': _L1_attn_in['Wr_ffn'], 'L1_attn_g1': _L1_attn_in['g1'], 'L1_attn_b1': _L1_attn_in['b1'], 'L1_attn_g2': _L1_attn_in['g2'], 'L1_attn_b2': _L1_attn_in['b2'], 'L1_attn_spatial_decay': _L1_attn_in['spatial_decay'], 'L1_attn_spatial_first': _L1_attn_in['spatial_first'], 'L1_ffn_gate_w': _L1_ffn_in['gate_w'], 'L1_ffn_gate_b': _L1_ffn_in['gate_b'], 'L1_ffn_w1': _L1_ffn_in['w1'], 'L1_ffn_b1': _L1_ffn_in['b1'], 'L1_ffn_w2': _L1_ffn_in['w2'], 'L1_ffn_b2': _L1_ffn_in['b2']}

def reference(x, L0_tok_leaf_ids, L0_tok_op_ids, L0_tok_comp_emb, L0_tok_op_emb, L0_tok_W_bin, L0_tok_b_bin, L0_tok_gamma, L0_tok_beta, L0_attn_WQ, L0_attn_WK, L0_attn_WV, L0_attn_Wout, L0_attn_bout, L0_ffn_Wq_pk, L0_ffn_pk_keys, L0_ffn_Wq, L0_ffn_keys_table, L0_ffn_values_table, L0_ffn_Wo, L1_attn_Wk, L1_attn_Wv, L1_attn_Wr, L1_attn_Wo, L1_attn_Wk_ffn, L1_attn_Wv_ffn, L1_attn_Wr_ffn, L1_attn_g1, L1_attn_b1, L1_attn_g2, L1_attn_b2, L1_attn_spatial_decay, L1_attn_spatial_first, L1_ffn_gate_w, L1_ffn_gate_b, L1_ffn_w1, L1_ffn_b1, L1_ffn_w2, L1_ffn_b2):
    import jax
    import jax.numpy as jnp

    def _L0_tok_ref(struct_indices, leaf_ids, op_ids, comp_emb, op_emb, W_bin, b_bin, gamma, beta):
        import jax, jax.numpy as jnp
        import numpy as np
        D = 64
        NLEAF = 8
        N_INTERNAL = 7
        N_STRUCT = 2048
        COMP_V = 256
        OP_V = 64
        EPS = 1e-05

        def _layer_norm(x, gamma, beta):
            mu = jnp.mean(x, axis=-1, keepdims=True)
            var = jnp.mean(jnp.square(x - mu), axis=-1, keepdims=True)
            return (x - mu) * jax.lax.rsqrt(var + EPS) * gamma + beta
        h = _layer_norm(comp_emb[leaf_ids], gamma, beta)
        off = 0
        while h.shape[1] > 1:
            n = h.shape[1] // 2
            ops = op_emb[op_ids[:, off:off + n]]
            cat = jnp.concatenate([ops, h[:, 0::2], h[:, 1::2]], axis=-1)
            h = _layer_norm(jnp.einsum('nkc,cd->nkd', cat, W_bin) + b_bin, gamma, beta)
            off += n
        root = h[:, 0]
        out = root[struct_indices]
        mask = (struct_indices > 1)[..., None]
        return jnp.where(mask, out, jnp.zeros((), dtype=out.dtype))

    def _L0_attn_ref(v, WQ, WK, WV, Wout, bout):
        import jax, jax.numpy as jnp
        import numpy as np
        IN_C = 64
        HID_C = 64
        HEADS = 8
        SCALE = 1.0 / np.sqrt(HID_C / HEADS).astype(np.float32)
        B, S, C = v.shape
        H = HEADS
        q = (v @ WQ).reshape(B, S, H, C)
        k = (v @ WK).reshape(B, S, H, C)
        val = (v @ WV).reshape(B, S, H, C)
        scores = jnp.einsum('bshc,bthc->bsth', q, k) * SCALE
        A = jax.nn.softmax(scores, axis=2)
        u = jnp.einsum('bsth,bthc->bshc', A, val).reshape(B, S, H * C)
        return u @ Wout + bout

    def _L0_ffn_ref(x, Wq_pk, pk_keys, Wq, keys_table, values_table, Wo):
        import jax, jax.numpy as jnp
        import numpy as np
        DIM = 64
        HEADS = 8
        NUM_KEYS = 64
        NUM_KV = NUM_KEYS ** 2
        PK_TOPK = 16
        FINAL_TOPK = 16
        DIM_KEY = DIM // 2
        P = 2

        def _pk(x, Wq_pk, pk_keys):
            b, n, _ = x.shape
            q = (x @ Wq_pk).reshape(b, n, P, HEADS, DIM_KEY).transpose(2, 0, 1, 3, 4)
            sim = jnp.einsum('pbnhd,pkhd->pbnhk', q, pk_keys)
            scores, idx = jax.lax.top_k(sim, PK_TOPK)
            idx0 = idx[0]
            idx1 = idx[1] * NUM_KEYS
            index = (idx0[..., :, None] + idx1[..., None, :]).reshape(b, n, HEADS, PK_TOPK * PK_TOPK)
            score = (scores[0][..., :, None] + scores[1][..., None, :]).reshape(b, n, HEADS, PK_TOPK * PK_TOPK)
            final_scores, pk_idx = jax.lax.top_k(score, FINAL_TOPK)
            final_indices = jnp.take_along_axis(index, pk_idx, axis=-1)
            final_scores = jax.nn.softmax(final_scores, axis=-1)
            return (final_scores, final_indices)
        b, n, d = x.shape
        q = (x @ Wq).reshape(b, n, HEADS, DIM) * DIM ** (-0.5)
        kv_scores, indices = _pk(x, Wq_pk, pk_keys)
        offsets = jnp.arange(HEADS, dtype=indices.dtype) * NUM_KV
        ind = indices + offsets[None, None, :, None]
        k = jnp.einsum('bnhk,bnhkd->bnhd', kv_scores, keys_table[ind])
        v = jnp.einsum('bnhk,bnhkd->bnhd', kv_scores, values_table[ind])
        sim = jnp.einsum('bihd,bjhd->bhij', q, k)
        neg = -jnp.finfo(sim.dtype).max
        causal = jnp.tril(jnp.ones((n, n), dtype=bool))
        sim = jnp.where(causal, sim, neg)
        attn = jax.nn.softmax(sim, axis=-1)
        out = jnp.einsum('bhij,bjhd->bhid', attn, v)
        out = out.transpose(0, 2, 1, 3).reshape(b, n, HEADS * DIM)
        return out @ Wo

    def _L1_attn_ref(x, Wk, Wv, Wr, Wo, Wk_ffn, Wv_ffn, Wr_ffn, g1, b1, g2, b2, spatial_decay, spatial_first):
        import jax, jax.numpy as jnp
        import numpy as np
        B, T, C, HR = (8, 1024, 64, 4)
        N_LAYER, LAYER_ID = (12, 3)
        HID = HR * C

        def _fancy_decay_first():
            r01 = LAYER_ID / (N_LAYER - 1)
            h = np.arange(C, dtype=np.float32)
            decay = -5.0 + 8.0 * (h / (C - 1)) ** (0.7 + 1.3 * r01)
            zig = (np.arange(1, C + 1) % 3 - 1).astype(np.float32) * 0.5
            first = np.float32(np.log(0.3)) + zig
            return (jnp.asarray(decay, jnp.float32), jnp.asarray(first, jnp.float32))

        def _ln(x, g, b):
            m = jnp.mean(x, axis=-1, keepdims=True)
            v = jnp.var(x, axis=-1, keepdims=True)
            return (x - m) * jax.lax.rsqrt(v + 1e-05) * g + b

        def _wkv(w, u, k, v):
            Bb, Tt, Cc = k.shape
            kT = jnp.swapaxes(k, 0, 1)
            vT = jnp.swapaxes(v, 0, 1)

            def step(carry, kv):
                p, q, o = carry
                kt, vt = kv
                no = jnp.maximum(o, u + kt)
                A = jnp.exp(o - no)
                E = jnp.exp(u + kt - no)
                y = (A * p + E * vt) / (A * q + E)
                no2 = jnp.maximum(w + o, kt)
                A2 = jnp.exp(w + o - no2)
                E2 = jnp.exp(kt - no2)
                return ((A2 * p + E2 * vt, A2 * q + E2, no2), y)
            init = (jnp.zeros((Bb, Cc), k.dtype), jnp.zeros((Bb, Cc), k.dtype), jnp.full((Bb, Cc), -1e+38, k.dtype))
            _, yT = jax.lax.scan(step, init, (kT, vT))
            return jnp.swapaxes(yT, 0, 1)
        Tlen = x.shape[1]
        h = _ln(x, g1, b1)
        k = h @ Wk
        v = h @ Wv
        sr = jax.nn.sigmoid(h @ Wr)
        y = _wkv(spatial_decay / Tlen, spatial_first / Tlen, k, v)
        x = x + sr * y @ Wo
        h2 = _ln(x, g2, b2)
        kk = jnp.square(jax.nn.relu(h2 @ Wk_ffn))
        x = x + jax.nn.sigmoid(h2 @ Wr_ffn) * (kk @ Wv_ffn)
        return x

    def _L1_ffn_ref(h, gate_w, gate_b, w1, b1, w2, b2):
        import math
        import jax, jax.numpy as jnp
        import numpy as np
        CAPACITY_FACTOR = 1.25
        B, L, D = h.shape
        E = gate_w.shape[1]
        T = B * L
        C = max(1, math.ceil(CAPACITY_FACTOR * T / E))
        x = h.reshape(T, D)
        logits = x @ gate_w + gate_b
        probs = jax.nn.softmax(logits, axis=-1)
        idx = jnp.argmax(probs, axis=-1)
        prb = jnp.take_along_axis(probs, idx[:, None], axis=1)[:, 0]
        one_hot = jax.nn.one_hot(idx, E, dtype=jnp.float32)
        pos = (jnp.cumsum(one_hot, axis=0) * one_hot).sum(-1).astype(jnp.int32) - 1
        kept = pos < C
        pos_safe = jnp.where(kept, pos, C)
        buf = jnp.zeros((E, C, D), dtype=h.dtype).at[idx, pos_safe].set(x, mode='drop')
        hmid = jax.nn.relu(jnp.einsum('ecd,edf->ecf', buf, w1) + b1[:, None, :])
        ybuf = jnp.einsum('ecf,efd->ecd', hmid, w2) + b2[:, None, :]
        pos_g = jnp.minimum(pos, C - 1)
        y_tok = ybuf[idx, pos_g] * (prb * kept)[:, None]
        y = y_tok.reshape(B, L, D)
        y = jnp.nan_to_num(y, nan=0.0, posinf=10000.0, neginf=-10000.0)
        return y
    h = _L0_tok_ref(x, L0_tok_leaf_ids, L0_tok_op_ids, L0_tok_comp_emb, L0_tok_op_emb, L0_tok_W_bin, L0_tok_b_bin, L0_tok_gamma, L0_tok_beta)
    h = h + _L0_attn_ref(_layernorm(h, axis=-1), L0_attn_WQ, L0_attn_WK, L0_attn_WV, L0_attn_Wout, L0_attn_bout)
    h = h + _L0_ffn_ref(_layernorm(h, axis=-1), L0_ffn_Wq_pk, L0_ffn_pk_keys, L0_ffn_Wq, L0_ffn_keys_table, L0_ffn_values_table, L0_ffn_Wo)
    h = h + _L1_attn_ref(_layernorm(h, axis=-1), L1_attn_Wk, L1_attn_Wv, L1_attn_Wr, L1_attn_Wo, L1_attn_Wk_ffn, L1_attn_Wv_ffn, L1_attn_Wr_ffn, L1_attn_g1, L1_attn_b1, L1_attn_g2, L1_attn_b2, L1_attn_spatial_decay, L1_attn_spatial_first)
    h = h + _L1_ffn_ref(_layernorm(h, axis=-1), L1_ffn_gate_w, L1_ffn_gate_b, L1_ffn_w1, L1_ffn_b1, L1_ffn_w2, L1_ffn_b2)
    return h

_drawn_inputs = setup_inputs


def setup_inputs(seed=0):
    import zlib

    import numpy as np

    out = dict(_drawn_inputs(seed))
    spreads = {'L0_tok_b_bin': (0.0, 0.1),
     'L0_tok_gamma': (1.0, 0.2),
     'L0_tok_beta': (0.0, 0.1),
     'L1_ffn_gate_b': (0.0, 0.8),
     'L1_ffn_b1': (0.0, 2.0),
     'L1_ffn_b2': (0.0, 2.0)}
    factors = {'L0_ffn_Wq_pk': 8.0,
     'L0_ffn_pk_keys': 8.0,
     'L0_ffn_Wq': 53.539,
     'L0_ffn_keys_table': 53.292,
     'L0_ffn_values_table': 8.0,
     'L0_ffn_Wo': 8.0,
     'L1_attn_Wk': 8.0,
     'L1_attn_Wv': 8.0,
     'L1_attn_Wr': 8.0,
     'L1_attn_Wo': 8.0,
     'L1_attn_Wk_ffn': 8.0,
     'L1_attn_Wv_ffn': 8.0,
     'L1_attn_Wr_ffn': 8.0,
     'L1_attn_g1': 8.0,
     'L1_attn_b1': 8.0,
     'L1_attn_g2': 8.0,
     'L1_attn_b2': 8.0,
     'L1_attn_spatial_decay': 8.0,
     'L1_attn_spatial_first': 200.0,
     'L1_ffn_gate_w': 8.0,
     'L1_ffn_w1': 8.0,
     'L1_ffn_w2': 8.0}
    for name, (base, spread) in spreads.items():
        noise = np.random.default_rng([zlib.crc32(name.encode()), seed]).standard_normal(out[name].shape)
        drawn = base * np.exp(spread * noise) if base else spread * noise
        out[name] = jnp.asarray(drawn.astype(out[name].dtype))
    for name, factor in factors.items():
        out[name] = (out[name] * factor).astype(out[name].dtype)
    return out
```

```python
import numpy as np
import concourse.bass as bass
from concourse import mybir
from contextlib import ExitStack

F32 = mybir.dt.float32
I32 = mybir.dt.int32
U32 = mybir.dt.uint32
ALU = mybir.AluOpType
ACT = mybir.ActivationFunctionType
AX = mybir.AxisListType

P = 128
D = 64
NB = 32
H = 8
EPS = 1e-5
NSTRUCT, NLEAF, NOPS, VOCAB, OPV = 2048, 8, 7, 256, 64
STILES = NSTRUCT // P
KEYS, TOPK, DKEY = 64, 16, 32
NUM_KV = KEYS * KEYS
ROWS = [TOPK // (i + 1) for i in range(TOPK)]
OFFS = [sum(ROWS[:i]) for i in range(TOPK)]
NCAND = sum(ROWS)
NE, F = 8, 256
FC = F // P
CAP = -(-5 * NB * P // (4 * NE))
ETILES = CAP // P
SLOTS = NE * CAP
HIDC = 256 // P

NEG = -3.0e38
HUGE = 3.4028234663852886e38
MAGIC = float(0x5F3759DF)

class Steps:

    def __init__(self, eng, sem):
        self.eng, self.sem, self.n = eng, sem, 0

    def inc(self, ins):
        self.n += 1
        ins.then_inc(self.sem, 1)

    def settle(self):
        self.eng.wait_ge(self.sem, self.n)

    def seq(self, ins):
        self.inc(ins)
        self.settle()

    def restart(self):
        self.settle()
        self.eng.sem_clear(self.sem)


def tower(nc, t, out):
    ctx = ExitStack()
    with ctx:
        def sb(name, shape, dt=F32):
            return ctx.enter_context(nc.sbuf_tensor(name, shape, dt))

        def sem(name):
            return ctx.enter_context(nc.semaphore(name))

        def cast_cols(ap, n):
            return ap.unsqueeze(2).to_broadcast([ap.shape[0], ap.shape[1], n])

        def rows_n(ap, n):
            return ap.unsqueeze(1).to_broadcast([ap.shape[0], n, ap.shape[1]])

        root_table = nc.dram_tensor("root_table", [NSTRUCT, D], F32, kind="Internal").ap()
        slots_x = nc.dram_tensor("slots_x", [SLOTS, D], F32, kind="Internal").ap()
        slots_y = nc.dram_tensor("slots_y", [SLOTS, D], F32, kind="Internal").ap()

        mem = sb("mem", [P, H, TOPK, P])
        memf = mem[:, :, :, :].rearrange("p h k d -> p (h k d)")
        lent = [0]

        def lend(parts, *shape, dt=F32):
            n = int(np.prod(shape))
            ap = memf[0:parts, lent[0]:lent[0] + n]
            lent[0] += n
            if dt is not F32:
                ap = ap.bitcast(dt)
            names = "abc"[:len(shape)]
            return ap if len(shape) == 1 else ap.rearrange(
                f"p ({' '.join(names)}) -> p {' '.join(names)}", **dict(zip(names, shape)))

        comp = sb("comp", [P, 2, D])
        opsb = sb("opsb", [OPV, D])
        wb0, wbL, wbR = sb("wb0", [D, D]), sb("wbL", [D, D]), sb("wbR", [D, D])
        wbLR = sb("wbLR", [2 * D, D])
        vec_names = ["L0_tok_b_bin", "L0_tok_gamma", "L0_tok_beta", "L0_attn_bout",
                     "L1_attn_g1", "L1_attn_b1", "L1_attn_g2", "L1_attn_b2"]
        vecs = sb("vecs", [P, len(vec_names), D])
        b_bin, gamma, beta, bout, g1, b1, g2, b2 = [vecs[:, k, :] for k in range(8)]
        gate_b = sb("gate_b", [P, NE])
        heads_in = lend(D, 4, H * D)
        wout = lend(2 * D, H // 2, D)
        pk_in = lend(KEYS, 2, H * DKEY)
        wT = lend(P, 20, D)
        wqk = sb("wqk", [P, H * D])
        wvo = sb("wvo", [D, H * D])
        wpk = sb("wpk", [D, 2 * H * KEYS])
        wq1 = sb("wq1", [P, H * D])
        wo1 = sb("wo1", [P, H, D])
        sq_names = ["L1_attn_Wk", "L1_attn_Wv", "L1_attn_Wr", "L1_attn_Wo", "L1_attn_Wr_ffn"]
        squares = sb("squares", [P, len(sq_names), D])
        rk, rv, rr, ro, rrf = [squares[:, k, :] for k in range(5)]
        wkf = sb("wkf", [D, HIDC * P])
        wvf = sb("wvf", [P, HIDC, D])
        gate_w = sb("gate_w", [D, NE])
        wu = sb("wu", [D, 2])

        ident = sb("ident", [P, P])
        ones = sb("ones", [P, P])
        upto = sb("upto", [P, P])
        causal = sb("causal", [P, P])
        iota_part = sb("iota_part", [P, 2])
        iota_cand = sb("iota_cand", [P, NCAND])
        iota_e = sb("iota_e", [P, NE])
        rev_e = sb("rev_e", [P, NE])
        head_base = sb("head_base", [P, H, TOPK])
        zeros = sb("zeros", [P, SLOTS * D // P // 4])

        compln = sb("compln", [P, 2, D])
        compT = sb("compT", [D, 2 * P])
        opT = sb("opT", [D, OPV])
        tabL, tabR, tab0 = sb("tabL", [P, 2, D]), sb("tabR", [P, 2, D]), sb("tab0", [OPV, D])
        leaf_ids = lend(P, P * NLEAF, dt=I32)
        op_ids = lend(OPV, P * NOPS, dt=I32)
        leaf_hot = lend(P, 2, NLEAF, P)
        op_hot = lend(OPV, NOPS, P)
        node = sb("node", [P, 4, D])
        nodeT = sb("nodeT", [P, 2, P])
        root = sb("root", [P, D])
        ln_st = sb("ln_st", [P, 4, 6])
        ln_mv = sb("ln_mv", [P, 4, 2])
        ln_v = sb("ln_v", [P, 4])
        ln_i = sb("ln_i", [P, 4], I32)
        ln_y = sb("ln_y", [P, 4], I32)
        ln_a = sb("ln_a", [P, 4])

        x_ids = sb("x_ids", [P, NB], I32)
        hid = sb("hid", [P, NB * D])
        hn = sb("hn", [P, 2 * D])
        hnT = sb("hnT", [P, P])
        qT = sb("qT", [D, H * P])
        val = sb("val", [P, H * D])
        prob = sb("prob", [P, H, P])
        probT = sb("probT", [P, H, P])
        mx = sb("mx", [P, H])
        zs = sb("zs", [P, H])
        att = sb("att", [P, D])
        xT = sb("xT", [P, P])
        sim = sb("sim", [P, 2 * H, KEYS])
        top = sb("top", [P, 2 * H, TOPK])
        topi = sb("topi", [P, 2 * H, TOPK], U32)
        topf = sb("topf", [P, 2 * H, TOPK])
        cand = sb("cand", [P, H, NCAND])
        cand2 = sb("cand2", [P, H, NCAND])
        candi = sb("candi", [P, H, NCAND])
        fin = sb("fin", [P, H, TOPK])
        fini = sb("fini", [P, H, TOPK], U32)
        finp = sb("finp", [P, H, TOPK])
        hot = sb("hot", [P, 2, TOPK, NCAND])
        rowf = sb("rowf", [P, H, TOPK])
        row_next = sb("row_next", [P, H * TOPK], I32)
        w_next = sb("w_next", [P, H, TOPK])
        wz = sb("wz", [P, H])
        row_now = sb("row_now", [P, H * TOPK], I32)
        w_now = sb("w_now", [P, H, TOPK])
        q1T = sb("q1T", [D, H * P])
        diag = sb("diag", [P, 2, TOPK, P])
        kvT = sb("kvT", [P, H, P])
        prob1 = sb("prob1", [P, H, P])
        prob1T = sb("prob1T", [P, H, P])
        vo = sb("vo", [P, H * D])
        x3 = sb("x3", [P, D])
        hk = sb("hk", [P, 2 * D])
        hkT = sb("hkT", [P, P])
        kvr = sb("kvr", [D, 3, P])
        om = sb("om", [D, P + 1])
        uk = sb("uk", [D, P])
        nom = sb("nom", [D, P])
        wdec = sb("wdec", [D, P])
        ex = sb("ex", [D, 4, P])
        ev = sb("ev", [D, P])
        pst = sb("pst", [D, P + 1])
        qst = sb("qst", [D, P + 1])
        num = sb("num", [D, P])
        den = sb("den", [D, P])
        ysr = sb("ysr", [D, P])
        x4 = sb("x4", [P, D])
        h2T = sb("h2T", [D, P])
        kk = sb("kk", [P, HIDC, P])
        sg = sb("sg", [P, D])
        xm = sb("xm", [P, 2 * D])
        xmT = sb("xmT", [D, P])
        lg = sb("lg", [P, NE])
        oh = sb("oh", [P, NE])
        sc8 = sb("sc8", [P, NE])
        cum = sb("cum", [P, NE])
        tick_pool, tick_dve = sb("tick_pool", [P, 1]), sb("tick_dve", [P, 1])
        count = sb("count", [P, NE])
        g4 = sb("g4", [P, 8])
        slot_s = sb("slot_s", [P, 1], I32)
        slot_g = sb("slot_g", [P, NB], I32)
        keep = sb("keep", [P, NB])
        lent[0] = 3 * NB * D
        w1 = lend(D, 2, F)
        w2 = lend(P, 2, FC * D)
        eb1 = lend(P, 2, FC)
        eb2 = lend(P, 2, D)
        ex_in = sb("ex_in", [P, 2, ETILES, 2 * D])
        w2 = w2.rearrange("p q (c d) -> p q c d", d=D)
        ex_T = lend(D, CAP)
        ex_h = lend(P, FC, CAP)
        ex_y = lend(P, 2, ETILES * D).rearrange("p q (j d) -> p q j d", d=D)

        y_tok = memf[:, 0:NB * D]
        y_bad = memf[:, NB * D:2 * NB * D]
        y_fill = memf[:, 2 * NB * D:3 * NB * D]

        psA = ctx.enter_context(nc.psum_tensor("psA", [P, 512], F32))
        psB = ctx.enter_context(nc.psum_tensor("psB", [P, 1024], F32))
        psD = ctx.enter_context(nc.psum_tensor("psD", [P, 512], F32))
        psE = ctx.enter_context(nc.psum_tensor("psE", [P, 512], F32))
        psF = ctx.enter_context(nc.psum_tensor("psF", [P, 1024], F32))
        psH = ctx.enter_context(nc.psum_tensor("psH", [P, 512], F32))

        PK_BANKS = (psA, psD, psE, psH)

        loaded = sem("loaded")
        consts_done = sem("consts_done")
        pool_steps, pool_ticks = sem("pool_steps"), sem("pool_ticks")
        zero_filled = sem("zero_filled")
        wT_psum, wT_ready = sem("wT_psum"), sem("wT_ready")
        fold_psum, fold_ready = sem("fold_psum"), sem("fold_ready")
        compln_ready = sem("compln_ready")
        compT_psum, compT_ready = sem("compT_psum"), sem("compT_ready")
        tab_psum, tab_ready = sem("tab_psum"), sem("tab_ready")
        dve_setup = sem("dve_setup")
        ids_loaded, hot_ready = sem("ids_loaded"), sem("hot_ready")
        level_psum, node_ready = sem("level_psum"), sem("node_ready")
        nodeT_psum, nodeT_ready = sem("nodeT_psum"), sem("nodeT_ready")
        root_ready, root_stored = sem("root_ready"), sem("root_stored")
        roots_masked, embedded = sem("roots_masked"), sem("embedded")
        dve_struct = sem("dve_struct")

        dve_pre = sem("dve_pre")
        hn_ready, hnT_psum, hnT_ready = sem("hn_ready"), sem("hnT_psum"), sem("hnT_ready")
        qT_psum, qT_ready, val_psum, val_ready = sem("qT_psum"), sem("qT_ready"), sem("val_psum"), sem("val_ready")
        s_psum, s_shifted, s_exp, p_ready = sem("s_psum"), sem("s_shifted"), sem("s_exp"), sem("p_ready")
        pT_psum, pT_ready, att_psum = sem("pT_psum"), sem("pT_ready"), sem("att_psum")
        x_ready, xT_psum, xT_ready, sim_psum = sem("x_ready"), sem("xT_psum"), sem("xT_ready"), sem("sim_psum")
        sim_read = sem("sim_read")
        w_shifted, w_exp, found = sem("w_shifted"), sem("w_exp"), sem("found")

        w_now_ready, q1T_psum, q1T_ready = sem("w_now_ready"), sem("q1T_psum"), sem("q1T_ready")
        rows_ready = sem("rows_ready")
        gathered = [sem(f"gathered{h}") for h in range(H)]

        dve_post = sem("dve_post")
        diag_ready, kv_psum, kv_ready = sem("diag_ready"), sem("kv_psum"), sem("kv_ready")
        s1_psum, s1_shifted, s1_exp, p1_ready = sem("s1_psum"), sem("s1_shifted"), sem("s1_exp"), sem("p1_ready")
        vo_psum, vo_ready = sem("vo_psum"), sem("vo_ready")
        p1T_psum, p1T_ready, att1_psum = sem("p1T_psum"), sem("p1T_ready"), sem("att1_psum")
        hk_ready, hkT_psum, hkT_ready = sem("hk_ready"), sem("hkT_psum"), sem("hkT_ready")
        kvr_psum, kvr_ready = sem("kvr_psum"), sem("kvr_ready")
        ex_shifted, ex_done, ysr_ready, ro_psum = sem("ex_shifted"), sem("ex_done"), sem("ysr_ready"), sem("ro_psum")
        h2_ready, h2T_psum, h2T_ready = sem("h2_ready"), sem("h2T_psum"), sem("h2T_ready")
        kk_psum, relu_done, kk_ready, ffn_psum = sem("kk_psum"), sem("relu_done"), sem("kk_ready"), sem("ffn_psum")
        kv_copied, sg_ready = sem("kv_copied"), sem("sg_ready")
        xm_ready, xmT_psum, xmT_ready = sem("xm_ready"), sem("xmT_psum"), sem("xmT_ready")
        gate_psum, lg_shifted, lg_exp = sem("gate_psum"), sem("lg_shifted"), sem("lg_exp")
        oh_ready, cum_psum, slot_ready = sem("oh_ready"), sem("cum_psum"), sem("slot_ready")
        scattered = sem("scattered")

        ew_loaded = [sem("ew_loaded0"), sem("ew_loaded1")]
        exT_psum, exT_ready = sem("exT_psum"), sem("exT_ready")
        eh_psum, eh_ready = sem("eh_psum"), sem("eh_ready")
        ey_psum, ey_ready, ey_stored = sem("ey_psum"), sem("ey_ready"), sem("ey_stored")
        y_gathered, dve_tail, out_ready, out_stored = sem("y_gathered"), sem("dve_tail"), sem("out_ready"), sem("out_stored")

        block = ctx.enter_context(nc.Block())
        loads = []

        def load(dst, src):
            loads.append((dst, src))

        for c in range(2):
            load(comp[:, c, :], t["L0_tok_comp_emb"][c * P:(c + 1) * P, :])
        load(opsb[:, :], t["L0_tok_op_emb"])
        load(wb0[:, :], t["L0_tok_W_bin"][0:D, :])
        load(wbL[:, :], t["L0_tok_W_bin"][D:2 * D, :])
        load(wbR[:, :], t["L0_tok_W_bin"][2 * D:3 * D, :])
        load(wbLR[:, :], t["L0_tok_W_bin"][D:3 * D, :])
        for k, name in enumerate(vec_names):
            load(vecs[:, k, :], t[name].partition_broadcast(P))
        load(gate_b[:, :], t["L1_ffn_gate_b"].partition_broadcast(P))
        for k, name in enumerate(["L0_attn_WQ", "L0_attn_WK", "L0_attn_WV", "L0_ffn_Wq_pk"]):
            load(heads_in[:, k, :], t[name])
        load(wout[:, :, :], t["L0_attn_Wout"].rearrange("(j p) o -> p j o", p=2 * D))
        load(pk_in[:, :, :], t["L0_ffn_pk_keys"].rearrange("p k h d -> k p (h d)"))
        load(wq1[0:D, :], t["L0_ffn_Wq"])
        load(wo1[D:P, :, :], t["L0_ffn_Wo"].rearrange("(h d) o -> d h o", d=D))
        for k, name in enumerate(sq_names):
            load(squares[0:D, k, :], t[name])
        load(wkf[:, :], t["L1_attn_Wk_ffn"])
        load(wvf[:, :, :], t["L1_attn_Wv_ffn"].rearrange("(c p) o -> p c o", p=P))
        load(gate_w[:, :], t["L1_ffn_gate_w"])
        load(wu[:, 0:1], t["L1_attn_spatial_decay"].rearrange("(c o) -> c o", o=1))
        load(wu[:, 1:2], t["L1_attn_spatial_first"].rearrange("(c o) -> c o", o=1))
        load(x_ids[:, :], t["x"].rearrange("b t -> t b"))
        ALL_LOADED = 16 * len(loads)

        @block.sync
        def _(sp):
            for dst, src in loads:
                sp.dma_start(dst, src, allow_slow_non_contiguous=True).then_inc(loaded, 16)
            sp.wait_ge(consts_done, 1)
            for k in range(4):
                sp.dma_start(slots_x.rearrange("(a p r) d -> a p (r d)", a=4, p=P)[k], zeros[:, :]).then_inc(zero_filled, 16)
            leaf_rows = t["L0_tok_leaf_ids"].rearrange("(s p) n -> s (p n)", p=P)
            op_rows = t["L0_tok_op_ids"].rearrange("(s p) n -> s (p n)", p=P)
            root_rows = root_table.rearrange("(s p) d -> s p d", p=P)
            with sp.Fori(0, STILES) as s:
                sp.wait_ge(hot_ready, s)
                sp.dma_start(leaf_ids[:, :], leaf_rows[bass.ds(s, 1), :].to_broadcast([P, P * NLEAF])).then_inc(ids_loaded, 16)
                sp.dma_start(op_ids[:, :], op_rows[bass.ds(s, 1), :].to_broadcast([OPV, P * NOPS])).then_inc(ids_loaded, 16)
                sp.wait_ge(root_ready, s + 1)
                sp.dma_start(root_rows[bass.ds(s, 1), :, :].rearrange("a p d -> (a p) d"), root[:, :]).then_inc(root_stored, 16)
            sp.wait_ge(root_stored, 16 * STILES)
            sp.dma_start(root_table[0:2, :], zeros[0:2, 0:D]).then_inc(roots_masked, 16)
            x_rows = slots_x.rearrange("(e j p) d -> e p j d", p=P, j=ETILES)
            y_rows = slots_y.rearrange("(e j p) d -> e p j d", p=P, j=ETILES)
            w2_rows = t["L1_ffn_w2"].rearrange("e (c p) d -> e p c d", p=P)
            b1_rows = t["L1_ffn_b1"].rearrange("e (c p) -> e p c", p=P)
            sp.wait_ge(scattered, 16 * NB)
            with sp.Fori(0, NE // 2) as i:
                for q in range(2):
                    e = i * 2 + q
                    sp.wait_ge(ey_ready, i * 2)
                    sp.dma_start(w1[:, q, :], t["L1_ffn_w1"][bass.ds(e, 1), :, :].rearrange("a d f -> (a d) f")).then_inc(ew_loaded[q], 16)
                    sp.dma_start(w2[:, q, :, :], w2_rows[bass.ds(e, 1)].rearrange("a p c d -> (a p) c d")).then_inc(ew_loaded[q], 16)
                    sp.dma_start(eb1[:, q, :], b1_rows[bass.ds(e, 1)].rearrange("a p c -> (a p) c"),
                                 allow_slow_non_contiguous=True).then_inc(ew_loaded[q], 16)
                    sp.dma_start(eb2[:, q, :], t["L1_ffn_b2"][bass.ds(e, 1), :].to_broadcast([P, D])).then_inc(ew_loaded[q], 16)
                    sp.dma_start(ex_in[:, q, :, 0:D], x_rows[bass.ds(e, 1)].rearrange("a p j d -> (a p) j d")).then_inc(ew_loaded[q], 16)
                for q in range(2):
                    e = i * 2 + q
                    sp.wait_ge(ey_ready, e + 1)
                    sp.dma_start(y_rows[bass.ds(e, 1)].rearrange("a p j d -> (a p) j d"), ex_y[:, q, :, :]).then_inc(ey_stored, 16)
            sp.wait_ge(out_ready, 1)
            sp.dma_start(out.rearrange("b t d -> t b d"), hid[:, :].rearrange("p (b d) -> p b d", d=D)).then_inc(out_stored, 16)
            sp.wait_ge(out_stored, 16)
            sp.wait_ge(zero_filled, 64)
            sp.wait_ge(ey_stored, 16 * NE)
            sp.wait_ge(roots_masked, 16)

        @block.gpsimd
        def _(pool):
            st = Steps(pool, pool_steps)
            st.inc(pool.memset(ident[:, :], 0.0))
            st.inc(pool.memset(ones[:, :], 1.0))
            st.inc(pool.memset(upto[:, :], 1.0))
            st.inc(pool.memset(causal[:, :], 0.0))
            st.inc(pool.memset(zeros[:, :], 0.0))
            for pad in (hn[:, D:2 * D], hk[:, D:2 * D], xm[:, D:2 * D], ex_in[:, :, :, D:2 * D]):
                st.inc(pool.memset(pad, 0.0))
            st.settle()
            for pad in (wqk[D:P, :], wq1[D:P, :], squares[D:P, :, :]):
                st.inc(pool.memset(pad, 0.0))
            st.settle()
            st.inc(pool.iota(iota_cand[:, :], [[1, NCAND]], 0, 0, allow_small_or_imprecise_dtypes=True))
            st.inc(pool.iota(iota_e[:, :], [[1, NE]], 0, 0, allow_small_or_imprecise_dtypes=True))
            st.inc(pool.iota(rev_e[:, :], [[-1, NE]], NE, 0, allow_small_or_imprecise_dtypes=True))
            st.inc(pool.iota(iota_part[:, :], [[P, 2]], 0, 1, allow_small_or_imprecise_dtypes=True))
            st.inc(pool.iota(head_base[:, :, :], [[NUM_KV, H], [0, TOPK]], 0, 0, allow_small_or_imprecise_dtypes=True))
            st.settle()
            st.inc(pool.affine_select(out=ident[:, :], in_=ident[:, :], compare_op=ALU.not_equal, fill=1.0,
                                      base=0, pattern=[[-1, P]], channel_multiplier=1))
            st.inc(pool.affine_select(out=upto[:, :], in_=upto[:, :], compare_op=ALU.is_ge, fill=0.0,
                                      base=0, pattern=[[1, P]], channel_multiplier=-1))
            st.inc(pool.affine_select(out=causal[:, :], in_=causal[:, :], compare_op=ALU.is_ge, fill=NEG,
                                      base=0, pattern=[[-1, P]], channel_multiplier=1))
            st.settle()
            pool.memset(count[:, :], 0.0).then_inc(consts_done, 1)

            pool.wait_ge(loaded, ALL_LOADED)
            pool.wait_ge(roots_masked, 16)
            for b in range(NB):
                pool.indirect_dma_start(out=hid[:, b * D:(b + 1) * D], out_offset=None, in_=root_table,
                                        in_offset=bass.IndirectOffsetOnAxis(ap=x_ids[:, b:b + 1], axis=0)).then_inc(embedded, 16)

            ticks = Steps(pool, pool_ticks)

            def tick():
                ticks.inc(pool.tensor_tensor(tick_pool[:, :], ones[:, 0:1], ones[:, 0:1], ALU.mult))
                ticks.restart()
                ticks.n = 0

            def gather(b):
                for h in range(H):
                    if h % 4 == 0:
                        pool.wait_ge(rows_ready, b * 2 + (h // 4 + 1))
                        tick()
                    for k in range(TOPK):
                        c = h * TOPK + k
                        pool.indirect_dma_start(out=mem[:, h, k, :], out_offset=None, in_=t["kv_table"],
                                                in_offset=bass.IndirectOffsetOnAxis(ap=row_now[:, c:c + 1], axis=0)).then_inc(gathered[h], 16)

            def scatter(b):
                pool.wait_ge(slot_ready, b + 1)
                tick()
                pool.indirect_dma_start(out=slots_x, out_offset=bass.IndirectOffsetOnAxis(ap=slot_s[:, 0:1], axis=0),
                                        in_=xm[:, 0:D], in_offset=None, bounds_check=SLOTS - 1,
                                        oob_is_err=False).then_inc(scattered, 16)

            gather(0)
            pool.wait_ge(zero_filled, 64)
            with pool.Fori(1, NB) as b:
                gather(b)
                scatter(b - 1)
            scatter(NB - 1)

            pool.wait_ge(ey_stored, 16 * NE)
            for b in range(NB):
                pool.indirect_dma_start(out=y_tok[:, b * D:(b + 1) * D], out_offset=None, in_=slots_y,
                                        in_offset=bass.IndirectOffsetOnAxis(ap=slot_g[:, b:b + 1], axis=0)).then_inc(y_gathered, 16)

        @block.vector
        def _(dve):
            V = nc.vector

            def norm(st, src, n, dst, gain=None, bias=None, done=None):
                for j in range(n):
                    st.inc(V.bn_stats(ln_st[:, j, :], src[:, j, :]))
                st.settle()
                for j in range(n):
                    st.inc(V.bn_aggr(ln_mv[:, j, :], ln_st[:, j, :]))
                st.settle()
                v, y, a = ln_v[:, 0:n], ln_y[:, 0:n].bitcast(F32), ln_a[:, 0:n]
                st.seq(V.tensor_scalar(v, ln_mv[:, 0:n, 1], EPS, None, ALU.add))
                st.seq(V.tensor_scalar(ln_i[:, 0:n], v.bitcast(I32), 1, None, ALU.logical_shift_right))
                st.seq(V.tensor_scalar(ln_y[:, 0:n], ln_i[:, 0:n], -1.0, MAGIC, ALU.mult, ALU.add))
                c = 1.0
                for _ in range(3):
                    st.seq(V.tensor_tensor(a, y, y, ALU.mult))
                    st.seq(V.tensor_tensor(a, a, v, ALU.mult))
                    st.seq(V.scalar_tensor_tensor(y, a, 3.0 * c * c, y, ALU.subtract, ALU.mult))
                    c = -2.0 * c * c * c
                st.seq(V.tensor_scalar(y, y, 1.0 / c, None, ALU.mult))
                last = done is not None and gain is None
                if n == 1:
                    i = V.tensor_scalar(dst[:, 0, :], src[:, 0, :], ln_mv[:, 0, 0:1], y[:, 0:1], ALU.subtract, ALU.mult)
                else:
                    st.seq(V.tensor_tensor(dst, src, cast_cols(ln_mv[:, 0:n, 0], D), ALU.subtract))
                    i = V.tensor_tensor(dst, dst, cast_cols(y, D), ALU.mult)
                if gain is not None:
                    st.seq(i)
                    st.seq(V.tensor_tensor(dst, dst, rows_n(gain, n), ALU.mult))
                    i = V.tensor_tensor(dst, dst, rows_n(bias, n), ALU.add)
                if done is None:
                    st.seq(i)
                else:
                    i.then_inc(done, 1)

            def tick(st):
                st.seq(V.memset(tick_dve[:, :], 0.0))

            def one(ap):
                return ap.unsqueeze(1)

            st = Steps(dve, dve_setup)
            dve.wait_ge(loaded, ALL_LOADED)
            dve.wait_ge(consts_done, 1)
            norm(st, comp[:, :, :], 2, compln[:, :, :], gamma, beta, compln_ready)
            st.inc(V.tensor_scalar(wu[:, :], wu[:, :], 1.0 / P, None, ALU.mult))
            st.inc(V.memset(om[:, 0:1], -1e38))
            st.inc(V.memset(pst[:, 0:1], 0.0))
            st.inc(V.memset(qst[:, 0:1], 0.0))
            st.settle()
            st.seq(V.tensor_scalar(wdec[:, :], ones[0:D, :], wu[:, 0:1], None, ALU.mult))
            for k in range(20 // 8 + 1):
                n = min(8, 20 - 8 * k)
                dve.wait_ge(wT_psum, k + 1)
                V.tensor_copy(wT[:, 8 * k:8 * k + n, :], [psA, psD, psE][k][:, 0:n * D].rearrange("p (a d) -> p a d", d=D)).then_inc(wT_ready, 1)
            dve.wait_ge(fold_psum, 1)
            for g in range(2):
                for k, w in enumerate((wqk, wvo)):
                    V.tensor_copy(w[0:D, :].rearrange("c (j g d) -> c g j d", g=2, d=D)[:, g],
                                  psB[0:D, 512 * g + 256 * k:512 * g + 256 * k + 256].rearrange("c (j d) -> c j d", d=D)).then_inc(fold_ready, 1)
            for g in range(4):
                V.tensor_copy(wpk[:, :].rearrange("c (j g k) -> c g j k", g=4, k=KEYS)[:, g],
                              PK_BANKS[g][0:D, 0:4 * KEYS].rearrange("c (j k) -> c j k", k=KEYS)).then_inc(fold_ready, 1)
            dve.wait_ge(compT_psum, 1)
            V.tensor_copy(compT[:, :], psA[0:D, 0:2 * P]).then_inc(compT_ready, 1)
            V.tensor_copy(opT[:, :], psA[0:D, 2 * P:2 * P + OPV]).then_inc(compT_ready, 1)
            dve.wait_ge(tab_psum, 1)
            V.tensor_copy(tabL[:, :, :], psD[:, 0:2 * D].rearrange("p (a d) -> p a d", d=D)).then_inc(tab_ready, 1)
            V.tensor_copy(tabR[:, :, :], psD[:, 2 * D:4 * D].rearrange("p (a d) -> p a d", d=D)).then_inc(tab_ready, 1)
            V.tensor_tensor(tab0[:, :], psD[0:OPV, 4 * D:5 * D], b_bin[0:OPV], ALU.add).then_inc(tab_ready, 1)

            with dve.Fori(0, STILES) as s:
                st = Steps(dve, dve_struct)
                dve.wait_ge(ids_loaded, s * 32 + 32)
                leaves = leaf_ids[:, :].rearrange("p (s n) -> p n s", n=NLEAF)
                for c in range(2):
                    st.inc(V.tensor_scalar(leaf_hot[:, c, :, :], leaves, iota_part[:, c:c + 1], None, ALU.is_equal))
                st.settle()
                V.tensor_scalar(op_hot[:, :, :], op_ids[:, :].rearrange("p (s n) -> p n s", n=NOPS),
                                iota_part[0:OPV, 0:1], None, ALU.is_equal).then_inc(hot_ready, 1)
                for level, n in enumerate((4, 2, 1)):
                    dve.wait_ge(level_psum, s * 3 + (level + 1))
                    tick(st)
                    src = psB[:, 0:n * D].rearrange("p (a d) -> p a d", d=D)
                    if level < 2:
                        norm(st, src, n, node[:, 0:n, :], gamma, beta, node_ready)
                    else:
                        dve.wait_ge(root_stored, s * 16)
                        tick(st)
                        norm(st, src, n, one(root[:, :]), gamma, beta, root_ready)
                st.restart()

            def softmax_shift(st, src, dst, done):
                st.seq(V.tensor_reduce(mx[:, :], src, AX.X, ALU.max))
                V.tensor_tensor(dst, src, cast_cols(mx[:, :], P), ALU.subtract).then_inc(done, 1)

            def softmax_scale(st, buf, done):
                st.seq(V.tensor_reduce(zs[:, :], buf, AX.X, ALU.add))
                st.seq(V.reciprocal(zs[:, :], zs[:, :]))
                V.tensor_tensor(buf, buf, cast_cols(zs[:, :], P), ALU.mult).then_inc(done, 1)

            def pairs(st, dst, l0, l1):
                for i in range(5):
                    n = ROWS[i]
                    st.inc(V.tensor_tensor(dst[:, :, OFFS[i]:OFFS[i] + n], l0[:, :, i:i + 1].to_broadcast([P, H, n]),
                                           l1[:, :, 0:n], ALU.add))
                o = dst[:, :, OFFS[5]:OFFS[8]].rearrange("p h (i j) -> p h i j", j=2)
                st.inc(V.tensor_tensor(o, l0[:, :, 5:8].unsqueeze(3).to_broadcast([P, H, 3, 2]),
                                       l1[:, :, 0:2].unsqueeze(2).to_broadcast([P, H, 3, 2]), ALU.add))
                st.inc(V.tensor_tensor(dst[:, :, OFFS[8]:NCAND], l0[:, :, 8:16],
                                       l1[:, :, 0:1].to_broadcast([P, H, 8]), ALU.add))

            def pre(b):
                n = b + 1
                st = Steps(dve, dve_pre)
                hb = hid[:, bass.ds(b * D, D)]
                norm(st, one(hb), 1, one(hn[:, 0:D]), done=hn_ready)
                s3 = psB[:, :].rearrange("p (h t) -> p h t", h=H)
                dve.wait_ge(s_psum, n)
                softmax_shift(st, s3, prob[:, :, :], s_shifted)
                dve.wait_ge(s_exp, n)
                softmax_scale(st, prob[:, :, :], p_ready)
                dve.wait_ge(att_psum, n)
                st.seq(V.tensor_tensor(att[:, :], psA[:, 0:D], bout, ALU.add))
                st.seq(V.tensor_tensor(hb, hb, att[:, :], ALU.add))
                norm(st, one(hb), 1, one(hn[:, 0:D]), done=x_ready)
                dve.wait_ge(sim_psum, n)
                tick(st)
                sp3 = psB[:, :].rearrange("p (u k) -> p u k", k=KEYS)
                for u in range(2 * H):
                    st.inc(V.max(top[:, u, 0:8], sp3[:, u, :]))
                st.settle()
                for u in range(2 * H):
                    st.inc(V.max_index(topi[:, u, 0:8], top[:, u, 0:8], sp3[:, u, :]))
                for u in range(2 * H):
                    st.inc(V.match_replace(sim[:, u, :], top[:, u, 0:8], sp3[:, u, :], NEG))
                st.settle()
                for u in range(2 * H):
                    st.inc(V.max(top[:, u, 8:16], sim[:, u, :]))
                st.settle()
                for u in range(2 * H):
                    i = V.max_index(topi[:, u, 8:16], top[:, u, 8:16], sim[:, u, :])
                    st.inc(i) if u < 2 * H - 1 else i.then_inc(sim_read, 1)
                dve.wait_ge(sim_read, n)
                st.settle()
                st.seq(V.tensor_copy(topf[:, :, :], topi[:, :, :]))
                st.inc(V.tensor_tensor(topf[:, 0:H, :], topf[:, 0:H, :], head_base[:, :, :], ALU.add))
                st.inc(V.tensor_scalar(topf[:, H:2 * H, :], topf[:, H:2 * H, :], float(KEYS), None, ALU.mult))
                pairs(st, cand[:, :, :], top[:, 0:H, :], top[:, H:2 * H, :])
                st.settle()
                pairs(st, candi[:, :, :], topf[:, 0:H, :], topf[:, H:2 * H, :])
                for h in range(H):
                    st.inc(V.max(fin[:, h, 0:8], cand[:, h, :]))
                st.settle()
                for h in range(H):
                    st.inc(V.max_index(fini[:, h, 0:8], fin[:, h, 0:8], cand[:, h, :]))
                for h in range(H):
                    st.inc(V.match_replace(cand2[:, h, :], fin[:, h, 0:8], cand[:, h, :], NEG))
                st.settle()
                for h in range(H):
                    st.inc(V.max(fin[:, h, 8:16], cand2[:, h, :]))
                st.settle()
                V.tensor_tensor(w_next[:, :, :], fin[:, :, :], fin[:, :, 0:1].to_broadcast([P, H, TOPK]),
                                ALU.subtract).then_inc(w_shifted, 1)
                for h in range(H):
                    st.inc(V.max_index(fini[:, h, 8:16], fin[:, h, 8:16], cand2[:, h, :]))
                st.settle()
                st.seq(V.tensor_copy(finp[:, :, :], fini[:, :, :]))
                for h0 in range(0, H, 2):
                    for q in range(2):
                        st.inc(V.tensor_tensor(hot[:, q, :, :], cast_cols(finp[:, h0 + q, :], NCAND),
                                               rows_n(iota_cand[:, :], TOPK), ALU.is_equal))
                    st.settle()
                    for q in range(2):
                        st.inc(V.tensor_tensor(hot[:, q, :, :], hot[:, q, :, :],
                                               rows_n(candi[:, h0 + q, :], TOPK), ALU.mult))
                    st.settle()
                    for q in range(2):
                        st.inc(V.tensor_reduce(rowf[:, h0 + q, :], hot[:, q, :, :], AX.X, ALU.add))
                    st.settle()
                dve.wait_ge(w_exp, n)
                st.seq(V.tensor_reduce(wz[:, :], w_next[:, :, :], AX.X, ALU.add))
                st.seq(V.reciprocal(wz[:, :], wz[:, :]))
                V.tensor_tensor(w_next[:, :, :], w_next[:, :, :], cast_cols(wz[:, :], TOPK), ALU.mult).then_inc(found, 1)
                st.inc(V.tensor_copy(row_next[:, :], rowf[:, :, :].rearrange("p h k -> p (h k)")))
                st.restart()

            def commit(half):
                c = half * H * TOPK // 2
                V.tensor_copy(row_now[:, c:c + H * TOPK // 2], row_next[:, c:c + H * TOPK // 2]).then_inc(rows_ready, 1)

            def carry(b):
                V.tensor_copy(w_now[:, :, :], w_next[:, :, :]).then_inc(w_now_ready, 1)
                dve.wait_ge(w_now_ready, b + 1)

            def post(b, more):
                n = b + 1
                st = Steps(dve, dve_post)
                for h in range(H):
                    if h >= 2:
                        dve.wait_ge(kv_psum, b * H + (h - 1))
                    V.tensor_tensor(diag[:, h % 2, :, :], rows_n(ident[:, :], TOPK),
                                    cast_cols(w_now[:, h, :], P), ALU.mult).then_inc(diag_ready, 1)
                    if more and h == 5:
                        dve.wait_ge(kv_psum, b * H + 4)
                        commit(0)
                if more:
                    dve.wait_ge(kv_psum, b * H + H)
                    commit(1)
                dve.wait_ge(s1_psum, n)
                s3 = psF[:, :].rearrange("p (h t) -> p h t", h=H)
                st.seq(V.tensor_tensor(prob1[:, :, :], s3, rows_n(causal[:, :], H), ALU.add))
                softmax_shift(st, prob1[:, :, :], prob1[:, :, :], s1_shifted)
                dve.wait_ge(s1_exp, n)
                softmax_scale(st, prob1[:, :, :], p1_ready)
                hb = hid[:, bass.ds(b * D, D)]
                dve.wait_ge(att1_psum, n)
                st.seq(V.tensor_tensor(hb, hb, psE[:, 0:D], ALU.add))
                norm(st, one(hb), 1, one(x3[:, :]))
                norm(st, one(x3[:, :]), 1, one(hk[:, 0:D]), g1, b1, hk_ready)
                dve.wait_ge(kv_copied, n)
                dve.wait_ge(kvr_ready, n)
                k, v, er = kvr[:, 0, :], kvr[:, 1, :], kvr[:, 2, :]
                o_old, o_new = om[:, 0:P], om[:, 1:P + 1]
                st.inc(V.tensor_tensor_scan(o_new, wdec[:, :], k, -1e38, ALU.add, ALU.max))
                st.inc(V.tensor_scalar(uk[:, :], k, wu[:, 1:2], None, ALU.add))
                st.inc(V.tensor_scalar(er, er, 1.0, None, ALU.add))
                st.settle()
                st.inc(V.tensor_tensor(nom[:, :], o_old, uk[:, :], ALU.max))
                st.inc(V.scalar_tensor_tensor(ex[:, 2, :], o_old, wu[:, 0:1], o_new, ALU.add, ALU.subtract))
                st.inc(V.tensor_tensor(ex[:, 3, :], k, o_new, ALU.subtract))
                st.inc(V.reciprocal(er, er))
                st.settle()
                st.inc(V.tensor_tensor(ex[:, 0, :], o_old, nom[:, :], ALU.subtract))
                V.tensor_tensor(ex[:, 1, :], uk[:, :], nom[:, :], ALU.subtract).then_inc(ex_shifted, 1)
                dve.wait_ge(ex_done, n)
                st.inc(V.tensor_tensor(ev[:, :], ex[:, 3, :], v, ALU.mult))
                st.inc(V.tensor_tensor_scan(qst[:, 1:P + 1], ex[:, 2, :], ex[:, 3, :], 0.0, ALU.mult, ALU.add))
                st.inc(V.tensor_tensor(num[:, :], ex[:, 1, :], v, ALU.mult))
                st.settle()
                st.inc(V.tensor_tensor_scan(pst[:, 1:P + 1], ex[:, 2, :], ev[:, :], 0.0, ALU.mult, ALU.add))
                st.inc(V.tensor_tensor(den[:, :], ex[:, 0, :], qst[:, 0:P], ALU.mult))
                st.settle()
                st.inc(V.tensor_tensor(ysr[:, :], ex[:, 0, :], pst[:, 0:P], ALU.mult))
                st.inc(V.tensor_tensor(den[:, :], den[:, :], ex[:, 1, :], ALU.add))
                st.settle()
                st.inc(V.tensor_tensor(num[:, :], num[:, :], ysr[:, :], ALU.add))
                st.inc(V.reciprocal(den[:, :], den[:, :]))
                st.settle()
                st.seq(V.tensor_tensor(num[:, :], num[:, :], den[:, :], ALU.mult))
                V.tensor_tensor(ysr[:, :], num[:, :], er, ALU.mult).then_inc(ysr_ready, 1)
                dve.wait_ge(ro_psum, n)
                st.seq(V.tensor_tensor(x4[:, :], x3[:, :], psE[:, 0:D], ALU.add))
                norm(st, one(x4[:, :]), 1, one(hk[:, 0:D]), g2, b2, h2_ready)
                dve.wait_ge(sg_ready, n)
                st.seq(V.tensor_scalar(sg[:, :], sg[:, :], 1.0, None, ALU.add))
                st.seq(V.reciprocal(sg[:, :], sg[:, :]))
                dve.wait_ge(ffn_psum, n)
                st.seq(V.tensor_tensor(sg[:, :], sg[:, :], psE[:, 0:D], ALU.mult))
                st.seq(V.tensor_tensor(x4[:, :], x4[:, :], sg[:, :], ALU.add))
                st.seq(V.tensor_tensor(hb, hb, x4[:, :], ALU.add))
                dve.wait_ge(scattered, b * 16)
                tick(st)
                norm(st, one(hb), 1, one(xm[:, 0:D]), done=xm_ready)
                dve.wait_ge(gate_psum, n)
                st.seq(V.tensor_tensor(lg[:, :], psE[:, 0:NE], gate_b[:, :], ALU.add))
                st.seq(V.tensor_reduce(g4[:, 0:1], lg[:, :], AX.X, ALU.max))
                V.tensor_scalar(lg[:, :], lg[:, :], g4[:, 0:1], None, ALU.subtract).then_inc(lg_shifted, 1)
                dve.wait_ge(lg_exp, n)
                st.inc(V.tensor_reduce(g4[:, 0:1], lg[:, :], AX.X, ALU.max))
                st.inc(V.tensor_reduce(g4[:, 1:2], lg[:, :], AX.X, ALU.add))
                st.settle()
                st.inc(V.reciprocal(g4[:, 1:2], g4[:, 1:2]))
                st.seq(V.scalar_tensor_tensor(sc8[:, :], lg[:, :], g4[:, 0:1], rev_e[:, :], ALU.is_ge, ALU.mult))
                st.seq(V.tensor_reduce(g4[:, 2:3], sc8[:, :], AX.X, ALU.max))
                V.tensor_scalar(oh[:, :], sc8[:, :], g4[:, 2:3], None, ALU.is_equal).then_inc(oh_ready, 1)
                dve.wait_ge(oh_ready, n)
                st.inc(V.tensor_tensor(sc8[:, :], oh[:, :], iota_e[:, :], ALU.mult))
                dve.wait_ge(cum_psum, n)
                st.seq(V.tensor_tensor(cum[:, :], psE[:, 64:64 + NE], count[:, :], ALU.add))
                st.inc(V.tensor_tensor(cum[:, :], cum[:, :], oh[:, :], ALU.mult))
                st.inc(V.tensor_tensor(count[:, :], count[:, :], psE[:, 128:128 + NE], ALU.add))
                st.inc(V.tensor_reduce(g4[:, 3:4], sc8[:, :], AX.X, ALU.add))
                st.settle()
                st.seq(V.tensor_reduce(g4[:, 4:5], cum[:, :], AX.X, ALU.add))
                st.inc(V.tensor_scalar(g4[:, 5:6], g4[:, 4:5], float(CAP), None, ALU.is_le))
                st.inc(V.tensor_scalar(g4[:, 6:7], g4[:, 4:5], float(CAP), -1.0, ALU.min, ALU.add))
                st.inc(V.tensor_scalar(g4[:, 4:5], g4[:, 4:5], float(CAP), float(SLOTS), ALU.is_gt, ALU.mult))
                st.inc(V.tensor_scalar(g4[:, 3:4], g4[:, 3:4], float(CAP), None, ALU.mult))
                st.inc(V.tensor_scalar(g4[:, 0:1], g4[:, 0:1], g4[:, 1:2], None, ALU.mult))
                st.settle()
                st.inc(V.tensor_tensor(g4[:, 6:7], g4[:, 6:7], g4[:, 3:4], ALU.add))
                st.settle()
                V.tensor_tensor(slot_s[:, :], g4[:, 6:7], g4[:, 4:5], ALU.add).then_inc(slot_ready, 1)
                st.inc(V.tensor_copy(slot_g[:, bass.ds(b, 1)], g4[:, 6:7]))
                st.inc(V.tensor_tensor(keep[:, bass.ds(b, 1)], g4[:, 0:1], g4[:, 5:6], ALU.mult))
                st.restart()

            dve.wait_ge(embedded, 16 * NB)
            pre(0)
            commit(0)
            commit(1)
            dve.wait_ge(rows_ready, 2)
            with dve.Fori(0, NB - 1) as b:
                carry(b)
                pre(b + 1)
                post(b, True)
            carry(NB - 1)
            post(NB - 1, False)

            with dve.Fori(0, NE // 2) as i:
                for q in range(2):
                    e = i * 2 + q
                    dve.wait_ge(ey_psum, e + 1)
                    dve.wait_ge(ey_stored, i * 32)
                    V.tensor_tensor(ex_y[:, q, :, :], psF[:, 0:ETILES * D].rearrange("p (j d) -> p j d", d=D),
                                    rows_n(eb2[:, q, :], ETILES), ALU.add).then_inc(ey_ready, 1)
            dve.wait_ge(y_gathered, 16 * NB)
            st = Steps(dve, dve_tail)
            y3 = y_tok.rearrange("p (b d) -> p b d", d=D)
            st.inc(V.memset(y_fill, 0.0))
            st.seq(V.tensor_tensor(y3, y3, cast_cols(keep[:, :], D), ALU.mult))
            for op, x, fill in ((ALU.not_equal, None, 0.0), (ALU.is_gt, HUGE, 1e4), (ALU.is_lt, -HUGE, -1e4)):
                if x is None:
                    st.inc(V.tensor_tensor(y_bad.bitcast(I32), y_tok, y_tok, op))
                else:
                    st.inc(V.memset(y_fill, fill))
                    st.inc(V.tensor_scalar(y_bad.bitcast(I32), y_tok, x, None, op))
                st.settle()
                st.seq(V.copy_predicated(y_tok, y_bad.bitcast(I32), y_fill))
            V.tensor_tensor(hid[:, :], hid[:, :], y_tok, ALU.add).then_inc(out_ready, 1)

        @block.scalar
        def _(act):
            A = nc.scalar

            def copy(dst, src, done, scale=1.0):
                A.activation(dst, src, ACT.Copy, scale=scale).then_inc(done, 1)

            with act.Fori(0, STILES) as s:
                for level in range(2):
                    act.wait_ge(nodeT_psum, s * 2 + (level + 1))
                    m = 2 - level
                    copy(nodeT[:, 0:m, :], psA[:, 0:m * P].rearrange("p (a t) -> p a t", t=P), nodeT_ready)

            def pre(b):
                n = b + 1
                act.wait_ge(hnT_psum, n)
                copy(hnT[:, :], psA[:, 0:P], hnT_ready)
                act.wait_ge(qT_psum, n)
                copy(qT[:, :], psB[0:D, :], qT_ready)
                act.wait_ge(val_psum, n)
                copy(val[:, :], psD[:, :], val_ready)
                act.wait_ge(s_shifted, n)
                A.activation(prob[:, :, :], prob[:, :, :], ACT.Exp, scale=float(1.0 / np.sqrt(D / H))).then_inc(s_exp, 1)
                act.wait_ge(pT_psum, n)
                copy(probT[:, :, :], psB[:, :].rearrange("p (h t) -> p h t", h=H), pT_ready)
                act.wait_ge(xT_psum, n)
                copy(xT[:, :], psA[:, 0:P], xT_ready)
                act.wait_ge(w_shifted, n)
                A.activation(w_next[:, :, :], w_next[:, :, :], ACT.Exp).then_inc(w_exp, 1)

            def carry(b):
                act.wait_ge(q1T_psum, b + 1)
                copy(q1T[:, :], psF[0:D, :], q1T_ready, scale=D ** -0.5)

            def post(b):
                n = b + 1
                for h in range(H):
                    act.wait_ge(kv_psum, b * H + (h + 1))
                    copy(kvT[:, h, :], (psH, psE)[h % 2][:, 0:P], kv_ready)
                act.wait_ge(vo_psum, n)
                copy(vo[:, :], psH[:, :], vo_ready)
                act.wait_ge(s1_shifted, n)
                A.activation(prob1[:, :, :], prob1[:, :, :], ACT.Exp).then_inc(s1_exp, 1)
                act.wait_ge(p1T_psum, n)
                copy(prob1T[:, :, :], psF[:, :].rearrange("p (h t) -> p h t", h=H), p1T_ready)
                act.wait_ge(hkT_psum, n)
                copy(hkT[:, :], psE[:, 0:P], hkT_ready)
                act.wait_ge(kvr_psum, n)
                A.activation(kvr[:, 0:2, :], psE[0:D, 0:2 * P].rearrange("p (a t) -> p a t", t=P), ACT.Copy).then_inc(kv_copied, 1)
                A.activation(kvr[:, 2, :], psE[0:D, 2 * P:3 * P], ACT.Exp, scale=-1.0).then_inc(kvr_ready, 1)
                act.wait_ge(ex_shifted, n)
                A.activation(ex[:, :, :], ex[:, :, :], ACT.Exp).then_inc(ex_done, 1)
                act.wait_ge(h2T_psum, n)
                copy(h2T[:, :], psE[0:D, 0:P], h2T_ready)
                act.wait_ge(kk_psum, n)
                A.activation(kk[:, :, :], psE[:, 0:HIDC * P].rearrange("p (c t) -> p c t", t=P), ACT.Relu).then_inc(relu_done, 1)
                A.activation(sg[:, :], psE[:, HIDC * P:HIDC * P + D], ACT.Exp, scale=-1.0).then_inc(sg_ready, 1)
                act.wait_ge(relu_done, n)
                A.activation(kk[:, :, :], kk[:, :, :], ACT.Square).then_inc(kk_ready, 1)
                act.wait_ge(xmT_psum, n)
                copy(xmT[:, :], psE[0:D, 0:P], xmT_ready)
                act.wait_ge(lg_shifted, n)
                A.activation(lg[:, :], lg[:, :], ACT.Exp).then_inc(lg_exp, 1)

            pre(0)
            with act.Fori(0, NB - 1) as b:
                carry(b)
                pre(b + 1)
                post(b)
            carry(NB - 1)
            post(NB - 1)

            with act.Fori(0, NE // 2) as i:
                for q in range(2):
                    e = i * 2 + q
                    act.wait_ge(exT_psum, e + 1)
                    copy(ex_T[:, :], psF[0:D, 0:CAP], exT_ready)
                    act.wait_ge(ew_loaded[q], i * 80 + 80)
                    for c in range(FC):
                        act.wait_ge(eh_psum, e * FC + (c + 1))
                        A.activation(ex_h[:, c, :], psB[:, 0:CAP], ACT.Relu, bias=eb1[:, q, c:c + 1]).then_inc(eh_ready, 1)

        @block.tensor
        def _(pe):
            T = nc.tensor
            SPLIT = ((0, 512), (512, CAP))

            pe.wait_ge(loaded, ALL_LOADED)
            pe.wait_ge(consts_done, 1)
            for k in range(20):
                if k < 16:
                    src = heads_in[:, k // 4, (k % 4) * P:(k % 4 + 1) * P]
                else:
                    src = pk_in[:, (k - 16) // 2, (k % 2) * P:(k % 2 + 1) * P]
                mm = T.transpose([psA, psD, psE][k // 8][:, (k % 8) * D:(k % 8 + 1) * D], src, ident[0:D, 0:D])
                if k % 8 == 7 or k == 19:
                    mm.then_inc(wT_psum, 1)
            pe.wait_ge(wT_ready, 3)
            for h in range(H):
                r, j = slice(D * (h % 2), D * (h % 2) + D), h // 2
                o = psB[0:D, 512 * (h % 2):512 * (h % 2) + 512]
                T.matmul(o[:, j * D:(j + 1) * D], wT[r, j, :], wT[r, 4 + j, :], start=True, stop=True)
                T.matmul(o[:, (4 + j) * D:(5 + j) * D], wT[r, 8 + j, :], wout[r, j, :], start=True, stop=True)
            for u in range(2 * H):
                g, j = u % 4, u // 4
                r = slice(DKEY * g, DKEY * g + DKEY)
                mm = T.matmul(PK_BANKS[g][0:D, j * KEYS:(j + 1) * KEYS], wT[r, 12 + j, :], wT[r, 16 + j, :], start=True, stop=True)
            mm.then_inc(fold_psum, 1)
            pe.wait_ge(fold_ready, 8)
            pe.wait_ge(compln_ready, 1)
            for c in range(2):
                T.transpose(psA[0:D, c * P:(c + 1) * P], compln[:, c, :], ident[:, :])
            T.transpose(psA[0:D, 2 * P:2 * P + OPV], opsb[:, :], ident[0:OPV, 0:OPV]).then_inc(compT_psum, 1)
            pe.wait_ge(compT_ready, 2)
            for c in range(2):
                T.matmul(psD[:, c * D:(c + 1) * D], compT[:, c * P:(c + 1) * P], wbL[:, :], start=True, stop=True)
                T.matmul(psD[:, (2 + c) * D:(3 + c) * D], compT[:, c * P:(c + 1) * P], wbR[:, :], start=True, stop=True)
            T.matmul(psD[0:OPV, 4 * D:5 * D], opT[:, :], wb0[:, :], start=True, stop=True).then_inc(tab_psum, 1)
            pe.wait_ge(tab_ready, 3)

            with pe.Fori(0, STILES) as s:
                pe.wait_ge(hot_ready, s + 1)
                pe.wait_ge(root_ready, s)
                for m in range(4):
                    o = psB[:, m * D:(m + 1) * D]
                    for c in range(2):
                        T.matmul(o, leaf_hot[:, c, 2 * m, :], tabL[:, c, :], start=(c == 0), stop=False)
                        T.matmul(o, leaf_hot[:, c, 2 * m + 1, :], tabR[:, c, :], start=False, stop=False)
                    mm = T.matmul(o, op_hot[:, m, :], tab0[:, :], start=False, stop=True)
                mm.then_inc(level_psum, 1)
                for level in range(2):
                    n = 2 - level
                    pe.wait_ge(node_ready, s * 2 + (level + 1))
                    for m in range(n):
                        mm = T.transpose(psA[:, m * P:(m + 1) * P], node[:, 2 * m:2 * m + 2, :].rearrange("p a d -> p (a d)"), ident[:, :])
                    mm.then_inc(nodeT_psum, 1)
                    pe.wait_ge(nodeT_ready, s * 2 + (level + 1))
                    for m in range(n):
                        o = psB[:, m * D:(m + 1) * D]
                        T.matmul(o, nodeT[:, m, :], wbLR[:, :], start=True, stop=False)
                        mm = T.matmul(o, op_hot[:, (4, 6)[level] + m, :], tab0[:, :], start=False, stop=True)
                    mm.then_inc(level_psum, 1)

            def pre(b):
                n = b + 1
                pe.wait_ge(hn_ready, n)
                T.transpose(psA[:, 0:P], hn[:, :], ident[:, :]).then_inc(hnT_psum, 1)
                pe.wait_ge(hnT_ready, n)
                pe.wait_ge(sim_read, b)
                for h in range(H):
                    mm = T.matmul(psB[0:D, h * P:(h + 1) * P], wqk[:, h * D:(h + 1) * D], hnT[:, :], start=True, stop=True)
                mm.then_inc(qT_psum, 1)
                T.matmul(psD[:, :], hnT[0:D, :], wvo[:, :], start=True, stop=True).then_inc(val_psum, 1)
                pe.wait_ge(qT_ready, n)
                for h in range(H):
                    mm = T.matmul(psB[:, h * P:(h + 1) * P], qT[:, h * P:(h + 1) * P], hnT[0:D, :], start=True, stop=True)
                mm.then_inc(s_psum, 1)
                pe.wait_ge(p_ready, n)
                for h in range(H):
                    mm = T.transpose(psB[:, h * P:(h + 1) * P], prob[:, h, :], ident[:, :])
                mm.then_inc(pT_psum, 1)
                pe.wait_ge(pT_ready, n)
                pe.wait_ge(val_ready, n)
                for h in range(H):
                    mm = T.matmul(psA[:, 0:D], probT[:, h, :], val[:, h * D:(h + 1) * D], start=(h == 0), stop=(h == H - 1))
                mm.then_inc(att_psum, 1)
                pe.wait_ge(x_ready, n)
                T.transpose(psA[:, 0:P], hn[:, :], ident[:, :]).then_inc(xT_psum, 1)
                pe.wait_ge(xT_ready, n)
                for p in range(2):
                    mm = T.matmul(psB[:, p * 512:(p + 1) * 512], xT[0:D, :], wpk[:, p * 512:(p + 1) * 512], start=True, stop=True)
                mm.then_inc(sim_psum, 1)

            def carry(b):
                pe.wait_ge(xT_ready, b + 1)
                for h in range(H):
                    mm = T.matmul(psF[0:D, h * P:(h + 1) * P], wq1[:, h * D:(h + 1) * D], xT[:, :], start=True, stop=True)
                mm.then_inc(q1T_psum, 1)

            def post(b):
                n = b + 1
                for h in range(H):
                    pe.wait_ge(diag_ready, b * H + (h + 1))
                    pe.wait_ge(gathered[h], b * 256 + 256)
                    if h >= 2:
                        pe.wait_ge(kv_ready, b * H + (h - 1))
                    for k in range(TOPK):
                        mm = T.matmul((psH, psE)[h % 2][:, 0:P], mem[:, h, k, :], diag[:, h % 2, k, :],
                                      start=(k == 0), stop=(k == TOPK - 1))
                    mm.then_inc(kv_psum, 1)
                pe.wait_ge(kv_ready, b * H + H)
                pe.wait_ge(q1T_ready, n)
                for h in range(H):
                    mm = T.matmul(psF[:, h * P:(h + 1) * P], q1T[:, h * P:(h + 1) * P], kvT[0:D, h, :], start=True, stop=True)
                mm.then_inc(s1_psum, 1)
                for h in range(H):
                    mm = T.matmul(psH[:, h * D:(h + 1) * D], kvT[D:P, h, :], wo1[D:P, h, :], start=True, stop=True)
                mm.then_inc(vo_psum, 1)
                pe.wait_ge(p1_ready, n)
                for h in range(H):
                    mm = T.transpose(psF[:, h * P:(h + 1) * P], prob1[:, h, :], ident[:, :])
                mm.then_inc(p1T_psum, 1)
                pe.wait_ge(p1T_ready, n)
                pe.wait_ge(vo_ready, n)
                for h in range(H):
                    mm = T.matmul(psE[:, 0:D], prob1T[:, h, :], vo[:, h * D:(h + 1) * D], start=(h == 0), stop=(h == H - 1))
                mm.then_inc(att1_psum, 1)
                pe.wait_ge(hk_ready, n)
                T.transpose(psE[:, 0:P], hk[:, :], ident[:, :]).then_inc(hkT_psum, 1)
                pe.wait_ge(hkT_ready, n)
                for k, w in enumerate((rk, rv, rr)):
                    mm = T.matmul(psE[0:D, k * P:(k + 1) * P], w, hkT[:, :], start=True, stop=True)
                mm.then_inc(kvr_psum, 1)
                pe.wait_ge(ysr_ready, n)
                T.matmul(psE[:, 0:D], ysr[:, :], ro[0:D], start=True, stop=True).then_inc(ro_psum, 1)
                pe.wait_ge(h2_ready, n)
                T.transpose(psE[:, 0:P], hk[:, :], ident[:, :]).then_inc(h2T_psum, 1)
                pe.wait_ge(h2T_ready, n)
                for c in range(HIDC):
                    T.matmul(psE[:, c * P:(c + 1) * P], wkf[:, c * P:(c + 1) * P], h2T[:, :], start=True, stop=True)
                T.matmul(psE[:, HIDC * P:HIDC * P + D], h2T[:, :], rrf[0:D], start=True, stop=True).then_inc(kk_psum, 1)
                pe.wait_ge(kk_ready, n)
                pe.wait_ge(sg_ready, n)
                for c in range(HIDC):
                    mm = T.matmul(psE[:, 0:D], kk[:, c, :], wvf[:, c, :], start=(c == 0), stop=(c == HIDC - 1))
                mm.then_inc(ffn_psum, 1)
                pe.wait_ge(xm_ready, n)
                T.transpose(psE[:, 0:P], xm[:, :], ident[:, :]).then_inc(xmT_psum, 1)
                pe.wait_ge(xmT_ready, n)
                T.matmul(psE[:, 0:NE], xmT[:, :], gate_w[:, :], start=True, stop=True).then_inc(gate_psum, 1)
                pe.wait_ge(oh_ready, n)
                T.matmul(psE[:, 64:64 + NE], upto[:, :], oh[:, :], start=True, stop=True)
                T.matmul(psE[:, 128:128 + NE], ones[:, :], oh[:, :], start=True, stop=True).then_inc(cum_psum, 1)

            pe.wait_ge(root_ready, STILES)
            pre(0)
            with pe.Fori(0, NB - 1) as b:
                carry(b)
                pre(b + 1)
                post(b)
            carry(NB - 1)
            post(NB - 1)

            with pe.Fori(0, NE // 2) as i:
                for q in range(2):
                    e = i * 2 + q
                    pe.wait_ge(ew_loaded[q], i * 80 + 80)
                    pe.wait_ge(ey_ready, e)
                    for j in range(ETILES):
                        mm = T.transpose(psF[:, j * P:(j + 1) * P], ex_in[:, q, j, :], ident[:, :])
                    mm.then_inc(exT_psum, 1)
                    pe.wait_ge(exT_ready, e + 1)
                    for c in range(FC):
                        if c:
                            pe.wait_ge(eh_ready, e * FC + c)
                        for a, z in SPLIT:
                            mm = T.matmul(psB[:, a:z], w1[:, q, c * P:(c + 1) * P], ex_T[:, a:z], start=True, stop=True)
                        mm.then_inc(eh_psum, 1)
                    pe.wait_ge(eh_ready, e * FC + FC)
                    for j in range(ETILES):
                        for c in range(FC):
                            mm = T.matmul(psF[:, j * D:(j + 1) * D], ex_h[:, c, j * P:(j + 1) * P], w2[:, q, c, :],
                                          start=(c == 0), stop=(c == FC - 1))
                    mm.then_inc(ey_psum, 1)


_KV = ("L0_ffn_keys_table", "L0_ffn_values_table")


def kernel(**inputs):
    import concourse.bacc as _bacc
    from concourse.bass_utils import run_bass_kernel_spmd as _run

    nc = _bacc.Bacc("TRN2", target_bir_lowering=False, num_devices=1)
    given = {k: np.ascontiguousarray(v) for k, v in inputs.items() if k not in _KV}
    given["kv_table"] = np.concatenate([np.asarray(inputs[k]) for k in _KV], axis=1)
    arrays, aps = {}, {}
    for name, a in given.items():
        arrays[f"in_{name}"] = a
        aps[name] = nc.dram_tensor(f"in_{name}", a.shape, mybir.dt.from_np(a.dtype), kind="ExternalInput").ap()
    out = nc.dram_tensor("out_0", (NB, P, D), F32, kind="ExternalOutput").ap()
    tower(nc, aps, out)
    r = _run(nc, [arrays], core_ids=[0])
    return r.results[0]["out_0"]
```

```python
import numpy as np
import concourse.bass as bass
from concourse import mybir
from contextlib import ExitStack

F32 = mybir.dt.float32
BF16 = mybir.dt.bfloat16
I32 = mybir.dt.int32
U32 = mybir.dt.uint32
ALU = mybir.AluOpType
ACT = mybir.ActivationFunctionType
AX = mybir.AxisListType

P = 128
D = 64
NB = 32
H = 8
EPS = 1e-5
NSTRUCT, NLEAF, NOPS, VOCAB, OPV = 2048, 8, 7, 256, 64
STILES = 2
SROUNDS = NSTRUCT // P // STILES
LEVELS = (4, 2, 1)
KEYS, TOPK, DKEY = 64, 16, 32
NUM_KV = KEYS * KEYS
ROWS = [TOPK // (i + 1) for i in range(TOPK)]
OFFS = [sum(ROWS[:i]) for i in range(TOPK)]
NCAND = sum(ROWS)
NE, F = 8, 256
FC = F // P
CAP = -(-5 * NB * P // (4 * NE))
ETILES = CAP // P
YGROUPS = 4
YB = NB // YGROUPS
SLOTS = NE * CAP
HIDC = 256 // P

NEG = -3.0e38
HUGE = 3.4028234663852886e38
MAGIC = float(0x5F3759DF)

class Steps:

    def __init__(self, eng, sem):
        self.eng, self.sem, self.n = eng, sem, 0

    def inc(self, ins):
        self.n += 1
        ins.then_inc(self.sem, 1)

    def settle(self):
        self.eng.wait_ge(self.sem, self.n)

    def seq(self, ins):
        self.inc(ins)
        self.settle()

    def restart(self):
        self.settle()
        self.eng.sem_clear(self.sem)


def weave(*stages):
    stages = list(stages)
    while stages:
        for stage in list(stages):
            try:
                next(stage)
            except StopIteration:
                stages.remove(stage)


def tower(nc, t, out):
    ctx = ExitStack()
    with ctx:
        def sb(name, shape, dt=F32):
            return ctx.enter_context(nc.sbuf_tensor(name, shape, dt))

        def sem(name):
            return ctx.enter_context(nc.semaphore(name))

        def cast_cols(ap, n):
            return ap.unsqueeze(2).to_broadcast([ap.shape[0], ap.shape[1], n])

        def rows_n(ap, n):
            return ap.unsqueeze(1).to_broadcast([ap.shape[0], n, ap.shape[1]])

        root_table = nc.dram_tensor("root_table", [NSTRUCT, D], F32, kind="Internal").ap()
        slots_x = nc.dram_tensor("slots_x", [SLOTS, D], F32, kind="Internal").ap()
        slots_y = nc.dram_tensor("slots_y", [SLOTS, D], F32, kind="Internal").ap()

        mem = sb("mem", [P, H, TOPK, P])
        memf = mem[:, :, :, :].rearrange("p h k d -> p (h k d)")
        lent = [0]

        def lend(parts, *shape, dt=F32):
            n = int(np.prod(shape)) // (2 if dt is BF16 else 1)
            ap = memf[0:parts, lent[0]:lent[0] + n]
            lent[0] += n
            if dt is not F32:
                ap = ap.bitcast(dt)
            names = "abc"[:len(shape)]
            return ap if len(shape) == 1 else ap.rearrange(
                f"p ({' '.join(names)}) -> p {' '.join(names)}", **dict(zip(names, shape)))

        comp = sb("comp", [P, 2, D])
        opsb = sb("opsb", [OPV, D])
        wb0, wbL, wbR = sb("wb0", [D, D]), sb("wbL", [D, D]), sb("wbR", [D, D])
        wbLR = sb("wbLR", [2 * D, D])
        gb_cols = sb("gb_cols", [2 * D, 2])
        wbLR_g = sb("wbLR_g", [2 * D, D])
        vec_names = ["L0_tok_b_bin", "L0_tok_gamma", "L0_tok_beta", "L0_attn_bout",
                     "L1_attn_g1", "L1_attn_b1", "L1_attn_g2", "L1_attn_b2"]
        vecs = sb("vecs", [P, len(vec_names), D])
        b_bin, gamma, beta, bout, g1, b1, g2, b2 = [vecs[:, k, :] for k in range(8)]
        gate_b = sb("gate_b", [P, NE])
        heads_in = lend(D, 4, H * D)
        wout = lend(2 * D, H // 2, D)
        pk_in = lend(KEYS, 2, H * DKEY)
        wT = lend(P, 20, D)
        wqk = sb("wqk", [P, H * D])
        wvo = sb("wvo", [D, H * D])
        wpk = sb("wpk", [D, 2 * H * KEYS])
        wq1 = sb("wq1", [P, H * D])
        wo1 = sb("wo1", [P, H, D])
        sq_names = ["L1_attn_Wk", "L1_attn_Wv", "L1_attn_Wr", "L1_attn_Wo", "L1_attn_Wr_ffn"]
        squares = sb("squares", [P, len(sq_names), D])
        rk, rv, rr, ro, rrf = [squares[:, k, :] for k in range(5)]
        wkf = sb("wkf", [D, HIDC * P])
        wvf = sb("wvf", [P, HIDC, D])
        gate_w = sb("gate_w", [D, NE])
        wu = sb("wu", [D, 2])

        ident = sb("ident", [P, P])
        ones = sb("ones", [P, P])
        upto = sb("upto", [P, P])
        causal = sb("causal", [P, P])
        iota_part = sb("iota_part", [P, 2])
        iota_cand = sb("iota_cand", [P, NCAND])
        iota_e = sb("iota_e", [P, NE])
        rev_e = sb("rev_e", [P, NE])
        head_base = sb("head_base", [P, H, TOPK])
        zeros = sb("zeros", [P, SLOTS * D // P // 4])

        compln = sb("compln", [P, 2, D])
        compT = sb("compT", [D, 2 * P])
        opT = sb("opT", [D, OPV])
        tab = sb("tab", [P, 6, D])
        LEFT, RIGHT, OP_LEAF, OP_UPPER = 0, 2, 4, 5
        tab_parts = sb("tab_parts", [P, 3, 6, D], BF16)
        beta_rep = sb("beta_rep", [2 * D, OPV])
        SP = STILES * P
        leaf_ids = lend(P, SP * NLEAF, dt=I32)
        op_ids = lend(OPV, SP * NOPS, dt=I32)
        leaf_hot = lend(P, 2, NLEAF, SP, dt=BF16)
        op_hot = lend(OPV, NOPS, SP, dt=BF16)
        roots = lend(P, NSTRUCT // P, D)
        node = [sb(f"node{k}", [P, STILES * LEVELS[k], D]) for k in range(2)]
        nodeT = [sb(f"nodeT{k}", [P, STILES * LEVELS[k + 1], P]) for k in range(2)]

        def norm_scratch(name, n):
            return (sb(f"{name}_stats", [P, n, 6]), sb(f"{name}_mean_var", [P, n, 2]), sb(f"{name}_v", [P, n]),
                    sb(f"{name}_bits", [P, n], I32), sb(f"{name}_y", [P, n], I32), sb(f"{name}_a", [P, n]))

        ln_struct, ln_pre, ln_tail = norm_scratch("struct", STILES * LEVELS[0]), norm_scratch("pre", 1), norm_scratch("tail", 1)

        x_ids = sb("x_ids", [P, NB], I32)
        hid = sb("hid", [P, NB * D])
        hn = sb("hn", [P, 2 * D])
        hnT = sb("hnT", [P, P])
        qT = sb("qT", [D, H * P])
        val = sb("val", [P, H * D])
        prob = sb("prob", [P, H, P])
        probT = sb("probT", [P, H, P])
        soft_pre = sb("mx_pre", [P, H]), sb("zs_pre", [P, H])
        soft_tail = sb("mx_tail", [P, H]), sb("zs_tail", [P, H])
        att = sb("att", [P, D])
        xT = sb("xT", [P, P])
        sim = sb("sim", [P, 2 * H, KEYS])
        top = sb("top", [P, 2 * H, TOPK])
        topi = sb("topi", [P, 2 * H, TOPK], U32)
        topf = sb("topf", [P, 2 * H, TOPK])
        cand = sb("cand", [P, H, NCAND])
        cand2 = sb("cand2", [P, H, NCAND])
        candi = sb("candi", [P, H, NCAND])
        fin = sb("fin", [P, H, TOPK])
        fini = sb("fini", [P, H, TOPK], U32)
        finp = sb("finp", [P, H, TOPK])
        hot = sb("hot", [P, 2, TOPK, NCAND])
        rowf = sb("rowf", [P, H, TOPK])
        row_next = sb("row_next", [P, H * TOPK], I32)
        w_next = sb("w_next", [P, H, TOPK])
        wz = sb("wz", [P, H])
        row_now = sb("row_now", [P, H * TOPK], I32)
        w_now = sb("w_now", [P, H, TOPK])
        q1T = sb("q1T", [D, H * P])
        diag = sb("diag", [P, 2, TOPK, P])
        kvT = sb("kvT", [P, H, P])
        prob1 = sb("prob1", [P, H, P])
        prob1T = sb("prob1T", [P, H, P])
        vo = sb("vo", [P, H * D])
        x3 = sb("x3", [P, D])
        hk = sb("hk", [P, 2 * D])
        hkT = sb("hkT", [P, P])
        kvr = sb("kvr", [D, 3, P])
        om = sb("om", [D, P + 1])
        uk = sb("uk", [D, P])
        nom = sb("nom", [D, P])
        wdec = sb("wdec", [D, P])
        ex = sb("ex", [D, 4, P])
        ev = sb("ev", [D, P])
        pst = sb("pst", [D, P + 1])
        qst = sb("qst", [D, P + 1])
        num = sb("num", [D, P])
        den = sb("den", [D, P])
        ysr = sb("ysr", [D, P])
        x4 = sb("x4", [P, D])
        h2T = sb("h2T", [D, P])
        kk = sb("kk", [P, HIDC, P])
        sg = sb("sg", [P, D])
        xm = sb("xm", [P, 2 * D])
        xmT = sb("xmT", [D, P])
        lg = sb("lg", [P, NE])
        oh = sb("oh", [P, NE])
        sc8 = sb("sc8", [P, NE])
        cum = sb("cum", [P, NE])
        tick_pool, tick_dve = sb("tick_pool", [P, 1]), sb("tick_dve", [P, 2])
        count = sb("count", [P, NE])
        g4 = sb("g4", [P, 8])
        slot_s = sb("slot_s", [P, 1], I32)
        slot_g = sb("slot_g", [P, NB], I32)
        keep = sb("keep", [P, NB])
        lent[0] = 3 * NB * D
        w1 = lend(D, 2, F)
        w2 = lend(P, 2, FC * D).rearrange("p q (c d) -> p q c d", d=D)
        eb1 = lend(P, 2, FC)
        eb2 = lend(P, 2, D)
        ex_in = sb("ex_in", [P, 2, ETILES, 2 * D])
        ex_T = lend(D, CAP)
        ex_h = lend(P, FC, CAP)
        ex_y = lend(P, NE * ETILES, D)

        y_tok = memf[:, 0:NB * D]
        y_bad = memf[:, NB * D:2 * NB * D]
        y_fill = memf[:, 2 * NB * D:3 * NB * D]

        psA = ctx.enter_context(nc.psum_tensor("psA", [P, 512], F32))
        psB = ctx.enter_context(nc.psum_tensor("psB", [P, 1024], F32))
        psD = ctx.enter_context(nc.psum_tensor("psD", [P, 512], F32))
        psE = ctx.enter_context(nc.psum_tensor("psE", [P, 512], F32))
        psF = ctx.enter_context(nc.psum_tensor("psF", [P, 1024], F32))
        psH = ctx.enter_context(nc.psum_tensor("psH", [P, 512], F32))

        PK_BANKS = (psA, psD, psE, psH)
        level_bank = (psB[:, 0:STILES * LEVELS[0] * D], psB[:, 512:512 + STILES * LEVELS[1] * D], psD[:, 0:STILES * LEVELS[2] * D])
        nodeT_bank = (psA[:, 0:STILES * LEVELS[1] * P], psE[:, 0:STILES * LEVELS[2] * P])

        tree_loaded, loaded = sem("tree_loaded"), sem("loaded")
        consts_done = sem("consts_done")
        pool_steps, pool_ticks = sem("pool_steps"), sem("pool_ticks")
        zero_filled = sem("zero_filled")
        wT_psum, wT_ready = sem("wT_psum"), sem("wT_ready")
        fold_psum, fold_ready = sem("fold_psum"), sem("fold_ready")
        compln_ready = sem("compln_ready")
        compT_psum, compT_ready = sem("compT_psum"), sem("compT_ready")
        beta_ready = sem("beta_ready")
        tab_psum, tab_ready = sem("tab_psum"), sem("tab_ready")
        dve_setup = sem("dve_setup")
        leaf_ids_loaded, op_ids_loaded = sem("leaf_ids_loaded"), sem("op_ids_loaded")
        leaf_hot_ready, op_hot_ready = sem("leaf_hot_ready"), sem("op_hot_ready")
        level_psum = [sem(f"level_psum{k}") for k in range(3)]
        node_ready = [sem(f"node_ready{k}") for k in range(2)]
        nodeT_psum, nodeT_ready = [[sem(f"{name}{k}") for k in range(2)] for name in ("nodeT_psum", "nodeT_ready")]
        roots_ready, root_stored = sem("roots_ready"), sem("root_stored")
        roots_masked, embedded_first, embedded = sem("roots_masked"), sem("embedded_first"), sem("embedded")
        dve_struct = sem("dve_struct")

        dve_pre = sem("dve_pre")
        hn_ready, hnT_psum, hnT_ready = sem("hn_ready"), sem("hnT_psum"), sem("hnT_ready")
        qT_psum, qT_ready, val_psum, val_ready = sem("qT_psum"), sem("qT_ready"), sem("val_psum"), sem("val_ready")
        s_psum, s_shifted, s_exp, p_ready = sem("s_psum"), sem("s_shifted"), sem("s_exp"), sem("p_ready")
        pT_psum, pT_ready, att_psum = sem("pT_psum"), sem("pT_ready"), sem("att_psum")
        x_ready, xT_psum, xT_ready, sim_psum = sem("x_ready"), sem("xT_psum"), sem("xT_ready"), sem("sim_psum")
        sim_read = sem("sim_read")
        w_shifted, w_exp, found = sem("w_shifted"), sem("w_exp"), sem("found")

        w_now_ready, q1T_psum, q1T_ready = sem("w_now_ready"), sem("q1T_psum"), sem("q1T_ready")
        rows_ready = sem("rows_ready")
        gathered = [sem(f"gathered{h}") for h in range(H)]

        dve_tail = sem("dve_tail")
        diag_ready, kv_psum, kv_ready = sem("diag_ready"), sem("kv_psum"), sem("kv_ready")
        s1_read = sem("s1_read")
        s1_psum, s1_shifted, s1_exp, p1_ready = sem("s1_psum"), sem("s1_shifted"), sem("s1_exp"), sem("p1_ready")
        vo_psum, vo_ready = sem("vo_psum"), sem("vo_ready")
        p1T_psum, p1T_ready, att1_psum = sem("p1T_psum"), sem("p1T_ready"), sem("att1_psum")
        hk_ready, hkT_psum, hkT_ready = sem("hk_ready"), sem("hkT_psum"), sem("hkT_ready")
        kvr_psum, kvr_ready = sem("kvr_psum"), sem("kvr_ready")
        ex_shifted, ex_done, ysr_ready, ro_psum = sem("ex_shifted"), sem("ex_done"), sem("ysr_ready"), sem("ro_psum")
        h2_ready, h2T_psum, h2T_ready = sem("h2_ready"), sem("h2T_psum"), sem("h2T_ready")
        kk_psum, relu_done, kk_ready, ffn_psum = sem("kk_psum"), sem("relu_done"), sem("kk_ready"), sem("ffn_psum")
        kv_copied, sg_ready = sem("kv_copied"), sem("sg_ready")
        xm_ready, xmT_psum, xmT_ready = sem("xm_ready"), sem("xmT_psum"), sem("xmT_ready")
        gate_psum, lg_shifted, lg_exp = sem("gate_psum"), sem("lg_shifted"), sem("lg_exp")
        oh_ready, cum_psum, slot_ready = sem("oh_ready"), sem("cum_psum"), sem("slot_ready")
        scattered = sem("scattered")

        x_loaded, w1_loaded, w2_loaded = [[sem(f"{name}{q}") for q in range(2)] for name in ("x_loaded", "w1_loaded", "w2_loaded")]
        exT_psum, exT_ready = sem("exT_psum"), sem("exT_ready")
        eh_psum, eh_ready = sem("eh_psum"), sem("eh_ready")
        ey_psum, ey_ready, ey_stored = sem("ey_psum"), sem("ey_ready"), sem("ey_stored")
        y_gathered = [sem(f"y_gathered{g}") for g in range(YGROUPS)]
        dve_last, out_ready, out_stored = sem("dve_last"), sem("out_ready"), sem("out_stored")

        block = ctx.enter_context(nc.Block())
        loads = []

        def load(dst, src):
            loads.append((dst, src))

        for c in range(2):
            load(comp[:, c, :], t["L0_tok_comp_emb"][c * P:(c + 1) * P, :])
        load(opsb[:, :], t["L0_tok_op_emb"])
        load(wb0[:, :], t["L0_tok_W_bin"][0:D, :])
        load(wbL[:, :], t["L0_tok_W_bin"][D:2 * D, :])
        load(wbR[:, :], t["L0_tok_W_bin"][2 * D:3 * D, :])
        load(wbLR[:, :], t["L0_tok_W_bin"][D:3 * D, :])
        for k, name in enumerate(["L0_tok_gamma", "L0_tok_beta"]):
            for half in range(2):
                load(gb_cols[half * D:(half + 1) * D, k:k + 1], t[name].rearrange("(c o) -> c o", o=1))
        for k, name in enumerate(vec_names[:3]):
            load(vecs[:, k, :], t[name].partition_broadcast(P))
        tree_loads, loads = loads, []
        for k, name in enumerate(vec_names[3:]):
            load(vecs[:, 3 + k, :], t[name].partition_broadcast(P))
        load(gate_b[:, :], t["L1_ffn_gate_b"].partition_broadcast(P))
        for k, name in enumerate(["L0_attn_WQ", "L0_attn_WK", "L0_attn_WV", "L0_ffn_Wq_pk"]):
            load(heads_in[:, k, :], t[name])
        load(wout[:, :, :], t["L0_attn_Wout"].rearrange("(j p) o -> p j o", p=2 * D))
        load(pk_in[:, :, :], t["L0_ffn_pk_keys"].rearrange("p k h d -> k p (h d)"))
        load(wq1[0:D, :], t["L0_ffn_Wq"])
        load(wo1[D:P, :, :], t["L0_ffn_Wo"].rearrange("(h d) o -> d h o", d=D))
        for k, name in enumerate(sq_names):
            load(squares[0:D, k, :], t[name])
        load(wkf[:, :], t["L1_attn_Wk_ffn"])
        load(wvf[:, :, :], t["L1_attn_Wv_ffn"].rearrange("(c p) o -> p c o", p=P))
        load(gate_w[:, :], t["L1_ffn_gate_w"])
        load(wu[:, 0:1], t["L1_attn_spatial_decay"].rearrange("(c o) -> c o", o=1))
        load(wu[:, 1:2], t["L1_attn_spatial_first"].rearrange("(c o) -> c o", o=1))
        load(x_ids[:, :], t["x"].rearrange("b t -> t b"))
        ALL_TREE_LOADED, ALL_LOADED = 16 * len(tree_loads), 16 * len(loads)

        @block.sync
        def _(sp):
            leaf_rows = t["L0_tok_leaf_ids"].rearrange("(s p) n -> s (p n)", p=SP)
            op_rows = t["L0_tok_op_ids"].rearrange("(s p) n -> s (p n)", p=SP)

            def load_leaf_ids(s):
                sp.dma_start(leaf_ids[:, :], leaf_rows[bass.ds(s, 1), :].to_broadcast([P, SP * NLEAF])).then_inc(leaf_ids_loaded, 16)

            def load_op_ids(s):
                sp.dma_start(op_ids[:, :], op_rows[bass.ds(s, 1), :].to_broadcast([OPV, SP * NOPS])).then_inc(op_ids_loaded, 16)

            for dst, src in tree_loads:
                sp.dma_start(dst, src, allow_slow_non_contiguous=True).then_inc(tree_loaded, 16)
            load_leaf_ids(0)
            load_op_ids(0)
            for dst, src in loads:
                sp.dma_start(dst, src, allow_slow_non_contiguous=True).then_inc(loaded, 16)
            sp.wait_ge(consts_done, 1)
            for k in range(4):
                sp.dma_start(slots_x.rearrange("(a p r) d -> a p (r d)", a=4, p=P)[k], zeros[:, :]).then_inc(zero_filled, 16)
            with sp.Fori(1, SROUNDS) as s:
                sp.wait_ge(leaf_hot_ready, s * 2)
                load_leaf_ids(s)
                sp.wait_ge(op_hot_ready, s * 2)
                load_op_ids(s)
            sp.wait_ge(roots_masked, 1)
            sp.dma_start(root_table.rearrange("(s p) d -> p s d", p=P), roots[:, :, :]).then_inc(root_stored, 16)

            x_rows = slots_x.rearrange("(e j p) d -> e p j d", p=P, j=ETILES)
            y_rows = slots_y.rearrange("(e j p) d -> e p j d", p=P, j=ETILES)
            w2_rows = t["L1_ffn_w2"].rearrange("e (c p) d -> e p c d", p=P)
            b1_rows = t["L1_ffn_b1"].rearrange("e (c p) -> e p c", p=P)

            def load_x(e, q):
                sp.dma_start(ex_in[:, q, :, 0:D], x_rows[bass.ds(e, 1)].rearrange("a p j d -> (a p) j d")).then_inc(x_loaded[q], 16)

            def load_first_map(e, q):
                sp.dma_start(w1[:, q, :], t["L1_ffn_w1"][bass.ds(e, 1), :, :].rearrange("a d f -> (a d) f")).then_inc(w1_loaded[q], 16)
                sp.dma_start(eb1[:, q, :], b1_rows[bass.ds(e, 1)].rearrange("a p c -> (a p) c"),
                             allow_slow_non_contiguous=True).then_inc(w1_loaded[q], 16)

            def load_second_map(e, q):
                sp.dma_start(w2[:, q, :, :], w2_rows[bass.ds(e, 1)].rearrange("a p c d -> (a p) c d")).then_inc(w2_loaded[q], 16)
                sp.dma_start(eb2[:, q, :], t["L1_ffn_b2"][bass.ds(e, 1), :].to_broadcast([P, D])).then_inc(w2_loaded[q], 16)

            def store_y(e):
                sp.dma_start(y_rows[bass.ds(e, 1)].rearrange("a p j d -> (a p) j d"),
                             ex_y[:, bass.ds(e * ETILES, ETILES), :]).then_inc(ey_stored, 16)

            sp.wait_ge(kv_psum, NB * H)
            for q in range(2):
                load_first_map(q, q)
                load_second_map(q, q)
            sp.wait_ge(scattered, 16 * NB)
            for q in range(2):
                load_x(q, q)
            with sp.Fori(0, NE // 2 - 1) as i:
                for q in range(2):
                    e = i * 2 + q
                    sp.wait_ge(exT_psum, e + 1)
                    load_x(e + 2, q)
                    sp.wait_ge(eh_ready, e * FC + FC)
                    load_first_map(e + 2, q)
                    sp.wait_ge(ey_ready, e + 1)
                    store_y(e)
                    load_second_map(e + 2, q)
            for e in (NE - 2, NE - 1):
                sp.wait_ge(ey_ready, e + 1)
                store_y(e)
            out_rows = out.rearrange("b t d -> t b d")
            for g in range(YGROUPS):
                sp.wait_ge(out_ready, g + 1)
                sp.dma_start(out_rows[:, g * YB:(g + 1) * YB, :],
                             hid[:, g * YB * D:(g + 1) * YB * D].rearrange("p (b d) -> p b d", d=D)).then_inc(out_stored, 16)
            sp.wait_ge(out_stored, 16 * YGROUPS)
            sp.wait_ge(zero_filled, 64)
            sp.wait_ge(ey_stored, 16 * NE)
            sp.wait_ge(root_stored, 16)

        @block.gpsimd
        def _(pool):
            st = Steps(pool, pool_steps)
            st.inc(pool.memset(ident[:, :], 0.0))
            st.inc(pool.memset(ones[:, :], 1.0))
            st.inc(pool.memset(upto[:, :], 1.0))
            st.inc(pool.memset(causal[:, :], 0.0))
            st.inc(pool.memset(zeros[:, :], 0.0))
            for pad in (hn[:, D:2 * D], hk[:, D:2 * D], xm[:, D:2 * D], ex_in[:, :, :, D:2 * D]):
                st.inc(pool.memset(pad, 0.0))
            st.settle()
            for pad in (wqk[D:P, :], wq1[D:P, :], squares[D:P, :, :]):
                st.inc(pool.memset(pad, 0.0))
            st.settle()
            st.inc(pool.iota(iota_cand[:, :], [[1, NCAND]], 0, 0, allow_small_or_imprecise_dtypes=True))
            st.inc(pool.iota(iota_e[:, :], [[1, NE]], 0, 0, allow_small_or_imprecise_dtypes=True))
            st.inc(pool.iota(rev_e[:, :], [[-1, NE]], NE, 0, allow_small_or_imprecise_dtypes=True))
            st.inc(pool.iota(iota_part[:, :], [[P, 2]], 0, 1, allow_small_or_imprecise_dtypes=True))
            st.inc(pool.iota(head_base[:, :, :], [[NUM_KV, H], [0, TOPK]], 0, 0, allow_small_or_imprecise_dtypes=True))
            st.settle()
            st.inc(pool.affine_select(out=ident[:, :], in_=ident[:, :], compare_op=ALU.not_equal, fill=1.0,
                                      base=0, pattern=[[-1, P]], channel_multiplier=1))
            st.inc(pool.affine_select(out=upto[:, :], in_=upto[:, :], compare_op=ALU.is_ge, fill=0.0,
                                      base=0, pattern=[[1, P]], channel_multiplier=-1))
            st.inc(pool.affine_select(out=causal[:, :], in_=causal[:, :], compare_op=ALU.is_ge, fill=NEG,
                                      base=0, pattern=[[-1, P]], channel_multiplier=1))
            st.settle()
            pool.memset(count[:, :], 0.0).then_inc(consts_done, 1)

            ticks = Steps(pool, pool_ticks)

            def tick():
                ticks.inc(pool.tensor_tensor(tick_pool[:, :], ones[:, 0:1], ones[:, 0:1], ALU.mult))
                ticks.restart()
                ticks.n = 0

            pool.wait_ge(loaded, ALL_LOADED)
            pool.wait_ge(root_stored, 16)
            for b in range(NB):
                pool.indirect_dma_start(out=hid[:, b * D:(b + 1) * D], out_offset=None, in_=root_table,
                                        in_offset=bass.IndirectOffsetOnAxis(ap=x_ids[:, b:b + 1], axis=0)).then_inc(embedded if b else embedded_first, 16)

            def gather(b):
                for h in range(H):
                    if h % 4 == 0:
                        pool.wait_ge(rows_ready, b * 2 + (h // 4 + 1))
                        tick()
                    for k in range(TOPK):
                        c = h * TOPK + k
                        pool.indirect_dma_start(out=mem[:, h, k, :], out_offset=None, in_=t["kv_table"],
                                                in_offset=bass.IndirectOffsetOnAxis(ap=row_now[:, c:c + 1], axis=0)).then_inc(gathered[h], 16)

            def scatter(b):
                pool.wait_ge(slot_ready, b + 1)
                tick()
                pool.indirect_dma_start(out=slots_x, out_offset=bass.IndirectOffsetOnAxis(ap=slot_s[:, 0:1], axis=0),
                                        in_=xm[:, 0:D], in_offset=None, bounds_check=SLOTS - 1,
                                        oob_is_err=False).then_inc(scattered, 16)

            gather(0)
            pool.wait_ge(zero_filled, 64)
            with pool.Fori(1, NB) as b:
                gather(b)
                scatter(b - 1)
            scatter(NB - 1)

            pool.wait_ge(ey_stored, 16 * NE)
            for b in range(NB):
                pool.indirect_dma_start(out=y_tok[:, b * D:(b + 1) * D], out_offset=None, in_=slots_y,
                                        in_offset=bass.IndirectOffsetOnAxis(ap=slot_g[:, b:b + 1], axis=0)).then_inc(y_gathered[b // YB], 16)

        @block.vector
        def _(dve):
            V = nc.vector

            def norm(st, scratch, src, n, dst, gain=None, bias=None, done=None):
                ln_st, ln_mv, ln_v, ln_i, ln_y, ln_a = scratch
                for j in range(n):
                    st.inc(V.bn_stats(ln_st[:, j, :], src[:, j, :]))
                st.settle()
                for j in range(n):
                    st.inc(V.bn_aggr(ln_mv[:, j, :], ln_st[:, j, :]))
                st.settle()
                v, y, a = ln_v[:, 0:n], ln_y[:, 0:n].bitcast(F32), ln_a[:, 0:n]
                st.seq(V.tensor_scalar(v, ln_mv[:, 0:n, 1], EPS, None, ALU.add))
                st.seq(V.tensor_scalar(ln_i[:, 0:n], v.bitcast(I32), 1, None, ALU.logical_shift_right))
                st.seq(V.tensor_scalar(ln_y[:, 0:n], ln_i[:, 0:n], -1.0, MAGIC, ALU.mult, ALU.add))
                c = 1.0
                for _ in range(3):
                    st.seq(V.tensor_tensor(a, y, y, ALU.mult))
                    st.seq(V.tensor_tensor(a, a, v, ALU.mult))
                    st.seq(V.scalar_tensor_tensor(y, a, 3.0 * c * c, y, ALU.subtract, ALU.mult))
                    c = -2.0 * c * c * c
                st.seq(V.tensor_scalar(y, y, 1.0 / c, None, ALU.mult))
                for j in range(n):
                    i = V.tensor_scalar(dst[:, j, :], src[:, j, :], ln_mv[:, j, 0:1], y[:, j:j + 1], ALU.subtract, ALU.mult)
                    if j < n - 1:
                        st.inc(i)
                if gain is not None:
                    st.seq(i)
                    st.seq(V.tensor_tensor(dst, dst, rows_n(gain, n), ALU.mult))
                    i = V.tensor_tensor(dst, dst, rows_n(bias, n), ALU.add)
                if done is None:
                    st.seq(i)
                else:
                    i.then_inc(done, 1)

            def tick(st, k=0):
                st.seq(V.memset(tick_dve[:, k:k + 1], 0.0))

            def one(ap):
                return ap.unsqueeze(1)

            def leaf_one_hot(s):
                dve.wait_ge(leaf_ids_loaded, s * 16 + 16)
                leaves = leaf_ids[:, :].rearrange("p (s n) -> p n s", n=NLEAF)
                for c in range(2):
                    V.tensor_scalar(leaf_hot[:, c, :, :], leaves, iota_part[:, c:c + 1], None, ALU.is_equal).then_inc(leaf_hot_ready, 1)

            def op_one_hot(s, a, z):
                dve.wait_ge(op_ids_loaded, s * 16 + 16)
                V.tensor_scalar(op_hot[:, a:z, :], op_ids[:, :].rearrange("p (s n) -> p n s", n=NOPS)[:, a:z, :],
                                iota_part[0:OPV, 0:1], None, ALU.is_equal).then_inc(op_hot_ready, 1)

            st = Steps(dve, dve_setup)
            dve.wait_ge(tree_loaded, ALL_TREE_LOADED)
            dve.wait_ge(consts_done, 1)
            norm(st, ln_struct, comp[:, :, :], 2, compln[:, :, :], gamma, beta, compln_ready)
            V.tensor_scalar(wbLR_g[:, :], wbLR[:, :], gb_cols[:, 0:1], None, ALU.mult).then_inc(beta_ready, 1)
            V.tensor_scalar(beta_rep[:, :], ones[:, 0:OPV], gb_cols[:, 1:2], None, ALU.mult).then_inc(beta_ready, 1)
            st.inc(V.memset(tab[OPV:P, OP_LEAF:OP_UPPER + 1, :], 0.0))
            st.inc(V.memset(om[:, 0:1], -1e38))
            st.inc(V.memset(pst[:, 0:1], 0.0))
            st.inc(V.memset(qst[:, 0:1], 0.0))
            leaf_one_hot(0)
            dve.wait_ge(compT_psum, 1)
            V.tensor_copy(compT[:, :], psA[0:D, 0:2 * P]).then_inc(compT_ready, 1)
            V.tensor_copy(opT[:, :], psA[0:D, 2 * P:2 * P + OPV]).then_inc(compT_ready, 1)
            op_one_hot(0, 0, LEVELS[0])
            op_one_hot(0, LEVELS[0], NOPS)
            dve.wait_ge(tab_psum, 1)
            st.inc(V.tensor_copy(tab[:, LEFT:OP_LEAF, :], psD[:, 0:4 * D].rearrange("p (a d) -> p a d", d=D)))
            st.seq(V.tensor_tensor(tab[0:OPV, OP_LEAF, :], psD[0:OPV, 4 * D:5 * D], b_bin[0:OPV], ALU.add))
            st.seq(V.tensor_tensor(tab[0:OPV, OP_UPPER, :], tab[0:OPV, OP_LEAF, :], psD[0:OPV, 5 * D:6 * D], ALU.add))
            for part in range(3):
                i = V.tensor_copy(tab_parts[:, part, :, :], tab[:, :, :])
                if part < 2:
                    st.seq(i)
                    st.seq(V.tensor_tensor(tab[:, :, :], tab[:, :, :], tab_parts[:, part, :, :], ALU.subtract))
                else:
                    i.then_inc(tab_ready, 1)

            def normalise_level(s, k):
                st = Steps(dve, dve_struct)
                n = STILES * LEVELS[k]
                src = level_bank[k].rearrange("p (a d) -> p a d", d=D)
                dve.wait_ge(level_psum[k], s + 1)
                tick(st)
                if k < 2:
                    norm(st, ln_struct, src, n, node[k][:, :, :], done=node_ready[k])
                else:
                    norm(st, ln_struct, src, n, roots[:, bass.ds(s * STILES, STILES), :], gamma, beta, roots_ready)
                st.restart()

            def struct_round(s, more):
                normalise_level(s, 1)
                normalise_level(s + 1, 0)
                if more:
                    leaf_one_hot(s + 2)
                dve.wait_ge(level_psum[2], s + 1)
                op_one_hot(s + 1, LEVELS[0], NOPS)
                normalise_level(s, 2)
                if more:
                    op_one_hot(s + 2, 0, LEVELS[0])

            normalise_level(0, 0)
            leaf_one_hot(1)
            op_one_hot(1, 0, LEVELS[0])
            with dve.Fori(0, SROUNDS - 2) as s:
                struct_round(s, True)
            struct_round(SROUNDS - 2, False)
            normalise_level(SROUNDS - 1, 1)
            normalise_level(SROUNDS - 1, 2)
            dve.wait_ge(roots_ready, SROUNDS)
            V.memset(roots[0:2, 0, :], 0.0).then_inc(roots_masked, 1)
            dve.wait_ge(loaded, ALL_LOADED)
            st = Steps(dve, dve_struct)
            st.seq(V.tensor_scalar(wu[:, :], wu[:, :], 1.0 / P, None, ALU.mult))
            st.seq(V.tensor_scalar(wdec[:, :], ones[0:D, :], wu[:, 0:1], None, ALU.mult))
            st.restart()

            def softmax_shift(st, soft, src, dst, done):
                mx = soft[0]
                st.seq(V.tensor_reduce(mx[:, :], src, AX.X, ALU.max))
                V.tensor_tensor(dst, src, cast_cols(mx[:, :], P), ALU.subtract).then_inc(done, 1)

            def softmax_scale(st, soft, buf, done):
                zs = soft[1]
                st.seq(V.tensor_reduce(zs[:, :], buf, AX.X, ALU.add))
                st.seq(V.reciprocal(zs[:, :], zs[:, :]))
                V.tensor_tensor(buf, buf, cast_cols(zs[:, :], P), ALU.mult).then_inc(done, 1)

            def pairs(st, dst, l0, l1):
                for i in range(5):
                    n = ROWS[i]
                    st.inc(V.tensor_tensor(dst[:, :, OFFS[i]:OFFS[i] + n], l0[:, :, i:i + 1].to_broadcast([P, H, n]),
                                           l1[:, :, 0:n], ALU.add))
                o = dst[:, :, OFFS[5]:OFFS[8]].rearrange("p h (i j) -> p h i j", j=2)
                st.inc(V.tensor_tensor(o, l0[:, :, 5:8].unsqueeze(3).to_broadcast([P, H, 3, 2]),
                                       l1[:, :, 0:2].unsqueeze(2).to_broadcast([P, H, 3, 2]), ALU.add))
                st.inc(V.tensor_tensor(dst[:, :, OFFS[8]:NCAND], l0[:, :, 8:16],
                                       l1[:, :, 0:1].to_broadcast([P, H, 8]), ALU.add))

            def pre(b):
                n = b + 1
                st = Steps(dve, dve_pre)
                hb = hid[:, bass.ds(b * D, D)]
                norm(st, ln_pre, one(hb), 1, one(hn[:, 0:D]), done=hn_ready)
                yield
                s3 = psB[:, :].rearrange("p (h t) -> p h t", h=H)
                dve.wait_ge(s_psum, n)
                softmax_shift(st, soft_pre, s3, prob[:, :, :], s_shifted)
                yield
                dve.wait_ge(s_exp, n)
                softmax_scale(st, soft_pre, prob[:, :, :], p_ready)
                yield
                dve.wait_ge(att_psum, n)
                st.seq(V.tensor_tensor(att[:, :], psA[:, 0:D], bout, ALU.add))
                st.seq(V.tensor_tensor(hb, hb, att[:, :], ALU.add))
                norm(st, ln_pre, one(hb), 1, one(hn[:, 0:D]), done=x_ready)
                yield
                dve.wait_ge(sim_psum, n)
                tick(st)
                sp3 = psB[:, :].rearrange("p (u k) -> p u k", k=KEYS)
                for u in range(2 * H):
                    st.inc(V.max(top[:, u, 0:8], sp3[:, u, :]))
                st.settle()
                for u in range(2 * H):
                    st.inc(V.max_index(topi[:, u, 0:8], top[:, u, 0:8], sp3[:, u, :]))
                for u in range(2 * H):
                    st.inc(V.match_replace(sim[:, u, :], top[:, u, 0:8], sp3[:, u, :], NEG))
                st.settle()
                yield
                for u in range(2 * H):
                    st.inc(V.max(top[:, u, 8:16], sim[:, u, :]))
                st.settle()
                for u in range(2 * H):
                    i = V.max_index(topi[:, u, 8:16], top[:, u, 8:16], sim[:, u, :])
                    st.inc(i) if u < 2 * H - 1 else i.then_inc(sim_read, 1)
                dve.wait_ge(sim_read, n)
                st.settle()
                yield
                st.seq(V.tensor_copy(topf[:, :, :], topi[:, :, :]))
                st.inc(V.tensor_tensor(topf[:, 0:H, :], topf[:, 0:H, :], head_base[:, :, :], ALU.add))
                st.inc(V.tensor_scalar(topf[:, H:2 * H, :], topf[:, H:2 * H, :], float(KEYS), None, ALU.mult))
                pairs(st, cand[:, :, :], top[:, 0:H, :], top[:, H:2 * H, :])
                st.settle()
                pairs(st, candi[:, :, :], topf[:, 0:H, :], topf[:, H:2 * H, :])
                yield
                for h in range(H):
                    st.inc(V.max(fin[:, h, 0:8], cand[:, h, :]))
                st.settle()
                for h in range(H):
                    st.inc(V.max_index(fini[:, h, 0:8], fin[:, h, 0:8], cand[:, h, :]))
                for h in range(H):
                    st.inc(V.match_replace(cand2[:, h, :], fin[:, h, 0:8], cand[:, h, :], NEG))
                st.settle()
                for h in range(H):
                    st.inc(V.max(fin[:, h, 8:16], cand2[:, h, :]))
                st.settle()
                yield
                V.tensor_tensor(w_next[:, :, :], fin[:, :, :], fin[:, :, 0:1].to_broadcast([P, H, TOPK]),
                                ALU.subtract).then_inc(w_shifted, 1)
                for h in range(H):
                    st.inc(V.max_index(fini[:, h, 8:16], fin[:, h, 8:16], cand2[:, h, :]))
                st.settle()
                st.seq(V.tensor_copy(finp[:, :, :], fini[:, :, :]))
                for h0 in range(0, H, 2):
                    for q in range(2):
                        st.inc(V.tensor_tensor(hot[:, q, :, :], cast_cols(finp[:, h0 + q, :], NCAND),
                                               rows_n(iota_cand[:, :], TOPK), ALU.is_equal))
                    st.settle()
                    for q in range(2):
                        st.inc(V.tensor_tensor(hot[:, q, :, :], hot[:, q, :, :],
                                               rows_n(candi[:, h0 + q, :], TOPK), ALU.mult))
                    st.settle()
                    for q in range(2):
                        st.inc(V.tensor_reduce(rowf[:, h0 + q, :], hot[:, q, :, :], AX.X, ALU.add))
                    st.settle()
                    yield
                dve.wait_ge(w_exp, n)
                st.seq(V.tensor_reduce(wz[:, :], w_next[:, :, :], AX.X, ALU.add))
                st.seq(V.reciprocal(wz[:, :], wz[:, :]))
                V.tensor_tensor(w_next[:, :, :], w_next[:, :, :], cast_cols(wz[:, :], TOPK), ALU.mult).then_inc(found, 1)
                st.inc(V.tensor_copy(row_next[:, :], rowf[:, :, :].rearrange("p h k -> p (h k)")))
                st.restart()

            def commit(half):
                c = half * H * TOPK // 2
                V.tensor_copy(row_now[:, c:c + H * TOPK // 2], row_next[:, c:c + H * TOPK // 2]).then_inc(rows_ready, 1)

            def carry(b):
                V.tensor_copy(w_now[:, :, :], w_next[:, :, :]).then_inc(w_now_ready, 1)
                dve.wait_ge(w_now_ready, b + 1)

            def mix(b, more):
                for h in range(H):
                    if h >= 2:
                        dve.wait_ge(kv_psum, b * H + (h - 1))
                    V.tensor_tensor(diag[:, h % 2, :, :], rows_n(ident[:, :], TOPK),
                                    cast_cols(w_now[:, h, :], P), ALU.mult).then_inc(diag_ready, 1)
                    if more and h == 5:
                        dve.wait_ge(kv_psum, b * H + 4)
                        commit(0)
                if more:
                    dve.wait_ge(kv_psum, b * H + H)
                    commit(1)

            def tail(b):
                n = b + 1
                st = Steps(dve, dve_tail)
                dve.wait_ge(s1_psum, n)
                s3 = psF[:, :].rearrange("p (h t) -> p h t", h=H)
                V.tensor_tensor(prob1[:, :, :], s3, rows_n(causal[:, :], H), ALU.add).then_inc(s1_read, 1)
                dve.wait_ge(s1_read, n)
                softmax_shift(st, soft_tail, prob1[:, :, :], prob1[:, :, :], s1_shifted)
                yield
                dve.wait_ge(s1_exp, n)
                softmax_scale(st, soft_tail, prob1[:, :, :], p1_ready)
                yield
                hb = hid[:, bass.ds(b * D, D)]
                dve.wait_ge(att1_psum, n)
                st.seq(V.tensor_tensor(hb, hb, psE[:, 0:D], ALU.add))
                norm(st, ln_tail, one(hb), 1, one(x3[:, :]))
                norm(st, ln_tail, one(x3[:, :]), 1, one(hk[:, 0:D]), g1, b1, hk_ready)
                yield
                dve.wait_ge(kv_copied, n)
                dve.wait_ge(kvr_ready, n)
                k, v, er = kvr[:, 0, :], kvr[:, 1, :], kvr[:, 2, :]
                o_old, o_new = om[:, 0:P], om[:, 1:P + 1]
                st.inc(V.tensor_tensor_scan(o_new, wdec[:, :], k, -1e38, ALU.add, ALU.max))
                st.inc(V.tensor_scalar(uk[:, :], k, wu[:, 1:2], None, ALU.add))
                st.inc(V.tensor_scalar(er, er, 1.0, None, ALU.add))
                st.settle()
                st.inc(V.tensor_tensor(nom[:, :], o_old, uk[:, :], ALU.max))
                st.inc(V.scalar_tensor_tensor(ex[:, 2, :], o_old, wu[:, 0:1], o_new, ALU.add, ALU.subtract))
                st.inc(V.tensor_tensor(ex[:, 3, :], k, o_new, ALU.subtract))
                st.inc(V.reciprocal(er, er))
                st.settle()
                st.inc(V.tensor_tensor(ex[:, 0, :], o_old, nom[:, :], ALU.subtract))
                V.tensor_tensor(ex[:, 1, :], uk[:, :], nom[:, :], ALU.subtract).then_inc(ex_shifted, 1)
                yield
                dve.wait_ge(ex_done, n)
                st.inc(V.tensor_tensor(ev[:, :], ex[:, 3, :], v, ALU.mult))
                st.inc(V.tensor_tensor_scan(qst[:, 1:P + 1], ex[:, 2, :], ex[:, 3, :], 0.0, ALU.mult, ALU.add))
                st.inc(V.tensor_tensor(num[:, :], ex[:, 1, :], v, ALU.mult))
                st.settle()
                st.inc(V.tensor_tensor_scan(pst[:, 1:P + 1], ex[:, 2, :], ev[:, :], 0.0, ALU.mult, ALU.add))
                st.inc(V.tensor_tensor(den[:, :], ex[:, 0, :], qst[:, 0:P], ALU.mult))
                st.settle()
                st.inc(V.tensor_tensor(ysr[:, :], ex[:, 0, :], pst[:, 0:P], ALU.mult))
                st.inc(V.tensor_tensor(den[:, :], den[:, :], ex[:, 1, :], ALU.add))
                st.settle()
                st.inc(V.tensor_tensor(num[:, :], num[:, :], ysr[:, :], ALU.add))
                st.inc(V.reciprocal(den[:, :], den[:, :]))
                st.settle()
                st.seq(V.tensor_tensor(num[:, :], num[:, :], den[:, :], ALU.mult))
                V.tensor_tensor(ysr[:, :], num[:, :], er, ALU.mult).then_inc(ysr_ready, 1)
                yield
                dve.wait_ge(ro_psum, n)
                st.seq(V.tensor_tensor(x4[:, :], x3[:, :], psE[:, 0:D], ALU.add))
                norm(st, ln_tail, one(x4[:, :]), 1, one(hk[:, 0:D]), g2, b2, h2_ready)
                yield
                dve.wait_ge(sg_ready, n)
                st.seq(V.tensor_scalar(sg[:, :], sg[:, :], 1.0, None, ALU.add))
                st.seq(V.reciprocal(sg[:, :], sg[:, :]))
                yield
                dve.wait_ge(ffn_psum, n)
                st.seq(V.tensor_tensor(sg[:, :], sg[:, :], psE[:, 0:D], ALU.mult))
                st.seq(V.tensor_tensor(x4[:, :], x4[:, :], sg[:, :], ALU.add))
                st.seq(V.tensor_tensor(hb, hb, x4[:, :], ALU.add))
                norm(st, ln_tail, one(hb), 1, one(xm[:, 0:D]), done=xm_ready)
                yield
                dve.wait_ge(gate_psum, n)
                st.seq(V.tensor_tensor(lg[:, :], psE[:, 0:NE], gate_b[:, :], ALU.add))
                st.seq(V.tensor_reduce(g4[:, 0:1], lg[:, :], AX.X, ALU.max))
                V.tensor_scalar(lg[:, :], lg[:, :], g4[:, 0:1], None, ALU.subtract).then_inc(lg_shifted, 1)
                yield
                dve.wait_ge(lg_exp, n)
                st.inc(V.tensor_reduce(g4[:, 0:1], lg[:, :], AX.X, ALU.max))
                st.inc(V.tensor_reduce(g4[:, 1:2], lg[:, :], AX.X, ALU.add))
                st.settle()
                st.inc(V.reciprocal(g4[:, 1:2], g4[:, 1:2]))
                st.seq(V.scalar_tensor_tensor(sc8[:, :], lg[:, :], g4[:, 0:1], rev_e[:, :], ALU.is_ge, ALU.mult))
                st.seq(V.tensor_reduce(g4[:, 2:3], sc8[:, :], AX.X, ALU.max))
                V.tensor_scalar(oh[:, :], sc8[:, :], g4[:, 2:3], None, ALU.is_equal).then_inc(oh_ready, 1)
                dve.wait_ge(oh_ready, n)
                st.inc(V.tensor_tensor(sc8[:, :], oh[:, :], iota_e[:, :], ALU.mult))
                yield
                dve.wait_ge(cum_psum, n)
                st.seq(V.tensor_tensor(cum[:, :], psE[:, 64:64 + NE], count[:, :], ALU.add))
                st.inc(V.tensor_tensor(cum[:, :], cum[:, :], oh[:, :], ALU.mult))
                st.inc(V.tensor_tensor(count[:, :], count[:, :], psE[:, 128:128 + NE], ALU.add))
                st.inc(V.tensor_reduce(g4[:, 3:4], sc8[:, :], AX.X, ALU.add))
                st.settle()
                st.seq(V.tensor_reduce(g4[:, 4:5], cum[:, :], AX.X, ALU.add))
                st.inc(V.tensor_scalar(g4[:, 5:6], g4[:, 4:5], float(CAP), None, ALU.is_le))
                st.inc(V.tensor_scalar(g4[:, 6:7], g4[:, 4:5], float(CAP), -1.0, ALU.min, ALU.add))
                st.inc(V.tensor_scalar(g4[:, 4:5], g4[:, 4:5], float(CAP), float(SLOTS), ALU.is_gt, ALU.mult))
                st.inc(V.tensor_scalar(g4[:, 3:4], g4[:, 3:4], float(CAP), None, ALU.mult))
                st.inc(V.tensor_scalar(g4[:, 0:1], g4[:, 0:1], g4[:, 1:2], None, ALU.mult))
                st.settle()
                st.inc(V.tensor_tensor(g4[:, 6:7], g4[:, 6:7], g4[:, 3:4], ALU.add))
                st.settle()
                V.tensor_tensor(slot_s[:, :], g4[:, 6:7], g4[:, 4:5], ALU.add).then_inc(slot_ready, 1)
                st.inc(V.tensor_copy(slot_g[:, bass.ds(b, 1)], g4[:, 6:7]))
                st.inc(V.tensor_tensor(keep[:, bass.ds(b, 1)], g4[:, 0:1], g4[:, 5:6], ALU.mult))
                st.restart()

            dve.wait_ge(embedded_first, 16)
            weave(pre(0))
            commit(0)
            commit(1)
            dve.wait_ge(rows_ready, 2)
            dve.wait_ge(embedded, 16 * (NB - 1))
            carry(0)
            weave(pre(1))
            mix(0, True)
            with dve.Fori(1, NB - 1) as b:
                before = tail(b - 1)
                next(before)
                carry(b)
                weave(pre(b + 1), before)
                mix(b, True)
                dve.wait_ge(scattered, b * 16)
                st = Steps(dve, dve_tail)
                tick(st, 1)
                st.restart()
            before = tail(NB - 2)
            next(before)
            carry(NB - 1)
            weave(before)
            mix(NB - 1, False)
            dve.wait_ge(scattered, 16 * (NB - 1))
            weave(tail(NB - 1))

            def copy_xT(e):
                dve.wait_ge(exT_psum, e + 1)
                V.tensor_copy(ex_T[:, 0:512], psA[0:D, :]).then_inc(exT_ready, 1)
                V.tensor_copy(ex_T[:, 512:CAP], psD[0:D, 0:CAP - 512]).then_inc(exT_ready, 1)

            def add_bias(e, q):
                dve.wait_ge(w2_loaded[q], (e - q) * 16 + 32)
                dve.wait_ge(ey_psum, e + 1)
                V.tensor_tensor(ex_y[:, bass.ds(e * ETILES, ETILES), :],
                                (psE, psH)[q][:, 0:ETILES * D].rearrange("p (j d) -> p j d", d=D),
                                rows_n(eb2[:, q, :], ETILES), ALU.add).then_inc(ey_ready, 1)

            copy_xT(0)
            with dve.Fori(0, NE // 2 - 1) as i:
                for q in range(2):
                    copy_xT(i * 2 + q + 1)
                    add_bias(i * 2 + q, q)
            copy_xT(NE - 1)
            add_bias(NE - 2, 0)
            add_bias(NE - 1, 1)

            st = Steps(dve, dve_last)
            for g in range(YGROUPS):
                dve.wait_ge(y_gathered[g], 16 * YB)
                c = slice(g * YB * D, (g + 1) * YB * D)
                y, bad, fill = y_tok[:, c], y_bad[:, 0:YB * D], y_fill[:, 0:YB * D]
                y3 = y.rearrange("p (b d) -> p b d", d=D)
                st.seq(V.tensor_tensor(y3, y3, cast_cols(keep[:, g * YB:(g + 1) * YB], D), ALU.mult))
                for op, x, value in ((ALU.not_equal, None, 0.0), (ALU.is_gt, HUGE, 1e4), (ALU.is_lt, -HUGE, -1e4)):
                    st.inc(V.memset(fill, value))
                    if x is None:
                        st.inc(V.tensor_tensor(bad.bitcast(I32), y, y, op))
                    else:
                        st.inc(V.tensor_scalar(bad.bitcast(I32), y, x, None, op))
                    st.settle()
                    st.seq(V.copy_predicated(y, bad.bitcast(I32), fill))
                V.tensor_tensor(hid[:, c], hid[:, c], y, ALU.add).then_inc(out_ready, 1)

        @block.scalar
        def _(act):
            A = nc.scalar

            def copy(dst, src, done, scale=1.0):
                A.activation(dst, src, ACT.Copy, scale=scale).then_inc(done, 1)

            def copy_nodeT(s, k):
                act.wait_ge(nodeT_psum[k], s + 1)
                copy(nodeT[k][:, :, :], nodeT_bank[k].rearrange("p (a t) -> p a t", t=P), nodeT_ready[k])

            act.wait_ge(wT_psum, 1)
            for a, z, bank in ((0, 16, psF), (16, 20, psH)):
                A.activation(wT[:, a:z, :], bank[:, 0:(z - a) * D].rearrange("p (a d) -> p a d", d=D), ACT.Copy).then_inc(wT_ready, 1)
            copy_nodeT(0, 0)
            act.wait_ge(fold_psum, 1)
            for g in range(2):
                for k, w in enumerate((wqk, wvo)):
                    A.activation(w[0:D, :].rearrange("c (j g d) -> c g j d", g=2, d=D)[:, g],
                                 psF[0:D, 512 * g + 256 * k:512 * g + 256 * k + 256].rearrange("c (j d) -> c j d", d=D),
                                 ACT.Copy).then_inc(fold_ready, 1)
            for g in range(4):
                A.activation(wpk[:, :].rearrange("c (j g k) -> c g j k", g=4, k=KEYS)[:, g],
                             PK_BANKS[g][0:D, 0:4 * KEYS].rearrange("c (j k) -> c j k", k=KEYS), ACT.Copy).then_inc(fold_ready, 1)
            with act.Fori(0, SROUNDS - 1) as s:
                copy_nodeT(s, 1)
                copy_nodeT(s + 1, 0)
            copy_nodeT(SROUNDS - 1, 1)

            def pre(b):
                n = b + 1
                act.wait_ge(hnT_psum, n)
                copy(hnT[:, :], psA[:, 0:P], hnT_ready)
                act.wait_ge(qT_psum, n)
                copy(qT[:, :], psB[0:D, :], qT_ready)
                act.wait_ge(val_psum, n)
                copy(val[:, :], psD[:, :], val_ready)
                yield
                act.wait_ge(s_shifted, n)
                A.activation(prob[:, :, :], prob[:, :, :], ACT.Exp, scale=float(1.0 / np.sqrt(D / H))).then_inc(s_exp, 1)
                yield
                act.wait_ge(pT_psum, n)
                copy(probT[:, :, :], psB[:, :].rearrange("p (h t) -> p h t", h=H), pT_ready)
                yield
                act.wait_ge(xT_psum, n)
                copy(xT[:, :], psA[:, 0:P], xT_ready)
                yield
                yield
                yield
                yield
                yield
                act.wait_ge(w_shifted, n)
                A.activation(w_next[:, :, :], w_next[:, :, :], ACT.Exp).then_inc(w_exp, 1)

            def carry(b):
                act.wait_ge(q1T_psum, b + 1)
                copy(q1T[:, :], psF[0:D, :], q1T_ready, scale=D ** -0.5)

            def mix(b):
                for h in range(H):
                    act.wait_ge(kv_psum, b * H + (h + 1))
                    copy(kvT[:, h, :], (psH, psE)[h % 2][:, 0:P], kv_ready)

            def tail(b):
                n = b + 1
                act.wait_ge(vo_psum, n)
                copy(vo[:, :], psH[:, :], vo_ready)
                act.wait_ge(s1_shifted, n)
                A.activation(prob1[:, :, :], prob1[:, :, :], ACT.Exp).then_inc(s1_exp, 1)
                yield
                act.wait_ge(p1T_psum, n)
                copy(prob1T[:, :, :], psF[:, :].rearrange("p (h t) -> p h t", h=H), p1T_ready)
                yield
                act.wait_ge(hkT_psum, n)
                copy(hkT[:, :], psE[:, 0:P], hkT_ready)
                act.wait_ge(kvr_psum, n)
                A.activation(kvr[:, 0:2, :], psE[0:D, 0:2 * P].rearrange("p (a t) -> p a t", t=P), ACT.Copy).then_inc(kv_copied, 1)
                A.activation(kvr[:, 2, :], psE[0:D, 2 * P:3 * P], ACT.Exp, scale=-1.0).then_inc(kvr_ready, 1)
                yield
                act.wait_ge(ex_shifted, n)
                A.activation(ex[:, :, :], ex[:, :, :], ACT.Exp).then_inc(ex_done, 1)
                yield
                yield
                act.wait_ge(h2T_psum, n)
                copy(h2T[:, :], psE[0:D, 0:P], h2T_ready)
                act.wait_ge(kk_psum, n)
                A.activation(kk[:, :, :], psE[:, 0:HIDC * P].rearrange("p (c t) -> p c t", t=P), ACT.Relu).then_inc(relu_done, 1)
                A.activation(sg[:, :], psE[:, HIDC * P:HIDC * P + D], ACT.Exp, scale=-1.0).then_inc(sg_ready, 1)
                act.wait_ge(relu_done, n)
                A.activation(kk[:, :, :], kk[:, :, :], ACT.Square).then_inc(kk_ready, 1)
                yield
                yield
                act.wait_ge(xmT_psum, n)
                copy(xmT[:, :], psE[0:D, 0:P], xmT_ready)
                yield
                act.wait_ge(lg_shifted, n)
                A.activation(lg[:, :], lg[:, :], ACT.Exp).then_inc(lg_exp, 1)
                yield
                yield

            weave(pre(0))
            carry(0)
            weave(pre(1))
            mix(0)
            with act.Fori(1, NB - 1) as b:
                before = tail(b - 1)
                next(before)
                carry(b)
                weave(pre(b + 1), before)
                mix(b)
            before = tail(NB - 2)
            next(before)
            carry(NB - 1)
            weave(before)
            mix(NB - 1)
            weave(tail(NB - 1))

            with act.Fori(0, NE // 2) as i:
                for q in range(2):
                    e = i * 2 + q
                    act.wait_ge(w1_loaded[q], i * 32 + 32)
                    for c in range(FC):
                        act.wait_ge(eh_psum, e * FC + (c + 1))
                        A.activation(ex_h[:, c, :], (psB, psF)[c][:, 0:CAP], ACT.Relu, bias=eb1[:, q, c:c + 1]).then_inc(eh_ready, 1)

        @block.tensor
        def _(pe):
            T = nc.tensor
            SPLIT = ((0, 512), (512, CAP))

            pe.wait_ge(compln_ready, 1)
            for c in range(2):
                T.transpose(psA[0:D, c * P:(c + 1) * P], compln[:, c, :], ident[:, :])
            T.transpose(psA[0:D, 2 * P:2 * P + OPV], opsb[:, :], ident[0:OPV, 0:OPV]).then_inc(compT_psum, 1)
            pe.wait_ge(compT_ready, 2)
            for c in range(2):
                T.matmul(psD[:, (LEFT + c) * D:(LEFT + c + 1) * D], compT[:, c * P:(c + 1) * P], wbL[:, :], start=True, stop=True)
                T.matmul(psD[:, (RIGHT + c) * D:(RIGHT + c + 1) * D], compT[:, c * P:(c + 1) * P], wbR[:, :], start=True, stop=True)
            T.matmul(psD[0:OPV, 4 * D:5 * D], opT[:, :], wb0[:, :], start=True, stop=True)
            pe.wait_ge(beta_ready, 2)
            T.matmul(psD[0:OPV, 5 * D:6 * D], beta_rep[:, :], wbLR[:, :], start=True, stop=True).then_inc(tab_psum, 1)
            pe.wait_ge(tab_ready, 1)

            def add_rows(o, hot, table, first, last):
                for part in range(3):
                    mm = T.matmul(o, hot, tab_parts[0:hot.shape[0], part, table, :],
                                  start=(first and part == 0), stop=(last and part == 2))
                return mm

            def leaf_level(s):
                pe.wait_ge(leaf_hot_ready, s * 2 + 2)
                pe.wait_ge(op_hot_ready, s * 2 + 1)
                for j in range(STILES):
                    tile = slice(j * P, (j + 1) * P)
                    for m in range(LEVELS[0]):
                        o = level_bank[0][:, (j * LEVELS[0] + m) * D:(j * LEVELS[0] + m + 1) * D]
                        for c in range(2):
                            add_rows(o, leaf_hot[:, c, 2 * m, tile], LEFT + c, c == 0, False)
                            add_rows(o, leaf_hot[:, c, 2 * m + 1, tile], RIGHT + c, False, False)
                        mm = add_rows(o, op_hot[:, m, tile], OP_LEAF, False, True)
                mm.then_inc(level_psum[0], 1)

            def upper_level(s, k):
                pe.wait_ge(node_ready[k - 1], s + 1)
                for m in range(STILES * LEVELS[k]):
                    mm = T.transpose(nodeT_bank[k - 1][:, m * P:(m + 1) * P],
                                     node[k - 1][:, 2 * m:2 * m + 2, :].rearrange("p a d -> p (a d)"), ident[:, :])
                mm.then_inc(nodeT_psum[k - 1], 1)
                pe.wait_ge(nodeT_ready[k - 1], s + 1)
                if k == 1:
                    pe.wait_ge(op_hot_ready, s * 2 + 2)
                for j in range(STILES):
                    for m in range(LEVELS[k]):
                        i = j * LEVELS[k] + m
                        o = level_bank[k][:, i * D:(i + 1) * D]
                        T.matmul(o, nodeT[k - 1][:, i, :], wbLR_g[:, :], start=True, stop=False)
                        mm = add_rows(o, op_hot[:, sum(LEVELS[:k]) + m, j * P:(j + 1) * P], OP_UPPER, False, True)
                mm.then_inc(level_psum[k], 1)

            leaf_level(0)
            pe.wait_ge(loaded, ALL_LOADED)
            pe.wait_ge(consts_done, 1)
            for k in range(20):
                if k < 16:
                    src = heads_in[:, k // 4, (k % 4) * P:(k % 4 + 1) * P]
                else:
                    src = pk_in[:, (k - 16) // 2, (k % 2) * P:(k % 2 + 1) * P]
                mm = T.transpose(psF[:, k * D:(k + 1) * D] if k < 16 else psH[:, (k - 16) * D:(k - 15) * D], src, ident[0:D, 0:D])
            mm.then_inc(wT_psum, 1)
            upper_level(0, 1)
            pe.wait_ge(wT_ready, 2)
            for h in range(H):
                r, j = slice(D * (h % 2), D * (h % 2) + D), h // 2
                o = psF[0:D, 512 * (h % 2):512 * (h % 2) + 512]
                T.matmul(o[:, j * D:(j + 1) * D], wT[r, j, :], wT[r, 4 + j, :], start=True, stop=True)
                T.matmul(o[:, (4 + j) * D:(5 + j) * D], wT[r, 8 + j, :], wout[r, j, :], start=True, stop=True)
            for u in range(2 * H):
                g, j = u % 4, u // 4
                r = slice(DKEY * g, DKEY * g + DKEY)
                mm = T.matmul(PK_BANKS[g][0:D, j * KEYS:(j + 1) * KEYS], wT[r, 12 + j, :], wT[r, 16 + j, :], start=True, stop=True)
            mm.then_inc(fold_psum, 1)
            pe.wait_ge(fold_ready, 8)
            with pe.Fori(0, SROUNDS - 1) as s:
                leaf_level(s + 1)
                upper_level(s, 2)
                upper_level(s + 1, 1)
            upper_level(SROUNDS - 1, 2)

            def pre(b):
                n = b + 1
                pe.wait_ge(hn_ready, n)
                T.transpose(psA[:, 0:P], hn[:, :], ident[:, :]).then_inc(hnT_psum, 1)
                pe.wait_ge(hnT_ready, n)
                if not (isinstance(b, int) and b == 0):
                    pe.wait_ge(sim_read, b)
                for h in range(H):
                    mm = T.matmul(psB[0:D, h * P:(h + 1) * P], wqk[:, h * D:(h + 1) * D], hnT[:, :], start=True, stop=True)
                mm.then_inc(qT_psum, 1)
                T.matmul(psD[:, :], hnT[0:D, :], wvo[:, :], start=True, stop=True).then_inc(val_psum, 1)
                pe.wait_ge(qT_ready, n)
                for h in range(H):
                    mm = T.matmul(psB[:, h * P:(h + 1) * P], qT[:, h * P:(h + 1) * P], hnT[0:D, :], start=True, stop=True)
                mm.then_inc(s_psum, 1)
                yield
                yield
                pe.wait_ge(p_ready, n)
                for h in range(H):
                    mm = T.transpose(psB[:, h * P:(h + 1) * P], prob[:, h, :], ident[:, :])
                mm.then_inc(pT_psum, 1)
                pe.wait_ge(pT_ready, n)
                pe.wait_ge(val_ready, n)
                for h in range(H):
                    mm = T.matmul(psA[:, 0:D], probT[:, h, :], val[:, h * D:(h + 1) * D], start=(h == 0), stop=(h == H - 1))
                mm.then_inc(att_psum, 1)
                yield
                pe.wait_ge(x_ready, n)
                T.transpose(psA[:, 0:P], hn[:, :], ident[:, :]).then_inc(xT_psum, 1)
                pe.wait_ge(xT_ready, n)
                for p in range(2):
                    mm = T.matmul(psB[:, p * 512:(p + 1) * 512], xT[0:D, :], wpk[:, p * 512:(p + 1) * 512], start=True, stop=True)
                mm.then_inc(sim_psum, 1)
                yield

            def carry(b):
                pe.wait_ge(xT_ready, b + 1)
                if not (isinstance(b, int) and b == 0):
                    pe.wait_ge(s1_read, b)
                for h in range(H):
                    mm = T.matmul(psF[0:D, h * P:(h + 1) * P], wq1[:, h * D:(h + 1) * D], xT[:, :], start=True, stop=True)
                mm.then_inc(q1T_psum, 1)
                pe.wait_ge(q1T_ready, b + 1)

            def mix(b):
                for h in range(H):
                    pe.wait_ge(diag_ready, b * H + (h + 1))
                    pe.wait_ge(gathered[h], b * 256 + 256)
                    if h >= 2:
                        pe.wait_ge(kv_ready, b * H + (h - 1))
                    for k in range(TOPK):
                        mm = T.matmul((psH, psE)[h % 2][:, 0:P], mem[:, h, k, :], diag[:, h % 2, k, :],
                                      start=(k == 0), stop=(k == TOPK - 1))
                    mm.then_inc(kv_psum, 1)

            def tail(b):
                n = b + 1
                pe.wait_ge(kv_ready, b * H + H)
                for h in range(H):
                    mm = T.matmul(psF[:, h * P:(h + 1) * P], q1T[:, h * P:(h + 1) * P], kvT[0:D, h, :], start=True, stop=True)
                mm.then_inc(s1_psum, 1)
                for h in range(H):
                    mm = T.matmul(psH[:, h * D:(h + 1) * D], kvT[D:P, h, :], wo1[D:P, h, :], start=True, stop=True)
                mm.then_inc(vo_psum, 1)
                yield
                pe.wait_ge(p1_ready, n)
                for h in range(H):
                    mm = T.transpose(psF[:, h * P:(h + 1) * P], prob1[:, h, :], ident[:, :])
                mm.then_inc(p1T_psum, 1)
                pe.wait_ge(p1T_ready, n)
                pe.wait_ge(vo_ready, n)
                for h in range(H):
                    mm = T.matmul(psE[:, 0:D], prob1T[:, h, :], vo[:, h * D:(h + 1) * D], start=(h == 0), stop=(h == H - 1))
                mm.then_inc(att1_psum, 1)
                yield
                pe.wait_ge(hk_ready, n)
                T.transpose(psE[:, 0:P], hk[:, :], ident[:, :]).then_inc(hkT_psum, 1)
                pe.wait_ge(hkT_ready, n)
                for k, w in enumerate((rk, rv, rr)):
                    mm = T.matmul(psE[0:D, k * P:(k + 1) * P], w, hkT[:, :], start=True, stop=True)
                mm.then_inc(kvr_psum, 1)
                yield
                yield
                pe.wait_ge(ysr_ready, n)
                T.matmul(psE[:, 0:D], ysr[:, :], ro[0:D], start=True, stop=True).then_inc(ro_psum, 1)
                yield
                pe.wait_ge(h2_ready, n)
                T.transpose(psE[:, 0:P], hk[:, :], ident[:, :]).then_inc(h2T_psum, 1)
                pe.wait_ge(h2T_ready, n)
                for c in range(HIDC):
                    T.matmul(psE[:, c * P:(c + 1) * P], wkf[:, c * P:(c + 1) * P], h2T[:, :], start=True, stop=True)
                T.matmul(psE[:, HIDC * P:HIDC * P + D], h2T[:, :], rrf[0:D], start=True, stop=True).then_inc(kk_psum, 1)
                yield
                pe.wait_ge(kk_ready, n)
                pe.wait_ge(sg_ready, n)
                for c in range(HIDC):
                    mm = T.matmul(psE[:, 0:D], kk[:, c, :], wvf[:, c, :], start=(c == 0), stop=(c == HIDC - 1))
                mm.then_inc(ffn_psum, 1)
                yield
                pe.wait_ge(xm_ready, n)
                T.transpose(psE[:, 0:P], xm[:, :], ident[:, :]).then_inc(xmT_psum, 1)
                pe.wait_ge(xmT_ready, n)
                T.matmul(psE[:, 0:NE], xmT[:, :], gate_w[:, :], start=True, stop=True).then_inc(gate_psum, 1)
                yield
                yield
                pe.wait_ge(oh_ready, n)
                T.matmul(psE[:, 64:64 + NE], upto[:, :], oh[:, :], start=True, stop=True)
                T.matmul(psE[:, 128:128 + NE], ones[:, :], oh[:, :], start=True, stop=True).then_inc(cum_psum, 1)

            pe.wait_ge(roots_ready, SROUNDS)
            weave(pre(0))
            carry(0)
            weave(pre(1))
            mix(0)
            with pe.Fori(1, NB - 1) as b:
                before = tail(b - 1)
                next(before)
                carry(b)
                weave(pre(b + 1), before)
                mix(b)
            before = tail(NB - 2)
            next(before)
            carry(NB - 1)
            weave(before)
            mix(NB - 1)
            weave(tail(NB - 1))

            def transpose_x(e, q):
                pe.wait_ge(x_loaded[q], (e - q) * 8 + 16)
                for j in range(ETILES):
                    o = psA[:, j * P:(j + 1) * P] if j < 4 else psD[:, 0:P]
                    mm = T.transpose(o, ex_in[:, q, j, :], ident[:, :])
                mm.then_inc(exT_psum, 1)

            def first_map(e, q):
                pe.wait_ge(w1_loaded[q], (e - q) * 16 + 32)
                pe.wait_ge(exT_ready, e * 2 + 2)
                for c in range(FC):
                    for a, z in SPLIT:
                        mm = T.matmul((psB, psF)[c][:, a:z], w1[:, q, c * P:(c + 1) * P], ex_T[:, a:z], start=True, stop=True)
                    mm.then_inc(eh_psum, 1)

            def second_map(e, q):
                pe.wait_ge(w2_loaded[q], (e - q) * 16 + 32)
                pe.wait_ge(eh_ready, e * FC + FC)
                for j in range(ETILES):
                    for c in range(FC):
                        mm = T.matmul((psE, psH)[q][:, j * D:(j + 1) * D], ex_h[:, c, j * P:(j + 1) * P], w2[:, q, c, :],
                                      start=(c == 0), stop=(c == FC - 1))
                mm.then_inc(ey_psum, 1)

            transpose_x(0, 0)
            with pe.Fori(0, NE // 2 - 1) as i:
                for q in range(2):
                    e = i * 2 + q
                    first_map(e, q)
                    transpose_x(e + 1, 1 - q)
                    second_map(e, q)
            first_map(NE - 2, 0)
            transpose_x(NE - 1, 1)
            second_map(NE - 2, 0)
            first_map(NE - 1, 1)
            second_map(NE - 1, 1)


_KV = ("L0_ffn_keys_table", "L0_ffn_values_table")


def kernel(**inputs):
    import concourse.bacc as _bacc
    from concourse.bass_utils import run_bass_kernel_spmd as _run

    nc = _bacc.Bacc("TRN2", target_bir_lowering=False, num_devices=1)
    given = {k: np.ascontiguousarray(v) for k, v in inputs.items() if k not in _KV}
    given["kv_table"] = np.concatenate([np.asarray(inputs[k]) for k in _KV], axis=1)
    arrays, aps = {}, {}
    for name, a in given.items():
        arrays[f"in_{name}"] = a
        aps[name] = nc.dram_tensor(f"in_{name}", a.shape, mybir.dt.from_np(a.dtype), kind="ExternalInput").ap()
    out = nc.dram_tensor("out_0", (NB, P, D), F32, kind="ExternalOutput").ap()
    tower(nc, aps, out)
    r = _run(nc, [arrays], core_ids=[0])
    return r.results[0]["out_0"]
```

```python
import numpy as np
import concourse.bass as bass
from concourse import mybir
from contextlib import ExitStack

F32 = mybir.dt.float32
BF16 = mybir.dt.bfloat16
I32 = mybir.dt.int32
U32 = mybir.dt.uint32
ALU = mybir.AluOpType
ACT = mybir.ActivationFunctionType
AX = mybir.AxisListType

P = 128
D = 64
NB = 32
H = 8
EPS = 1e-5
SCALE0 = float(1.0 / np.sqrt(D / H))
NSTRUCT, NLEAF, NOPS, VOCAB, OPV = 2048, 8, 7, 256, 64
STILES = 4
SROUNDS = NSTRUCT // P // STILES
LEVELS = (4, 2, 1)
KEYS, TOPK, DKEY = 64, 16, 32
GH = H - 1
CHUNKS = 8
CKEYS = KEYS // CHUNKS
CTILES = KEYS * CKEYS // P
TABLE_LOADS = 8
NUM_KV = KEYS * KEYS
ROWS = [TOPK // (i + 1) for i in range(TOPK)]
OFFS = [sum(ROWS[:i]) for i in range(TOPK)]
NCAND = sum(ROWS)
NE, F = 8, 256
FC = F // P
CAP = -(-5 * NB * P // (4 * NE))
ETILES = CAP // P
YGROUPS = 8
YB = NB // YGROUPS
SLOTS = NE * CAP
HIDC = 256 // P

NEG = -3.0e38
HUGE = 3.4028234663852886e38
MAGIC = float(0x5F3759DF)
PRE_STEPS_PER_HALF = 5
HALF_FOUND = 4 + PRE_STEPS_PER_HALF
FIND_TURN = 0
DENSE_TURN = 0
MIX_TURN = 2

class Steps:

    def __init__(self, eng, sem):
        self.eng, self.sem, self.n = eng, sem, 0

    def inc(self, ins):
        self.n += 1
        ins.then_inc(self.sem, 1)

    def settle(self):
        self.eng.wait_ge(self.sem, self.n)

    def seq(self, ins):
        self.inc(ins)
        self.settle()

    def restart(self):
        self.settle()
        self.eng.sem_clear(self.sem)


def weave(*stages):
    stages = list(stages)
    while stages:
        for stage in list(stages):
            try:
                next(stage)
            except StopIteration:
                stages.remove(stage)


def later(turns, stage):
    for _ in range(turns):
        yield
    yield from stage


def tower(nc, t, out):
    ctx = ExitStack()
    with ctx:
        def sb(name, shape, dt=F32):
            return ctx.enter_context(nc.sbuf_tensor(name, shape, dt))

        def sem(name):
            return ctx.enter_context(nc.semaphore(name))

        def cast_cols(ap, n):
            return ap.unsqueeze(2).to_broadcast([ap.shape[0], ap.shape[1], n])

        def rows_n(ap, n):
            return ap.unsqueeze(1).to_broadcast([ap.shape[0], n, ap.shape[1]])

        root_table = nc.dram_tensor("root_table", [NSTRUCT, D], F32, kind="Internal").ap()
        slots_x = nc.dram_tensor("slots_x", [SLOTS, D], F32, kind="Internal").ap()
        slots_y = nc.dram_tensor("slots_y", [SLOTS, D], F32, kind="Internal").ap()

        mem = sb("mem", [P, H, TOPK, P])
        memf = mem[:, :, :, :].rearrange("p h k d -> p (h k d)")
        diag = sb("diag", [P, 2, TOPK, P])
        diagf = diag[:, :, :, :].rearrange("p q k t -> p (q k t)")
        lent, lent_diag = [0], [0]

        def lend(parts, *shape, dt=F32, space=memf, lent=lent):
            n = int(np.prod(shape)) // (2 if dt is BF16 else 1)
            ap = space[0:parts, lent[0]:lent[0] + n]
            lent[0] += n
            if dt is not F32:
                ap = ap.bitcast(dt)
            names = "abc"[:len(shape)]
            return ap if len(shape) == 1 else ap.rearrange(
                f"p ({' '.join(names)}) -> p {' '.join(names)}", **dict(zip(names, shape)))

        comp = sb("comp", [P, 2, D])
        opsb = sb("opsb", [OPV, D])
        wb0, wbL, wbR = sb("wb0", [D, D]), sb("wbL", [D, D]), sb("wbR", [D, D])
        wbLR = sb("wbLR", [2 * D, D])
        gb_cols = sb("gb_cols", [2 * D, 2])
        wbLR_g = sb("wbLR_g", [2 * D, D])
        vec_names = ["L0_tok_b_bin", "L0_tok_gamma", "L0_tok_beta", "L0_attn_bout",
                     "L1_attn_g1", "L1_attn_b1", "L1_attn_g2", "L1_attn_b2"]
        vecs = sb("vecs", [P, len(vec_names), D])
        b_bin, gamma, beta, bout, g1, b1, g2, b2 = [vecs[:, k, :] for k in range(8)]
        gate_b = sb("gate_b", [P, NE])
        in_diag = dict(space=diagf, lent=lent_diag)
        heads_in = lend(D, 4, H * D, **in_diag)
        wout = lend(2 * D, H // 2, D, **in_diag)
        pk_in = lend(KEYS, 2, H * DKEY, **in_diag)
        wT = lend(P, 20, D, **in_diag)
        wqk = sb("wqk", [P, H * D])
        wvo = sb("wvo", [D, H * D])
        wpk = sb("wpk", [D, 2 * H * KEYS])
        wq1 = sb("wq1", [P, H * D])
        wo1 = sb("wo1", [P, H, D])
        sq_names = ["L1_attn_Wk", "L1_attn_Wv", "L1_attn_Wr", "L1_attn_Wo", "L1_attn_Wr_ffn"]
        squares = sb("squares", [P, len(sq_names), D])
        rk, rv, rr, ro, rrf = [squares[:, k, :] for k in range(5)]
        wkf = sb("wkf", [D, HIDC * P])
        wvf = sb("wvf", [P, HIDC, D])
        gate_w = sb("gate_w", [D, NE])
        wu = sb("wu", [D, 2])

        ident = sb("ident", [P, P])
        ones = sb("ones", [P, P])
        upto = sb("upto", [P, P])
        causal = sb("causal", [P, P])
        iota_part = sb("iota_part", [P, 2])
        iota_cand = sb("iota_cand", [P, NCAND])
        iota_e = sb("iota_e", [P, NE])
        rev_e = sb("rev_e", [P, NE])
        head_base = sb("head_base", [P, H, TOPK])

        compln = sb("compln", [P, 2, D])
        compT = sb("compT", [D, 2 * P])
        opT = sb("opT", [D, OPV])
        tab = sb("tab", [P, 6, D])
        LEFT, RIGHT, OP_LEAF, OP_UPPER = 0, 2, 4, 5
        tab_parts = sb("tab_parts", [P, 3, 6, D], BF16)
        beta_rep = sb("beta_rep", [2 * D, OPV])
        SP = STILES * P
        leaf_ids = lend(P, SP * NLEAF, dt=I32)
        op_ids = lend(OPV, SP * NOPS, dt=I32)
        leaf_hot = lend(P, 2, NLEAF, SP, dt=BF16)
        op_hot = lend(OPV, NOPS, SP, dt=BF16)
        roots = lend(P, NSTRUCT // P, D)
        node = [lend(P, STILES * LEVELS[k], D) for k in range(2)]
        spread, spreadT = sb("spread", [P, 2, CKEYS, KEYS]), sb("spreadT", [P, CTILES, P])
        nodeT = [spread[:, :, :, :].rearrange("p q j i -> p (q j i)").rearrange("p (n t) -> p n t", t=P), spreadT]

        def norm_scratch(name, n):
            return (sb(f"{name}_stats", [P, n, 6]), sb(f"{name}_mean_var", [P, n, 2]), sb(f"{name}_v", [P, n]),
                    sb(f"{name}_bits", [P, n], I32), sb(f"{name}_y", [P, n], I32), sb(f"{name}_a", [P, n]))

        ln_struct, ln_pre, ln_tail = norm_scratch("struct", STILES * LEVELS[0]), norm_scratch("pre", 1), norm_scratch("tail", 1)

        x_ids = sb("x_ids", [P, NB], I32)
        hid = sb("hid", [P, NB * D])
        hn = sb("hn", [P, 2 * D])
        hnT = sb("hnT", [P, P])
        qT = sb("qT", [D, H * P])
        val = sb("val", [P, H * D])
        prob = sb("prob", [P, H, P])
        probT = sb("probT", [P, H, P])
        soft_pre = sb("mx_pre", [P, H]), sb("zs_pre", [P, H])
        soft_tail = sb("mx_tail", [P, H]), sb("zs_tail", [P, H])
        att = sb("att", [P, D])
        xT = sb("xT", [P, P])
        sim = sb("sim", [P, 2 * H, KEYS])
        top = sb("top", [P, 2 * H, TOPK])
        topi = sb("topi", [P, 2 * H, TOPK], U32)
        topf = sb("topf", [P, 2 * H, TOPK])
        cand = sb("cand", [P, H, NCAND])
        cand2 = sb("cand2", [P, H, NCAND])
        candi = sb("candi", [P, H, NCAND])
        fin = sb("fin", [P, H, TOPK])
        fini = sb("fini", [P, H, TOPK], U32)
        finp = sb("finp", [P, H, TOPK])
        hot = sb("hot", [P, 2, TOPK, NCAND])
        rowf = sb("rowf", [P, H, TOPK])
        row_next = sb("row_next", [P, H // 2 * TOPK], I32)
        w_next = sb("w_next", [P, H, TOPK])
        wz = sb("wz", [P, H])
        DEPTH, RANK, EXP0, EXP1 = range(4)
        by_key, by_key_now = sb("by_key", [P, 4, KEYS]), sb("by_key_now", [P, 4, KEYS])
        offs = sb("offs", [P, TOPK])
        iota_key = sb("iota_key", [P, 2, KEYS])
        passed, depth_rank = sb("passed", [P, TOPK + 1]), sb("depth_rank", [P, 2, TOPK])
        table_a, table_b = memf[:, 0:TOPK * P].rearrange("p (c d) -> p c d", d=P), sb("table_b", [P, TOPK, P])
        zeros = table_b[:, :, :].rearrange("p c d -> p (c d)")[:, 0:SLOTS * D // P // 4]
        row_now = sb("row_now", [P, H * TOPK], I32)
        w_now = sb("w_now", [P, H, TOPK])
        q1T = sb("q1T", [D, H * P])
        kvT = sb("kvT", [P, H, P])
        prob1 = sb("prob1", [P, H, P])
        prob1T = sb("prob1T", [P, H, P])
        vo = sb("vo", [P, H * D])
        x3 = sb("x3", [P, D])
        hk = sb("hk", [P, 2 * D])
        hkT = sb("hkT", [P, P])
        kvr = sb("kvr", [D, 3, P])
        om = sb("om", [D, P + 1])
        uk = sb("uk", [D, P])
        nom = sb("nom", [D, P])
        wdec = sb("wdec", [D, P])
        ex = sb("ex", [D, 4, P])
        ev = sb("ev", [D, P])
        pst = sb("pst", [D, P + 1])
        qst = sb("qst", [D, P + 1])
        num = sb("num", [D, P])
        den = sb("den", [D, P])
        ysr = sb("ysr", [D, P])
        x4 = sb("x4", [P, D])
        h2T = sb("h2T", [D, P])
        kk = sb("kk", [P, HIDC, P])
        sg = sb("sg", [P, D])
        xm = sb("xm", [P, 2 * D])
        xmT = sb("xmT", [D, P])
        lg = sb("lg", [P, NE])
        oh = sb("oh", [P, NE])
        sc8 = sb("sc8", [P, NE])
        cum = sb("cum", [P, NE])
        tick_pool, tick_dve = sb("tick_pool", [P, 1]), sb("tick_dve", [P, 2])
        count = sb("count", [P, NE])
        g4 = sb("g4", [P, 8])
        slot_s = sb("slot_s", [P, 1], I32)
        slot_g = sb("slot_g", [P, NB], I32)
        keep = sb("keep", [P, NB])
        lent[0] = 3 * NB * D
        w1 = lend(D, 2, F)
        w2 = lend(P, 2, FC * D).rearrange("p q (c d) -> p q c d", d=D)
        eb1 = lend(P, 2, FC)
        eb2 = lend(P, 2, D)
        ex_in = sb("ex_in", [P, 2, ETILES, 2 * D])
        ex_T = lend(D, CAP)
        ex_h = lend(P, FC, CAP)
        ex_y = lend(P, NE * ETILES, D)

        y_tok = memf[:, 0:NB * D]
        y_bad = memf[:, NB * D:2 * NB * D]
        y_fill = memf[:, 2 * NB * D:3 * NB * D]

        psA = ctx.enter_context(nc.psum_tensor("psA", [P, 512], F32))
        psB = ctx.enter_context(nc.psum_tensor("psB", [P, 1024], F32))
        psD = ctx.enter_context(nc.psum_tensor("psD", [P, 512], F32))
        psE = ctx.enter_context(nc.psum_tensor("psE", [P, 512], F32))
        psF = ctx.enter_context(nc.psum_tensor("psF", [P, 1024], F32))
        psH = ctx.enter_context(nc.psum_tensor("psH", [P, 512], F32))

        PK_BANKS = (psA, psD, psE, psB[:, 512:1024])
        level_bank = (psB[:, 0:STILES * LEVELS[0] * D], psH[:, 0:STILES * LEVELS[1] * D], psD[:, 0:STILES * LEVELS[2] * D])
        nodeT_bank = (psF[:, 0:STILES * LEVELS[1] * P], psE[:, 0:STILES * LEVELS[2] * P])

        tree_loaded, loaded = sem("tree_loaded"), sem("loaded")
        consts_done = sem("consts_done")
        pool_steps, pool_ticks = sem("pool_steps"), sem("pool_ticks")
        zero_filled = sem("zero_filled")
        wT_psum, wT_ready = sem("wT_psum"), sem("wT_ready")
        fold_psum, fold_ready = sem("fold_psum"), sem("fold_ready")
        compln_ready = sem("compln_ready")
        compT_psum, compT_ready = sem("compT_psum"), sem("compT_ready")
        beta_ready = sem("beta_ready")
        tab_psum, tab_ready = sem("tab_psum"), sem("tab_ready")
        dve_setup = sem("dve_setup")
        leaf_ids_loaded, op_ids_loaded = sem("leaf_ids_loaded"), sem("op_ids_loaded")
        leaf_hot_ready, op_hot_ready = sem("leaf_hot_ready"), sem("op_hot_ready")
        level_psum = [sem(f"level_psum{k}") for k in range(3)]
        node_ready = [sem(f"node_ready{k}") for k in range(2)]
        nodeT_psum, nodeT_ready = [[sem(f"{name}{k}") for k in range(2)] for name in ("nodeT_psum", "nodeT_ready")]
        roots_ready, root_stored = sem("roots_ready"), sem("root_stored")
        roots_masked, embedded_first, embedded = sem("roots_masked"), sem("embedded_first"), sem("embedded")
        dve_struct = sem("dve_struct")

        dve_pre = sem("dve_pre")
        hn_ready, hnT_psum, hnT_ready = sem("hn_ready"), sem("hnT_psum"), sem("hnT_ready")
        qT_psum, qT_ready, val_psum, val_ready = sem("qT_psum"), sem("qT_ready"), sem("val_psum"), sem("val_ready")
        s_psum, s_shifted, s_exp, p_ready = sem("s_psum"), sem("s_shifted"), sem("s_exp"), sem("p_ready")
        pT_psum, pT_ready, att_psum = sem("pT_psum"), sem("pT_ready"), sem("att_psum")
        x_ready, xT_psum, xT_ready, sim_psum = sem("x_ready"), sem("xT_psum"), sem("xT_ready"), sem("sim_psum")
        sim_read = sem("sim_read")
        w_shifted, w_exp, found = sem("w_shifted"), sem("w_exp"), sem("found")

        w_now_ready, q1T_psum, q1T_ready = sem("w_now_ready"), sem("q1T_psum"), sem("q1T_ready")
        rows_ready = sem("rows_ready")
        gathered = [sem(f"gathered{h}") for h in range(H)]

        dve_find, dve_tail, dve_dense = sem("dve_find"), sem("dve_tail"), sem("dve_dense")
        table_loaded, keys_shifted, keys_exp = sem("table_loaded"), sem("keys_shifted"), sem("keys_exp")
        spreadT_used = sem("spreadT_used")
        spread_ready, spreadT_psum, spreadT_ready = sem("spread_ready"), sem("spreadT_psum"), sem("spreadT_ready")
        diag_ready, kv_psum, kv_ready = sem("diag_ready"), sem("kv_psum"), sem("kv_ready")
        s1_read = sem("s1_read")
        s1_psum, s1_shifted, s1_exp, p1_ready = sem("s1_psum"), sem("s1_shifted"), sem("s1_exp"), sem("p1_ready")
        vo_psum, vo_ready = sem("vo_psum"), sem("vo_ready")
        p1T_psum, p1T_ready, att1_psum = sem("p1T_psum"), sem("p1T_ready"), sem("att1_psum")
        hk_ready, hkT_psum, hkT_ready = sem("hk_ready"), sem("hkT_psum"), sem("hkT_ready")
        kvr_psum, kvr_ready = sem("kvr_psum"), sem("kvr_ready")
        ex_shifted, ex_done, ysr_ready, ro_psum = sem("ex_shifted"), sem("ex_done"), sem("ysr_ready"), sem("ro_psum")
        h2_ready, h2T_psum, h2T_ready = sem("h2_ready"), sem("h2T_psum"), sem("h2T_ready")
        kk_psum, relu_done, kk_ready, ffn_psum = sem("kk_psum"), sem("relu_done"), sem("kk_ready"), sem("ffn_psum")
        kv_copied, sg_ready = sem("kv_copied"), sem("sg_ready")
        xm_ready, xmT_psum, xmT_ready = sem("xm_ready"), sem("xmT_psum"), sem("xmT_ready")
        gate_psum, lg_shifted, lg_exp = sem("gate_psum"), sem("lg_shifted"), sem("lg_exp")
        oh_ready, cum_psum, slot_ready = sem("oh_ready"), sem("cum_psum"), sem("slot_ready")
        scattered = sem("scattered")

        x_loaded, w1_loaded, w2_loaded = [[sem(f"{name}{q}") for q in range(2)] for name in ("x_loaded", "w1_loaded", "w2_loaded")]
        exT_psum, exT_ready = sem("exT_psum"), sem("exT_ready")
        eh_psum, eh_ready = sem("eh_psum"), sem("eh_ready")
        ey_psum, ey_ready, ey_stored = sem("ey_psum"), sem("ey_ready"), sem("ey_stored")
        y_gathered = [sem(f"y_gathered{g}") for g in range(YGROUPS)]
        dve_last, out_ready, out_stored = sem("dve_last"), sem("out_ready"), sem("out_stored")

        block = ctx.enter_context(nc.Block())
        loads = []

        def load(dst, src):
            loads.append((dst, src))

        for c in range(2):
            load(comp[:, c, :], t["L0_tok_comp_emb"][c * P:(c + 1) * P, :])
        load(opsb[:, :], t["L0_tok_op_emb"])
        load(wb0[:, :], t["L0_tok_W_bin"][0:D, :])
        load(wbL[:, :], t["L0_tok_W_bin"][D:2 * D, :])
        load(wbR[:, :], t["L0_tok_W_bin"][2 * D:3 * D, :])
        load(wbLR[:, :], t["L0_tok_W_bin"][D:3 * D, :])
        for k, name in enumerate(["L0_tok_gamma", "L0_tok_beta"]):
            for half in range(2):
                load(gb_cols[half * D:(half + 1) * D, k:k + 1], t[name].rearrange("(c o) -> c o", o=1))
        for k, name in enumerate(vec_names[:3]):
            load(vecs[:, k, :], t[name].partition_broadcast(P))
        tree_loads, loads = loads, []
        for k, name in enumerate(vec_names[3:]):
            load(vecs[:, 3 + k, :], t[name].partition_broadcast(P))
        load(gate_b[:, :], t["L1_ffn_gate_b"].partition_broadcast(P))
        for k, name in enumerate(["L0_attn_WQ", "L0_attn_WK", "L0_attn_WV", "L0_ffn_Wq_pk"]):
            load(heads_in[:, k, :], t[name])
        load(wout[:, :, :], t["L0_attn_Wout"].rearrange("(j p) o -> p j o", p=2 * D))
        load(pk_in[:, :, :], t["L0_ffn_pk_keys"].rearrange("p k h d -> k p (h d)"))
        load(wq1[0:D, :], t["L0_ffn_Wq"])
        load(wo1[D:P, :, :], t["L0_ffn_Wo"].rearrange("(h d) o -> d h o", d=D))
        for k, name in enumerate(sq_names):
            load(squares[0:D, k, :], t[name])
        load(wkf[:, :], t["L1_attn_Wk_ffn"])
        load(wvf[:, :, :], t["L1_attn_Wv_ffn"].rearrange("(c p) o -> p c o", p=P))
        load(gate_w[:, :], t["L1_ffn_gate_w"])
        load(wu[:, 0:1], t["L1_attn_spatial_decay"].rearrange("(c o) -> c o", o=1))
        load(wu[:, 1:2], t["L1_attn_spatial_first"].rearrange("(c o) -> c o", o=1))
        load(x_ids[:, :], t["x"].rearrange("b t -> t b"))
        ALL_TREE_LOADED, ALL_LOADED = 16 * len(tree_loads), 16 * len(loads)

        @block.sync
        def _(sp):
            leaf_rows = t["L0_tok_leaf_ids"].rearrange("(s p) n -> s (p n)", p=SP)
            op_rows = t["L0_tok_op_ids"].rearrange("(s p) n -> s (p n)", p=SP)

            def load_leaf_ids(s):
                sp.dma_start(leaf_ids[:, :], leaf_rows[bass.ds(s, 1), :].to_broadcast([P, SP * NLEAF])).then_inc(leaf_ids_loaded, 16)

            def load_op_ids(s):
                sp.dma_start(op_ids[:, :], op_rows[bass.ds(s, 1), :].to_broadcast([OPV, SP * NOPS])).then_inc(op_ids_loaded, 16)

            for dst, src in tree_loads:
                sp.dma_start(dst, src, allow_slow_non_contiguous=True).then_inc(tree_loaded, 16)
            load_leaf_ids(0)
            load_op_ids(0)
            for dst, src in loads:
                sp.dma_start(dst, src, allow_slow_non_contiguous=True).then_inc(loaded, 16)
            sp.wait_ge(consts_done, 1)
            for k in range(4):
                sp.dma_start(slots_x.rearrange("(a p r) d -> a p (r d)", a=4, p=P)[k], zeros).then_inc(zero_filled, 16)
            with sp.Fori(1, SROUNDS) as s:
                sp.wait_ge(leaf_hot_ready, s * 2)
                load_leaf_ids(s)
                sp.wait_ge(op_hot_ready, s * 2)
                load_op_ids(s)
            sp.wait_ge(roots_masked, 1)
            sp.dma_start(root_table.rearrange("(s p) d -> p s d", p=P), roots[:, :, :]).then_inc(root_stored, 16)
            sp.wait_ge(zero_filled, 64)
            for k in range(TABLE_LOADS):
                n = KEYS * KEYS // P // TABLE_LOADS
                part = (table_a, table_b[:, :, :])[k * n // TOPK][:, k * n % TOPK:k * n % TOPK + n, :]
                rows = t["kv_table"][k * n * P:(k + 1) * n * P, :]
                sp.dma_start(part, rows.rearrange("(c p) d -> p c d", p=P)).then_inc(table_loaded, 16)

            x_rows = slots_x.rearrange("(e j p) d -> e p j d", p=P, j=ETILES)
            y_rows = slots_y.rearrange("(e j p) d -> e p j d", p=P, j=ETILES)
            w2_rows = t["L1_ffn_w2"].rearrange("e (c p) d -> e p c d", p=P)
            b1_rows = t["L1_ffn_b1"].rearrange("e (c p) -> e p c", p=P)

            def load_x(e, q):
                sp.dma_start(ex_in[:, q, :, 0:D], x_rows[bass.ds(e, 1)].rearrange("a p j d -> (a p) j d")).then_inc(x_loaded[q], 16)

            def load_first_map(e, q):
                sp.dma_start(w1[:, q, :], t["L1_ffn_w1"][bass.ds(e, 1), :, :].rearrange("a d f -> (a d) f")).then_inc(w1_loaded[q], 16)
                sp.dma_start(eb1[:, q, :], b1_rows[bass.ds(e, 1)].rearrange("a p c -> (a p) c"),
                             allow_slow_non_contiguous=True).then_inc(w1_loaded[q], 16)

            def load_second_map(e, q):
                sp.dma_start(w2[:, q, :, :], w2_rows[bass.ds(e, 1)].rearrange("a p c d -> (a p) c d")).then_inc(w2_loaded[q], 16)
                sp.dma_start(eb2[:, q, :], t["L1_ffn_b2"][bass.ds(e, 1), :].to_broadcast([P, D])).then_inc(w2_loaded[q], 16)

            def store_y(e):
                sp.dma_start(y_rows[bass.ds(e, 1)].rearrange("a p j d -> (a p) j d"),
                             ex_y[:, bass.ds(e * ETILES, ETILES), :]).then_inc(ey_stored, 16)

            sp.wait_ge(kv_psum, NB * GH)
            for q in range(2):
                load_first_map(q, q)
                load_second_map(q, q)
            sp.wait_ge(scattered, 16 * NB)
            for q in range(2):
                load_x(q, q)
            with sp.Fori(0, NE // 2 - 1) as i:
                for q in range(2):
                    e = i * 2 + q
                    sp.wait_ge(exT_psum, e + 1)
                    load_x(e + 2, q)
                    sp.wait_ge(eh_ready, e * FC + FC)
                    load_first_map(e + 2, q)
                    sp.wait_ge(ey_ready, e + 1)
                    store_y(e)
                    load_second_map(e + 2, q)
            for e in (NE - 2, NE - 1):
                sp.wait_ge(ey_ready, e + 1)
                store_y(e)
            out_rows = out.rearrange("b t d -> t b d")
            for g in range(YGROUPS):
                sp.wait_ge(out_ready, g + 1)
                sp.dma_start(out_rows[:, g * YB:(g + 1) * YB, :],
                             hid[:, g * YB * D:(g + 1) * YB * D].rearrange("p (b d) -> p b d", d=D)).then_inc(out_stored, 16)
            sp.wait_ge(out_stored, 16 * YGROUPS)
            sp.wait_ge(zero_filled, 64)
            sp.wait_ge(ey_stored, 16 * NE)
            sp.wait_ge(root_stored, 16)

        @block.gpsimd
        def _(pool):
            st = Steps(pool, pool_steps)
            st.inc(pool.memset(ident[:, :], 0.0))
            st.inc(pool.memset(ones[:, :], 1.0))
            st.inc(pool.memset(upto[:, :], 1.0))
            st.inc(pool.memset(causal[:, :], 0.0))
            st.inc(pool.memset(zeros, 0.0))
            for pad in (hn[:, D:2 * D], hk[:, D:2 * D], xm[:, D:2 * D], ex_in[:, :, :, D:2 * D]):
                st.inc(pool.memset(pad, 0.0))
            st.settle()
            for pad in (wqk[D:P, :], wq1[D:P, :], squares[D:P, :, :]):
                st.inc(pool.memset(pad, 0.0))
            st.settle()
            st.inc(pool.iota(iota_cand[:, :], [[1, NCAND]], 0, 0, allow_small_or_imprecise_dtypes=True))
            for c in range(2):
                st.inc(pool.iota(iota_key[:, c, :], [[(1, KEYS)[c], KEYS]], 0, 0, allow_small_or_imprecise_dtypes=True))
            for i in range(TOPK):
                st.inc(pool.memset(offs[:, i:i + 1], float(OFFS[i])))
            st.inc(pool.memset(passed[:, TOPK:TOPK + 1], 0.0))
            st.inc(pool.iota(depth_rank[:, 1, :], [[1, TOPK]], -TOPK, 0, allow_small_or_imprecise_dtypes=True))
            st.inc(pool.iota(iota_e[:, :], [[1, NE]], 0, 0, allow_small_or_imprecise_dtypes=True))
            st.inc(pool.iota(rev_e[:, :], [[-1, NE]], NE, 0, allow_small_or_imprecise_dtypes=True))
            st.inc(pool.iota(iota_part[:, :], [[P, 2]], 0, 1, allow_small_or_imprecise_dtypes=True))
            st.inc(pool.iota(head_base[:, :, :], [[NUM_KV, H], [0, TOPK]], 0, 0, allow_small_or_imprecise_dtypes=True))
            st.settle()
            st.inc(pool.affine_select(out=ident[:, :], in_=ident[:, :], compare_op=ALU.not_equal, fill=1.0,
                                      base=0, pattern=[[-1, P]], channel_multiplier=1))
            st.inc(pool.affine_select(out=upto[:, :], in_=upto[:, :], compare_op=ALU.is_ge, fill=0.0,
                                      base=0, pattern=[[1, P]], channel_multiplier=-1))
            st.inc(pool.affine_select(out=causal[:, :], in_=causal[:, :], compare_op=ALU.is_ge, fill=NEG,
                                      base=0, pattern=[[-1, P]], channel_multiplier=1))
            st.settle()
            pool.memset(count[:, :], 0.0).then_inc(consts_done, 1)

            ticks = Steps(pool, pool_ticks)

            def tick():
                ticks.inc(pool.tensor_tensor(tick_pool[:, :], ones[:, 0:1], ones[:, 0:1], ALU.mult))
                ticks.restart()
                ticks.n = 0

            pool.wait_ge(loaded, ALL_LOADED)
            pool.wait_ge(root_stored, 16)
            for b in range(NB):
                pool.indirect_dma_start(out=hid[:, b * D:(b + 1) * D], out_offset=None, in_=root_table,
                                        in_offset=bass.IndirectOffsetOnAxis(ap=x_ids[:, b:b + 1], axis=0)).then_inc(embedded if b else embedded_first, 16)

            def scatter(b):
                pool.wait_ge(slot_ready, b + 1)
                tick()
                pool.indirect_dma_start(out=slots_x, out_offset=bass.IndirectOffsetOnAxis(ap=slot_s[:, 0:1], axis=0),
                                        in_=xm[:, 0:D], in_offset=None, bounds_check=SLOTS - 1,
                                        oob_is_err=False).then_inc(scattered, 16)

            def gather(b):
                for h in range(1, H):
                    if h in (1, H // 2):
                        if h > 1 and not (isinstance(b, int) and b < 2):
                            scatter(b - 2)
                        pool.wait_ge(rows_ready, b * 2 + (h // 4 + 1))
                        tick()
                    for k in range(TOPK):
                        c = h * TOPK + k
                        pool.indirect_dma_start(out=mem[:, h, k, :], out_offset=None, in_=t["kv_table"],
                                                in_offset=bass.IndirectOffsetOnAxis(ap=row_now[:, c:c + 1], axis=0)).then_inc(gathered[h], 16)

            gather(0)
            pool.wait_ge(zero_filled, 64)
            gather(1)
            with pool.Fori(1, NB // 2) as i:
                for q in range(2):
                    gather(i * 2 + q)
            scatter(NB - 2)
            scatter(NB - 1)

            pool.wait_ge(ey_stored, 16 * NE)
            for b in range(NB):
                pool.indirect_dma_start(out=y_tok[:, b * D:(b + 1) * D], out_offset=None, in_=slots_y,
                                        in_offset=bass.IndirectOffsetOnAxis(ap=slot_g[:, b:b + 1], axis=0)).then_inc(y_gathered[b // YB], 16)

        @block.vector
        def _(dve):
            V = nc.vector

            def norm(st, scratch, src, n, dst, gain=None, bias=None, done=None):
                ln_st, ln_mv, ln_v, ln_i, ln_y, ln_a = scratch
                for j in range(n):
                    st.inc(V.bn_stats(ln_st[:, j, :], src[:, j, :]))
                st.settle()
                for j in range(n):
                    st.inc(V.bn_aggr(ln_mv[:, j, :], ln_st[:, j, :]))
                st.settle()
                v, y, a = ln_v[:, 0:n], ln_y[:, 0:n].bitcast(F32), ln_a[:, 0:n]
                st.seq(V.tensor_scalar(v, ln_mv[:, 0:n, 1], EPS, None, ALU.add))
                st.seq(V.tensor_scalar(ln_i[:, 0:n], v.bitcast(I32), 1, None, ALU.logical_shift_right))
                st.seq(V.tensor_scalar(ln_y[:, 0:n], ln_i[:, 0:n], -1.0, MAGIC, ALU.mult, ALU.add))
                c = 1.0
                for _ in range(3):
                    st.seq(V.tensor_tensor(a, y, y, ALU.mult))
                    st.seq(V.tensor_tensor(a, a, v, ALU.mult))
                    st.seq(V.scalar_tensor_tensor(y, a, 3.0 * c * c, y, ALU.subtract, ALU.mult))
                    c = -2.0 * c * c * c
                st.seq(V.tensor_scalar(y, y, 1.0 / c, None, ALU.mult))
                for j in range(n):
                    i = V.tensor_scalar(dst[:, j, :], src[:, j, :], ln_mv[:, j, 0:1], y[:, j:j + 1], ALU.subtract, ALU.mult)
                    if j < n - 1:
                        st.inc(i)
                if gain is not None:
                    st.seq(i)
                    st.seq(V.tensor_tensor(dst, dst, rows_n(gain, n), ALU.mult))
                    i = V.tensor_tensor(dst, dst, rows_n(bias, n), ALU.add)
                if done is None:
                    st.seq(i)
                else:
                    i.then_inc(done, 1)

            def tick(st, k=0):
                st.seq(V.memset(tick_dve[:, k:k + 1], 0.0))

            def one(ap):
                return ap.unsqueeze(1)

            def leaf_one_hot(s):
                dve.wait_ge(leaf_ids_loaded, s * 16 + 16)
                leaves = leaf_ids[:, :].rearrange("p (s n) -> p n s", n=NLEAF)
                for c in range(2):
                    V.tensor_scalar(leaf_hot[:, c, :, :], leaves, iota_part[:, c:c + 1], None, ALU.is_equal).then_inc(leaf_hot_ready, 1)

            def op_one_hot(s, a, z):
                dve.wait_ge(op_ids_loaded, s * 16 + 16)
                V.tensor_scalar(op_hot[:, a:z, :], op_ids[:, :].rearrange("p (s n) -> p n s", n=NOPS)[:, a:z, :],
                                iota_part[0:OPV, 0:1], None, ALU.is_equal).then_inc(op_hot_ready, 1)

            st = Steps(dve, dve_setup)
            dve.wait_ge(tree_loaded, ALL_TREE_LOADED)
            dve.wait_ge(consts_done, 1)
            norm(st, ln_struct, comp[:, :, :], 2, compln[:, :, :], gamma, beta, compln_ready)
            V.tensor_scalar(wbLR_g[:, :], wbLR[:, :], gb_cols[:, 0:1], None, ALU.mult).then_inc(beta_ready, 1)
            V.tensor_scalar(beta_rep[:, :], ones[:, 0:OPV], gb_cols[:, 1:2], None, ALU.mult).then_inc(beta_ready, 1)
            st.inc(V.memset(tab[OPV:P, OP_LEAF:OP_UPPER + 1, :], 0.0))
            st.inc(V.memset(om[:, 0:1], -1e38))
            st.inc(V.memset(pst[:, 0:1], 0.0))
            st.inc(V.memset(qst[:, 0:1], 0.0))
            leaf_one_hot(0)
            dve.wait_ge(compT_psum, 1)
            V.tensor_copy(compT[:, :], psA[0:D, 0:2 * P]).then_inc(compT_ready, 1)
            V.tensor_copy(opT[:, :], psA[0:D, 2 * P:2 * P + OPV]).then_inc(compT_ready, 1)
            op_one_hot(0, 0, LEVELS[0])
            op_one_hot(0, LEVELS[0], NOPS)
            dve.wait_ge(tab_psum, 1)
            st.inc(V.tensor_copy(tab[:, LEFT:OP_LEAF, :], psD[:, 0:4 * D].rearrange("p (a d) -> p a d", d=D)))
            st.seq(V.tensor_tensor(tab[0:OPV, OP_LEAF, :], psD[0:OPV, 4 * D:5 * D], b_bin[0:OPV], ALU.add))
            st.seq(V.tensor_tensor(tab[0:OPV, OP_UPPER, :], tab[0:OPV, OP_LEAF, :], psD[0:OPV, 5 * D:6 * D], ALU.add))
            for part in range(3):
                i = V.tensor_copy(tab_parts[:, part, :, :], tab[:, :, :])
                if part < 2:
                    st.seq(i)
                    st.seq(V.tensor_tensor(tab[:, :, :], tab[:, :, :], tab_parts[:, part, :, :], ALU.subtract))
                else:
                    i.then_inc(tab_ready, 1)

            def normalise_level(s, k):
                st = Steps(dve, dve_struct)
                n = STILES * LEVELS[k]
                src = level_bank[k].rearrange("p (a d) -> p a d", d=D)
                dve.wait_ge(level_psum[k], s + 1)
                tick(st)
                if k < 2:
                    norm(st, ln_struct, src, n, node[k][:, :, :], done=node_ready[k])
                else:
                    norm(st, ln_struct, src, n, roots[:, bass.ds(s * STILES, STILES), :], gamma, beta, roots_ready)
                st.restart()

            def struct_round(s, more):
                normalise_level(s, 1)
                normalise_level(s + 1, 0)
                if more:
                    leaf_one_hot(s + 2)
                dve.wait_ge(level_psum[2], s + 1)
                op_one_hot(s + 1, LEVELS[0], NOPS)
                normalise_level(s, 2)
                if more:
                    op_one_hot(s + 2, 0, LEVELS[0])

            normalise_level(0, 0)
            leaf_one_hot(1)
            op_one_hot(1, 0, LEVELS[0])
            with dve.Fori(0, SROUNDS - 2) as s:
                struct_round(s, True)
            struct_round(SROUNDS - 2, False)
            normalise_level(SROUNDS - 1, 1)
            normalise_level(SROUNDS - 1, 2)
            dve.wait_ge(roots_ready, SROUNDS)
            V.memset(roots[0:2, 0, :], 0.0).then_inc(roots_masked, 1)
            dve.wait_ge(loaded, ALL_LOADED)
            st = Steps(dve, dve_struct)
            st.seq(V.tensor_scalar(wu[:, :], wu[:, :], 1.0 / P, None, ALU.mult))
            st.seq(V.tensor_scalar(wdec[:, :], ones[0:D, :], wu[:, 0:1], None, ALU.mult))
            st.restart()

            def softmax_bias(st, soft, src, scale, done):
                bias = soft[0]
                st.seq(V.tensor_reduce(bias[:, :], src, AX.X, ALU.max))
                V.tensor_scalar(bias[:, :], bias[:, :], -scale, None, ALU.mult).then_inc(done, 1)

            def softmax_scale(st, soft, buf, done):
                zs = soft[1]
                st.seq(V.reciprocal(zs[:, :], zs[:, :]))
                V.tensor_tensor(buf, buf, cast_cols(zs[:, :], P), ALU.mult).then_inc(done, 1)

            def pairs(st, dst, l0, l1):
                heads = dst.shape[1]
                for i in range(5):
                    n = ROWS[i]
                    st.inc(V.tensor_tensor(dst[:, :, OFFS[i]:OFFS[i] + n], l0[:, :, i:i + 1].to_broadcast([P, heads, n]),
                                           l1[:, :, 0:n], ALU.add))
                o = dst[:, :, OFFS[5]:OFFS[8]].rearrange("p h (i j) -> p h i j", j=2)
                st.inc(V.tensor_tensor(o, l0[:, :, 5:8].unsqueeze(3).to_broadcast([P, heads, 3, 2]),
                                       l1[:, :, 0:2].unsqueeze(2).to_broadcast([P, heads, 3, 2]), ALU.add))
                st.inc(V.tensor_tensor(dst[:, :, OFFS[8]:NCAND], l0[:, :, 8:16],
                                       l1[:, :, 0:1].to_broadcast([P, heads, 8]), ALU.add))

            def look_up(st, h0):
                qs = range(1 if h0 == 0 else 0, 2)
                for q in qs:
                    st.inc(V.tensor_tensor(hot[:, q, :, :], cast_cols(finp[:, h0 + q, :], NCAND),
                                           rows_n(iota_cand[:, :], TOPK), ALU.is_equal))
                st.settle()
                for q in qs:
                    st.inc(V.tensor_tensor(hot[:, q, :, :], hot[:, q, :, :],
                                           rows_n(candi[:, h0 + q, :], TOPK), ALU.mult))
                st.settle()
                for q in qs:
                    st.inc(V.tensor_reduce(rowf[:, h0 + q, :], hot[:, q, :, :], AX.X, ALU.add))
                st.settle()

            def find_rest(b):
                st = Steps(dve, dve_find)
                for h0 in range(H // 2, H, 2):
                    look_up(st, h0)
                    if h0 < H - 2:
                        yield
                if not (isinstance(b, int) and b == 0):
                    dve.wait_ge(kv_psum, b * GH)
                V.tensor_copy(row_now[:, H // 2 * TOPK:H * TOPK],
                              rowf[:, H // 2:H, :].rearrange("p h k -> p (h k)")).then_inc(rows_ready, 1)
                st.restart()
                yield

            def describe_head0(st):
                hotf = hot[:, :, :, :].rearrange("p q k c -> p (q k c)")
                past = hotf[:, 0:TOPK * TOPK].rearrange("p (i k) -> p i k", k=TOPK)
                at_key = hotf[:, 0:KEYS * TOPK].rearrange("p (i k) -> p i k", k=TOPK)
                st.seq(V.tensor_tensor(past, rows_n(finp[:, 0, :], TOPK), cast_cols(offs[:, :], TOPK), ALU.is_ge))
                st.seq(V.tensor_reduce(passed[:, 0:TOPK], past, AX.X, ALU.add))
                st.seq(V.tensor_tensor(depth_rank[:, 0, :], passed[:, 0:TOPK], passed[:, 1:TOPK + 1], ALU.subtract))
                for c in range(2):
                    st.seq(V.tensor_tensor(at_key, rows_n(topf[:, c * H, :], KEYS), cast_cols(iota_key[:, c, :], TOPK), ALU.is_equal))
                    st.seq(V.tensor_tensor(at_key, at_key, rows_n(depth_rank[:, c, :], KEYS), ALU.mult))
                    st.seq(V.tensor_reduce(by_key[:, (DEPTH, RANK)[c], :], at_key, AX.X, ALU.add))
                st.seq(V.tensor_scalar(by_key[:, DEPTH, :], by_key[:, DEPTH, :], float(-TOPK), None, ALU.add))

            def dense(b):
                st = Steps(dve, dve_dense)
                hotf = hot[:, :, :, :].rearrange("p q k c -> p (q k c)")
                for c in range(CHUNKS):
                    now, keys = spread[:, c % 2, :, :], slice(c * CKEYS, (c + 1) * CKEYS)
                    best = hotf[:, 0:CKEYS * KEYS].rearrange("p (j i) -> p j i", i=KEYS)
                    st.inc(V.tensor_tensor(best, rows_n(by_key_now[:, DEPTH, :], CKEYS),
                                           cast_cols(by_key_now[:, RANK, keys], KEYS), ALU.is_gt))
                    if c >= 2:
                        dve.wait_ge(spreadT_psum, b * CHUNKS + (c - 1))
                    st.inc(V.tensor_tensor(now, rows_n(by_key_now[:, EXP0, :], CKEYS),
                                           cast_cols(by_key_now[:, EXP1, keys], KEYS), ALU.mult))
                    st.settle()
                    V.tensor_tensor(now, now, best, ALU.mult).then_inc(spread_ready, 1)
                    dve.wait_ge(spread_ready, b * CHUNKS + (c + 1))
                    tick(st)
                    if c == CHUNKS - 1:
                        st.restart()
                    yield

            def pre(b):
                n = b + 1
                st = Steps(dve, dve_pre)
                hb = hid[:, bass.ds(b * D, D)]
                norm(st, ln_pre, one(hb), 1, one(hn[:, 0:D]), done=hn_ready)
                yield
                s3 = psB[:, :].rearrange("p (h t) -> p h t", h=H)
                dve.wait_ge(s_psum, n)
                softmax_bias(st, soft_pre, s3, SCALE0, s_shifted)
                yield
                dve.wait_ge(s_exp, n)
                softmax_scale(st, soft_pre, prob[:, :, :], p_ready)
                yield
                dve.wait_ge(att_psum, n)
                st.seq(V.tensor_tensor(att[:, :], psA[:, 0:D], bout, ALU.add))
                st.seq(V.tensor_tensor(hb, hb, att[:, :], ALU.add))
                norm(st, ln_pre, one(hb), 1, one(hn[:, 0:D]), done=x_ready)
                yield
                sp3 = psB[:, :].rearrange("p (u k) -> p u k", k=KEYS)
                dve.wait_ge(sim_psum, n)
                tick(st)
                for half in range(2):
                    heads = range(half * H // 2, (half + 1) * H // 2)
                    hs = slice(heads[0], heads[-1] + 1)
                    lists = [c * H + h for c in range(2) for h in heads]
                    for u in lists:
                        st.inc(V.max(top[:, u, 0:8], sp3[:, u, :]))
                    st.settle()
                    for u in lists:
                        st.inc(V.max_index(topi[:, u, 0:8], top[:, u, 0:8], sp3[:, u, :]))
                    for u in lists:
                        st.inc(V.match_replace(sim[:, u, :], top[:, u, 0:8], sp3[:, u, :], NEG))
                    st.settle()
                    for u in lists:
                        st.inc(V.max(top[:, u, 8:16], sim[:, u, :]))
                    st.settle()
                    for u in lists:
                        i = V.max_index(topi[:, u, 8:16], top[:, u, 8:16], sim[:, u, :])
                        st.inc(i) if half == 0 or u != lists[-1] else i.then_inc(sim_read, 1)
                    if half == 1:
                        dve.wait_ge(sim_read, n)
                    st.settle()
                    if half == 0:
                        own = [ap.rearrange("p (c h) k -> p c h k", c=2)[:, :, 0, :] for ap in (sp3, top[:, :, :])]
                        V.tensor_tensor(by_key[:, EXP0:EXP1 + 1, :], own[0], own[1][:, :, 0:1].to_broadcast([P, 2, KEYS]),
                                        ALU.subtract).then_inc(keys_shifted, 1)
                    yield
                    both = [ap[:, :, :].rearrange("p (c h) k -> p c h k", c=2)[:, :, hs] for ap in (topf, topi)]
                    st.seq(V.tensor_copy(both[0], both[1]))
                    t0, t1 = topf[:, hs, :], topf[:, H + hs.start:H + hs.stop, :]
                    st.inc(V.tensor_tensor(t0, t0, head_base[:, hs, :], ALU.add))
                    st.inc(V.tensor_scalar(t1, t1, float(KEYS), None, ALU.mult))
                    pairs(st, cand[:, hs, :], top[:, hs, :], top[:, H + hs.start:H + hs.stop, :])
                    st.settle()
                    pairs(st, candi[:, hs, :], t0, t1)
                    yield
                    for h in heads:
                        st.inc(V.max(fin[:, h, 0:8], cand[:, h, :]))
                    st.settle()
                    for h in heads:
                        st.inc(V.max_index(fini[:, h, 0:8], fin[:, h, 0:8], cand[:, h, :]))
                    for h in heads:
                        st.inc(V.match_replace(cand2[:, h, :], fin[:, h, 0:8], cand[:, h, :], NEG))
                    st.settle()
                    for h in heads:
                        st.inc(V.max(fin[:, h, 8:16], cand2[:, h, :]))
                    st.settle()
                    yield
                    if half == 1:
                        V.tensor_tensor(w_next[:, :, :], fin[:, :, :], fin[:, :, 0:1].to_broadcast([P, H, TOPK]),
                                        ALU.subtract).then_inc(w_shifted, 1)
                    for h in heads:
                        st.inc(V.max_index(fini[:, h, 8:16], fin[:, h, 8:16], cand2[:, h, :]))
                    st.settle()
                    st.seq(V.tensor_copy(finp[:, hs, :], fini[:, hs, :]))
                    if half == 0:
                        for h0 in heads[::2]:
                            if h0 == 0:
                                describe_head0(st)
                            look_up(st, h0)
                            if h0 == heads[-2]:
                                st.seq(V.tensor_copy(row_next[:, TOPK:H // 2 * TOPK],
                                                     rowf[:, 1:H // 2, :].rearrange("p h k -> p (h k)")))
                            yield
                yield
                dve.wait_ge(w_exp, n)
                st.seq(V.tensor_reduce(wz[:, :], w_next[:, :, :], AX.X, ALU.add))
                st.seq(V.reciprocal(wz[:, :], wz[:, :]))
                dve.wait_ge(keys_exp, n)
                tick(st)
                st.inc(V.tensor_scalar(by_key[:, EXP0, :], by_key[:, EXP0, :], wz[:, 0:1], None, ALU.mult))
                V.tensor_tensor(w_next[:, :, :], w_next[:, :, :], cast_cols(wz[:, :], TOPK), ALU.mult).then_inc(found, 1)
                st.restart()

            def commit():
                V.tensor_copy(row_now[:, TOPK:H // 2 * TOPK], row_next[:, TOPK:H // 2 * TOPK]).then_inc(rows_ready, 1)

            def carry(b):
                V.tensor_copy(by_key_now[:, :, :], by_key[:, :, :])
                V.tensor_copy(w_now[:, :, :], w_next[:, :, :]).then_inc(w_now_ready, 1)
                dve.wait_ge(w_now_ready, b + 1)

            def replace_rows(b):
                dve.wait_ge(kv_psum, b * GH + H // 2 - 1)
                commit()
                yield

            def tail(b):
                n = b + 1
                st = Steps(dve, dve_tail)
                dve.wait_ge(s1_psum, n)
                s3 = psF[:, :].rearrange("p (h t) -> p h t", h=H)
                V.tensor_tensor(prob1[:, :, :], s3, rows_n(causal[:, :], H), ALU.add).then_inc(s1_read, 1)
                dve.wait_ge(s1_read, n)
                softmax_bias(st, soft_tail, prob1[:, :, :], 1.0, s1_shifted)
                yield
                dve.wait_ge(s1_exp, n)
                softmax_scale(st, soft_tail, prob1[:, :, :], p1_ready)
                yield
                hb = hid[:, bass.ds(b * D, D)]
                dve.wait_ge(att1_psum, n)
                st.seq(V.tensor_tensor(hb, hb, psE[:, 0:D], ALU.add))
                norm(st, ln_tail, one(hb), 1, one(x3[:, :]))
                norm(st, ln_tail, one(x3[:, :]), 1, one(hk[:, 0:D]), g1, b1, hk_ready)
                yield
                dve.wait_ge(kv_copied, n)
                dve.wait_ge(kvr_ready, n)
                k, v, er = kvr[:, 0, :], kvr[:, 1, :], kvr[:, 2, :]
                o_old, o_new = om[:, 0:P], om[:, 1:P + 1]
                st.inc(V.tensor_tensor_scan(o_new, wdec[:, :], k, -1e38, ALU.add, ALU.max))
                st.inc(V.tensor_scalar(uk[:, :], k, wu[:, 1:2], None, ALU.add))
                st.inc(V.tensor_scalar(er, er, 1.0, None, ALU.add))
                st.settle()
                st.inc(V.tensor_tensor(nom[:, :], o_old, uk[:, :], ALU.max))
                st.inc(V.scalar_tensor_tensor(ex[:, 2, :], o_old, wu[:, 0:1], o_new, ALU.add, ALU.subtract))
                st.inc(V.tensor_tensor(ex[:, 3, :], k, o_new, ALU.subtract))
                st.inc(V.reciprocal(er, er))
                st.settle()
                st.inc(V.tensor_tensor(ex[:, 0, :], o_old, nom[:, :], ALU.subtract))
                V.tensor_tensor(ex[:, 1, :], uk[:, :], nom[:, :], ALU.subtract).then_inc(ex_shifted, 1)
                yield
                dve.wait_ge(ex_done, n)
                st.inc(V.tensor_tensor(ev[:, :], ex[:, 3, :], v, ALU.mult))
                st.inc(V.tensor_tensor_scan(qst[:, 1:P + 1], ex[:, 2, :], ex[:, 3, :], 0.0, ALU.mult, ALU.add))
                st.inc(V.tensor_tensor(num[:, :], ex[:, 1, :], v, ALU.mult))
                st.settle()
                st.inc(V.tensor_tensor_scan(pst[:, 1:P + 1], ex[:, 2, :], ev[:, :], 0.0, ALU.mult, ALU.add))
                st.inc(V.tensor_tensor(den[:, :], ex[:, 0, :], qst[:, 0:P], ALU.mult))
                st.settle()
                st.inc(V.tensor_tensor(ysr[:, :], ex[:, 0, :], pst[:, 0:P], ALU.mult))
                st.inc(V.tensor_tensor(den[:, :], den[:, :], ex[:, 1, :], ALU.add))
                st.settle()
                st.inc(V.tensor_tensor(num[:, :], num[:, :], ysr[:, :], ALU.add))
                st.inc(V.reciprocal(den[:, :], den[:, :]))
                st.settle()
                st.seq(V.tensor_tensor(num[:, :], num[:, :], den[:, :], ALU.mult))
                V.tensor_tensor(ysr[:, :], num[:, :], er, ALU.mult).then_inc(ysr_ready, 1)
                yield
                dve.wait_ge(ro_psum, n)
                st.seq(V.tensor_tensor(x4[:, :], x3[:, :], psE[:, 0:D], ALU.add))
                norm(st, ln_tail, one(x4[:, :]), 1, one(hk[:, 0:D]), g2, b2, h2_ready)
                yield
                dve.wait_ge(sg_ready, n)
                st.seq(V.tensor_scalar(sg[:, :], sg[:, :], 1.0, None, ALU.add))
                st.seq(V.reciprocal(sg[:, :], sg[:, :]))
                yield
                dve.wait_ge(ffn_psum, n)
                st.seq(V.tensor_tensor(sg[:, :], sg[:, :], psE[:, 0:D], ALU.mult))
                st.seq(V.tensor_tensor(x4[:, :], x4[:, :], sg[:, :], ALU.add))
                st.seq(V.tensor_tensor(hb, hb, x4[:, :], ALU.add))
                if not (isinstance(b, int) and b == 0):
                    dve.wait_ge(scattered, b * 16)
                    tick(st, 1)
                norm(st, ln_tail, one(hb), 1, one(xm[:, 0:D]), done=xm_ready)
                yield
                dve.wait_ge(gate_psum, n)
                st.seq(V.tensor_tensor(lg[:, :], psE[:, 0:NE], gate_b[:, :], ALU.add))
                st.seq(V.tensor_reduce(g4[:, 0:1], lg[:, :], AX.X, ALU.max))
                V.tensor_scalar(lg[:, :], lg[:, :], g4[:, 0:1], None, ALU.subtract).then_inc(lg_shifted, 1)
                yield
                dve.wait_ge(lg_exp, n)
                st.inc(V.tensor_reduce(g4[:, 0:1], lg[:, :], AX.X, ALU.max))
                st.inc(V.tensor_reduce(g4[:, 1:2], lg[:, :], AX.X, ALU.add))
                st.settle()
                st.inc(V.reciprocal(g4[:, 1:2], g4[:, 1:2]))
                st.seq(V.scalar_tensor_tensor(sc8[:, :], lg[:, :], g4[:, 0:1], rev_e[:, :], ALU.is_ge, ALU.mult))
                st.seq(V.tensor_reduce(g4[:, 2:3], sc8[:, :], AX.X, ALU.max))
                V.tensor_scalar(oh[:, :], sc8[:, :], g4[:, 2:3], None, ALU.is_equal).then_inc(oh_ready, 1)
                dve.wait_ge(oh_ready, n)
                st.inc(V.tensor_tensor(sc8[:, :], oh[:, :], iota_e[:, :], ALU.mult))
                yield
                dve.wait_ge(cum_psum, n)
                st.seq(V.tensor_tensor(cum[:, :], psE[:, 64:64 + NE], count[:, :], ALU.add))
                st.inc(V.tensor_tensor(cum[:, :], cum[:, :], oh[:, :], ALU.mult))
                st.inc(V.tensor_tensor(count[:, :], count[:, :], psE[:, 128:128 + NE], ALU.add))
                st.inc(V.tensor_reduce(g4[:, 3:4], sc8[:, :], AX.X, ALU.add))
                st.settle()
                st.seq(V.tensor_reduce(g4[:, 4:5], cum[:, :], AX.X, ALU.add))
                st.inc(V.tensor_scalar(g4[:, 5:6], g4[:, 4:5], float(CAP), None, ALU.is_le))
                st.inc(V.tensor_scalar(g4[:, 6:7], g4[:, 4:5], float(CAP), -1.0, ALU.min, ALU.add))
                st.inc(V.tensor_scalar(g4[:, 4:5], g4[:, 4:5], float(CAP), float(SLOTS), ALU.is_gt, ALU.mult))
                st.inc(V.tensor_scalar(g4[:, 3:4], g4[:, 3:4], float(CAP), None, ALU.mult))
                st.inc(V.tensor_scalar(g4[:, 0:1], g4[:, 0:1], g4[:, 1:2], None, ALU.mult))
                st.settle()
                st.inc(V.tensor_tensor(g4[:, 6:7], g4[:, 6:7], g4[:, 3:4], ALU.add))
                st.settle()
                V.tensor_tensor(slot_s[:, :], g4[:, 6:7], g4[:, 4:5], ALU.add).then_inc(slot_ready, 1)
                st.inc(V.tensor_copy(slot_g[:, bass.ds(b, 1)], g4[:, 6:7]))
                st.inc(V.tensor_tensor(keep[:, bass.ds(b, 1)], g4[:, 0:1], g4[:, 5:6], ALU.mult))
                st.restart()

            dve.wait_ge(embedded_first, 16)
            first = pre(0)
            for _ in range(HALF_FOUND):
                next(first)
            commit()
            weave(first)
            weave(find_rest(0))
            dve.wait_ge(rows_ready, 2)
            dve.wait_ge(embedded, 16 * (NB - 1))
            carry(0)
            weave(later(HALF_FOUND, replace_rows(0)), pre(1), later(DENSE_TURN, dense(0)))

            def batch(b):
                before = tail(b - 1)
                next(before)
                carry(b)
                weave(later(HALF_FOUND, replace_rows(b)), pre(b + 1), later(FIND_TURN, find_rest(b)), before, later(DENSE_TURN, dense(b)))

            batch(1)
            with dve.Fori(2, NB - 1) as b:
                batch(b)
            before = tail(NB - 2)
            next(before)
            carry(NB - 1)
            weave(before, later(FIND_TURN, find_rest(NB - 1)), later(DENSE_TURN, dense(NB - 1)))
            weave(tail(NB - 1))

            def copy_xT(e):
                dve.wait_ge(exT_psum, e + 1)
                V.tensor_copy(ex_T[:, 0:512], psA[0:D, :]).then_inc(exT_ready, 1)
                V.tensor_copy(ex_T[:, 512:CAP], psD[0:D, 0:CAP - 512]).then_inc(exT_ready, 1)

            def add_bias(e, q):
                dve.wait_ge(w2_loaded[q], (e - q) * 16 + 32)
                dve.wait_ge(ey_psum, e + 1)
                V.tensor_tensor(ex_y[:, bass.ds(e * ETILES, ETILES), :],
                                (psE, psH)[q][:, 0:ETILES * D].rearrange("p (j d) -> p j d", d=D),
                                rows_n(eb2[:, q, :], ETILES), ALU.add).then_inc(ey_ready, 1)

            copy_xT(0)
            with dve.Fori(0, NE // 2 - 1) as i:
                for q in range(2):
                    copy_xT(i * 2 + q + 1)
                    add_bias(i * 2 + q, q)
            copy_xT(NE - 1)
            add_bias(NE - 2, 0)
            add_bias(NE - 1, 1)

            st = Steps(dve, dve_last)
            for g in range(YGROUPS):
                dve.wait_ge(y_gathered[g], 16 * YB)
                c = slice(g * YB * D, (g + 1) * YB * D)
                y, bad, fill = y_tok[:, c], y_bad[:, 0:YB * D], y_fill[:, 0:YB * D]
                y3 = y.rearrange("p (b d) -> p b d", d=D)
                st.seq(V.tensor_tensor(y3, y3, cast_cols(keep[:, g * YB:(g + 1) * YB], D), ALU.mult))
                for op, x, value in ((ALU.not_equal, None, 0.0), (ALU.is_gt, HUGE, 1e4), (ALU.is_lt, -HUGE, -1e4)):
                    st.inc(V.memset(fill, value))
                    if x is None:
                        st.inc(V.tensor_tensor(bad.bitcast(I32), y, y, op))
                    else:
                        st.inc(V.tensor_scalar(bad.bitcast(I32), y, x, None, op))
                    st.settle()
                    st.seq(V.copy_predicated(y, bad.bitcast(I32), fill))
                V.tensor_tensor(hid[:, c], hid[:, c], y, ALU.add).then_inc(out_ready, 1)

        @block.scalar
        def _(act):
            A = nc.scalar

            def copy(dst, src, done, scale=1.0):
                A.activation(dst, src, ACT.Copy, scale=scale).then_inc(done, 1)

            def copy_nodeT(s, k):
                act.wait_ge(nodeT_psum[k], s + 1)
                copy(nodeT[k][:, :, :], nodeT_bank[k].rearrange("p (a t) -> p a t", t=P), nodeT_ready[k])

            act.wait_ge(wT_psum, 1)
            for a, z, bank in ((0, 16, psF), (16, 20, psH)):
                A.activation(wT[:, a:z, :], bank[:, 0:(z - a) * D].rearrange("p (a d) -> p a d", d=D), ACT.Copy).then_inc(wT_ready, 1)
            copy_nodeT(0, 0)
            act.wait_ge(fold_psum, 1)
            for g in range(2):
                for k, w in enumerate((wqk, wvo)):
                    A.activation(w[0:D, :].rearrange("c (j g d) -> c g j d", g=2, d=D)[:, g],
                                 psF[0:D, 512 * g + 256 * k:512 * g + 256 * k + 256].rearrange("c (j d) -> c j d", d=D),
                                 ACT.Copy).then_inc(fold_ready, 1)
            for g in range(4):
                A.activation(wpk[:, :].rearrange("c (j g k) -> c g j k", g=4, k=KEYS)[:, g],
                             PK_BANKS[g][0:D, 0:4 * KEYS].rearrange("c (j k) -> c j k", k=KEYS), ACT.Copy).then_inc(fold_ready, 1)
            with act.Fori(0, SROUNDS - 1) as s:
                copy_nodeT(s, 1)
                copy_nodeT(s + 1, 0)
            copy_nodeT(SROUNDS - 1, 1)

            def softmax_exp(dst, src, soft, scale, done):
                for h in range(H):
                    i = A.activation(dst[:, h, :], src[:, h, :], ACT.Exp, scale=scale, bias=soft[0][:, h:h + 1],
                                     accum_out=soft[1][:, h:h + 1])
                i.then_inc(done, 1)

            def pre(b):
                n = b + 1
                act.wait_ge(hnT_psum, n)
                copy(hnT[:, :], psA[:, 0:P], hnT_ready)
                act.wait_ge(qT_psum, n)
                copy(qT[:, :], psB[0:D, :], qT_ready)
                act.wait_ge(val_psum, n)
                copy(val[:, :], psD[:, :], val_ready)
                yield
                act.wait_ge(s_shifted, n)
                softmax_exp(prob, psB[:, :].rearrange("p (h t) -> p h t", h=H), soft_pre, SCALE0, s_exp)
                yield
                act.wait_ge(pT_psum, n)
                copy(probT[:, :, :], psB[:, :].rearrange("p (h t) -> p h t", h=H), pT_ready)
                yield
                act.wait_ge(xT_psum, n)
                copy(xT[:, :], psA[:, 0:P], xT_ready)
                for _ in range(2):
                    yield
                act.wait_ge(keys_shifted, n)
                A.activation(by_key[:, EXP0:EXP1 + 1, :], by_key[:, EXP0:EXP1 + 1, :], ACT.Exp).then_inc(keys_exp, 1)
                for _ in range(PRE_STEPS_PER_HALF + 2):
                    yield
                act.wait_ge(w_shifted, n)
                A.activation(w_next[:, :, :], w_next[:, :, :], ACT.Exp).then_inc(w_exp, 1)

            def carry(b):
                act.wait_ge(q1T_psum, b + 1)
                copy(q1T[:, :], psF[0:D, :], q1T_ready, scale=D ** -0.5)

            def dense(b):
                for c in range(CHUNKS):
                    act.wait_ge(spreadT_psum, b * CHUNKS + (c + 1))
                    if c:
                        act.wait_ge(spreadT_used, b * CHUNKS + c)
                    copy(spreadT[:, :, :], psF[:, c % 2 * 512:c % 2 * 512 + 512].rearrange("p (a t) -> p a t", t=P), spreadT_ready)
                    yield

            def mix(b):
                act.wait_ge(w_now_ready, b + 1)
                for h in range(1, H):
                    if h == H // 2:
                        copy_kvT(b, 0)
                    if h >= 3:
                        act.wait_ge(kv_psum, b * GH + (h - 2))
                    for k in range(TOPK):
                        i = A.activation(diag[:, h % 2, k, :], ident[:, :], ACT.Copy, scale=w_now[:, h, k:k + 1])
                    i.then_inc(diag_ready, 1)
                    yield

            def copy_kvT(b, half):
                hs = slice((1, H // 2)[half], (H // 2, H)[half])
                act.wait_ge(kv_psum, b * GH + (hs.stop - 1))
                copy(kvT[:, hs, :], psH[:, :].rearrange("p (h t) -> p h t", t=P)[:, hs.start % 4:], kv_ready)
                if half:
                    act.wait_ge(spreadT_used, b * CHUNKS + CHUNKS)
                    copy(kvT[:, 0, :], psD[:, 0:P], kv_ready)

            def tail(b):
                n = b + 1
                act.wait_ge(vo_psum, n)
                copy(vo[:, :], psH[:, :], vo_ready)
                act.wait_ge(s1_shifted, n)
                softmax_exp(prob1, prob1, soft_tail, 1.0, s1_exp)
                yield
                act.wait_ge(p1T_psum, n)
                copy(prob1T[:, :, :], psF[:, :].rearrange("p (h t) -> p h t", h=H), p1T_ready)
                yield
                act.wait_ge(hkT_psum, n)
                copy(hkT[:, :], psE[:, 0:P], hkT_ready)
                act.wait_ge(kvr_psum, n)
                A.activation(kvr[:, 0:2, :], psE[0:D, 0:2 * P].rearrange("p (a t) -> p a t", t=P), ACT.Copy).then_inc(kv_copied, 1)
                A.activation(kvr[:, 2, :], psE[0:D, 2 * P:3 * P], ACT.Exp, scale=-1.0).then_inc(kvr_ready, 1)
                yield
                act.wait_ge(ex_shifted, n)
                A.activation(ex[:, :, :], ex[:, :, :], ACT.Exp).then_inc(ex_done, 1)
                yield
                yield
                act.wait_ge(h2T_psum, n)
                copy(h2T[:, :], psE[0:D, 0:P], h2T_ready)
                act.wait_ge(kk_psum, n)
                A.activation(kk[:, :, :], psE[:, 0:HIDC * P].rearrange("p (c t) -> p c t", t=P), ACT.Relu).then_inc(relu_done, 1)
                A.activation(sg[:, :], psE[:, HIDC * P:HIDC * P + D], ACT.Exp, scale=-1.0).then_inc(sg_ready, 1)
                act.wait_ge(relu_done, n)
                A.activation(kk[:, :, :], kk[:, :, :], ACT.Square).then_inc(kk_ready, 1)
                yield
                yield
                act.wait_ge(xmT_psum, n)
                copy(xmT[:, :], psE[0:D, 0:P], xmT_ready)
                yield
                act.wait_ge(lg_shifted, n)
                A.activation(lg[:, :], lg[:, :], ACT.Exp).then_inc(lg_exp, 1)
                yield
                yield

            weave(pre(0))
            carry(0)
            weave(pre(1), later(DENSE_TURN + 1, dense(0)), later(MIX_TURN, mix(0)))
            copy_kvT(0, 1)
            with act.Fori(1, NB - 1) as b:
                before = tail(b - 1)
                next(before)
                carry(b)
                weave(pre(b + 1), before, later(DENSE_TURN + 1, dense(b)), later(MIX_TURN, mix(b)))
                copy_kvT(b, 1)
            before = tail(NB - 2)
            next(before)
            carry(NB - 1)
            weave(before, later(DENSE_TURN + 1, dense(NB - 1)), later(MIX_TURN, mix(NB - 1)))
            copy_kvT(NB - 1, 1)
            weave(tail(NB - 1))

            with act.Fori(0, NE // 2) as i:
                for q in range(2):
                    e = i * 2 + q
                    act.wait_ge(w1_loaded[q], i * 32 + 32)
                    for c in range(FC):
                        act.wait_ge(eh_psum, e * FC + (c + 1))
                        A.activation(ex_h[:, c, :], (psB, psF)[c][:, 0:CAP], ACT.Relu, bias=eb1[:, q, c:c + 1]).then_inc(eh_ready, 1)

        @block.tensor
        def _(pe):
            T = nc.tensor
            SPLIT = ((0, 512), (512, CAP))

            pe.wait_ge(compln_ready, 1)
            for c in range(2):
                T.transpose(psA[0:D, c * P:(c + 1) * P], compln[:, c, :], ident[:, :])
            T.transpose(psA[0:D, 2 * P:2 * P + OPV], opsb[:, :], ident[0:OPV, 0:OPV]).then_inc(compT_psum, 1)
            pe.wait_ge(compT_ready, 2)
            for c in range(2):
                T.matmul(psD[:, (LEFT + c) * D:(LEFT + c + 1) * D], compT[:, c * P:(c + 1) * P], wbL[:, :], start=True, stop=True)
                T.matmul(psD[:, (RIGHT + c) * D:(RIGHT + c + 1) * D], compT[:, c * P:(c + 1) * P], wbR[:, :], start=True, stop=True)
            T.matmul(psD[0:OPV, 4 * D:5 * D], opT[:, :], wb0[:, :], start=True, stop=True)
            pe.wait_ge(beta_ready, 2)
            T.matmul(psD[0:OPV, 5 * D:6 * D], beta_rep[:, :], wbLR[:, :], start=True, stop=True).then_inc(tab_psum, 1)
            pe.wait_ge(tab_ready, 1)

            def add_rows(o, hot, table, first, last):
                for part in range(3):
                    mm = T.matmul(o, hot, tab_parts[0:hot.shape[0], part, table, :],
                                  start=(first and part == 0), stop=(last and part == 2))
                return mm

            def leaf_level(s):
                pe.wait_ge(leaf_hot_ready, s * 2 + 2)
                pe.wait_ge(op_hot_ready, s * 2 + 1)
                for j in range(STILES):
                    tile = slice(j * P, (j + 1) * P)
                    for m in range(LEVELS[0]):
                        o = level_bank[0][:, (j * LEVELS[0] + m) * D:(j * LEVELS[0] + m + 1) * D]
                        for c in range(2):
                            add_rows(o, leaf_hot[:, c, 2 * m, tile], LEFT + c, c == 0, False)
                            add_rows(o, leaf_hot[:, c, 2 * m + 1, tile], RIGHT + c, False, False)
                        mm = add_rows(o, op_hot[:, m, tile], OP_LEAF, False, True)
                mm.then_inc(level_psum[0], 1)

            def upper_level(s, k):
                pe.wait_ge(node_ready[k - 1], s + 1)
                for m in range(STILES * LEVELS[k]):
                    mm = T.transpose(nodeT_bank[k - 1][:, m * P:(m + 1) * P],
                                     node[k - 1][:, 2 * m:2 * m + 2, :].rearrange("p a d -> p (a d)"), ident[:, :])
                mm.then_inc(nodeT_psum[k - 1], 1)
                pe.wait_ge(nodeT_ready[k - 1], s + 1)
                if k == 1:
                    pe.wait_ge(op_hot_ready, s * 2 + 2)
                for j in range(STILES):
                    for m in range(LEVELS[k]):
                        i = j * LEVELS[k] + m
                        o = level_bank[k][:, i * D:(i + 1) * D]
                        T.matmul(o, nodeT[k - 1][:, i, :], wbLR_g[:, :], start=True, stop=False)
                        mm = add_rows(o, op_hot[:, sum(LEVELS[:k]) + m, j * P:(j + 1) * P], OP_UPPER, False, True)
                mm.then_inc(level_psum[k], 1)

            leaf_level(0)
            pe.wait_ge(loaded, ALL_LOADED)
            pe.wait_ge(consts_done, 1)
            for k in range(20):
                if k < 16:
                    src = heads_in[:, k // 4, (k % 4) * P:(k % 4 + 1) * P]
                else:
                    src = pk_in[:, (k - 16) // 2, (k % 2) * P:(k % 2 + 1) * P]
                mm = T.transpose(psF[:, k * D:(k + 1) * D] if k < 16 else psH[:, (k - 16) * D:(k - 15) * D], src, ident[0:D, 0:D])
            mm.then_inc(wT_psum, 1)
            pe.wait_ge(wT_ready, 2)
            upper_level(0, 1)
            for h in range(H):
                r, j = slice(D * (h % 2), D * (h % 2) + D), h // 2
                o = psF[0:D, 512 * (h % 2):512 * (h % 2) + 512]
                T.matmul(o[:, j * D:(j + 1) * D], wT[r, j, :], wT[r, 4 + j, :], start=True, stop=True)
                T.matmul(o[:, (4 + j) * D:(5 + j) * D], wT[r, 8 + j, :], wout[r, j, :], start=True, stop=True)
            for u in range(2 * H):
                g, j = u % 4, u // 4
                r = slice(DKEY * g, DKEY * g + DKEY)
                mm = T.matmul(PK_BANKS[g][0:D, j * KEYS:(j + 1) * KEYS], wT[r, 12 + j, :], wT[r, 16 + j, :], start=True, stop=True)
            mm.then_inc(fold_psum, 1)
            pe.wait_ge(fold_ready, 8)
            with pe.Fori(0, SROUNDS - 1) as s:
                leaf_level(s + 1)
                upper_level(s, 2)
                upper_level(s + 1, 1)
            upper_level(SROUNDS - 1, 2)

            def pre(b):
                n = b + 1
                pe.wait_ge(hn_ready, n)
                T.transpose(psA[:, 0:P], hn[:, :], ident[:, :]).then_inc(hnT_psum, 1)
                pe.wait_ge(hnT_ready, n)
                if not (isinstance(b, int) and b == 0):
                    pe.wait_ge(sim_read, b)
                for h in range(H):
                    mm = T.matmul(psB[0:D, h * P:(h + 1) * P], wqk[:, h * D:(h + 1) * D], hnT[:, :], start=True, stop=True)
                mm.then_inc(qT_psum, 1)
                T.matmul(psD[:, :], hnT[0:D, :], wvo[:, :], start=True, stop=True).then_inc(val_psum, 1)
                pe.wait_ge(qT_ready, n)
                for h in range(H):
                    mm = T.matmul(psB[:, h * P:(h + 1) * P], qT[:, h * P:(h + 1) * P], hnT[0:D, :], start=True, stop=True)
                mm.then_inc(s_psum, 1)
                yield
                pe.wait_ge(val_ready, n)
                yield
                pe.wait_ge(p_ready, n)
                for h in range(H):
                    mm = T.transpose(psB[:, h * P:(h + 1) * P], prob[:, h, :], ident[:, :])
                mm.then_inc(pT_psum, 1)
                pe.wait_ge(pT_ready, n)
                for h in range(H):
                    mm = T.matmul(psA[:, 0:D], probT[:, h, :], val[:, h * D:(h + 1) * D], start=(h == 0), stop=(h == H - 1))
                mm.then_inc(att_psum, 1)
                yield
                pe.wait_ge(x_ready, n)
                T.transpose(psA[:, 0:P], hn[:, :], ident[:, :]).then_inc(xT_psum, 1)
                pe.wait_ge(xT_ready, n)
                for p in range(2):
                    mm = T.matmul(psB[:, p * 512:(p + 1) * 512], xT[0:D, :], wpk[:, p * 512:(p + 1) * 512], start=True, stop=True)
                mm.then_inc(sim_psum, 1)
                yield

            def carry(b):
                pe.wait_ge(xT_ready, b + 1)
                if not (isinstance(b, int) and b == 0):
                    pe.wait_ge(s1_read, b)
                for h in range(H):
                    mm = T.matmul(psF[0:D, h * P:(h + 1) * P], wq1[:, h * D:(h + 1) * D], xT[:, :], start=True, stop=True)
                mm.then_inc(q1T_psum, 1)
                pe.wait_ge(q1T_ready, b + 1)

            def dense(b):
                for c in range(CHUNKS + 1):
                    if c < CHUNKS:
                        pe.wait_ge(spread_ready, b * CHUNKS + (c + 1))
                        w = spread[:, c % 2, :, :].rearrange("p j i -> p (j i)")
                        for a in range(CTILES):
                            mm = T.transpose(psF[:, c % 2 * 512 + a * P:c % 2 * 512 + (a + 1) * P], w[:, a * P:(a + 1) * P], ident[:, :])
                        mm.then_inc(spreadT_psum, 1)
                    if c:
                        pe.wait_ge(spreadT_ready, b * CHUNKS + c)
                        for a in range(CTILES):
                            tile = (c - 1) * CTILES + a
                            rows = table_a[:, tile, :] if tile < TOPK else table_b[:, tile - TOPK, :]
                            mm = T.matmul(psD[:, 0:P], rows, spreadT[:, a, :], start=(tile == 0), stop=(tile == CHUNKS * CTILES - 1))
                        mm.then_inc(spreadT_used, 1)
                    yield

            def mix(b):
                for h in range(1, H):
                    if h == H // 2:
                        pe.wait_ge(kv_ready, b * 3 + 1)
                    pe.wait_ge(diag_ready, b * GH + h)
                    pe.wait_ge(gathered[h], b * 256 + 256)
                    for k in range(TOPK):
                        mm = T.matmul(psH[:, (h % 4) * P:(h % 4 + 1) * P], mem[:, h, k, :], diag[:, h % 2, k, :],
                                      start=(k == 0), stop=(k == TOPK - 1))
                    mm.then_inc(kv_psum, 1)
                    yield

            def tail(b):
                n = b + 1
                pe.wait_ge(kv_ready, b * 3 + 3)
                for h in range(H):
                    mm = T.matmul(psF[:, h * P:(h + 1) * P], q1T[:, h * P:(h + 1) * P], kvT[0:D, h, :], start=True, stop=True)
                mm.then_inc(s1_psum, 1)
                for h in range(H):
                    mm = T.matmul(psH[:, h * D:(h + 1) * D], kvT[D:P, h, :], wo1[D:P, h, :], start=True, stop=True)
                mm.then_inc(vo_psum, 1)
                yield
                pe.wait_ge(p1_ready, n)
                for h in range(H):
                    mm = T.transpose(psF[:, h * P:(h + 1) * P], prob1[:, h, :], ident[:, :])
                mm.then_inc(p1T_psum, 1)
                pe.wait_ge(p1T_ready, n)
                pe.wait_ge(vo_ready, n)
                for h in range(H):
                    mm = T.matmul(psE[:, 0:D], prob1T[:, h, :], vo[:, h * D:(h + 1) * D], start=(h == 0), stop=(h == H - 1))
                mm.then_inc(att1_psum, 1)
                yield
                pe.wait_ge(hk_ready, n)
                T.transpose(psE[:, 0:P], hk[:, :], ident[:, :]).then_inc(hkT_psum, 1)
                pe.wait_ge(hkT_ready, n)
                for k, w in enumerate((rk, rv, rr)):
                    mm = T.matmul(psE[0:D, k * P:(k + 1) * P], w, hkT[:, :], start=True, stop=True)
                mm.then_inc(kvr_psum, 1)
                yield
                yield
                pe.wait_ge(ysr_ready, n)
                T.matmul(psE[:, 0:D], ysr[:, :], ro[0:D], start=True, stop=True).then_inc(ro_psum, 1)
                yield
                pe.wait_ge(h2_ready, n)
                T.transpose(psE[:, 0:P], hk[:, :], ident[:, :]).then_inc(h2T_psum, 1)
                pe.wait_ge(h2T_ready, n)
                for c in range(HIDC):
                    T.matmul(psE[:, c * P:(c + 1) * P], wkf[:, c * P:(c + 1) * P], h2T[:, :], start=True, stop=True)
                T.matmul(psE[:, HIDC * P:HIDC * P + D], h2T[:, :], rrf[0:D], start=True, stop=True).then_inc(kk_psum, 1)
                yield
                pe.wait_ge(kk_ready, n)
                pe.wait_ge(sg_ready, n)
                for c in range(HIDC):
                    mm = T.matmul(psE[:, 0:D], kk[:, c, :], wvf[:, c, :], start=(c == 0), stop=(c == HIDC - 1))
                mm.then_inc(ffn_psum, 1)
                yield
                pe.wait_ge(xm_ready, n)
                T.transpose(psE[:, 0:P], xm[:, :], ident[:, :]).then_inc(xmT_psum, 1)
                pe.wait_ge(xmT_ready, n)
                T.matmul(psE[:, 0:NE], xmT[:, :], gate_w[:, :], start=True, stop=True).then_inc(gate_psum, 1)
                yield
                yield
                pe.wait_ge(oh_ready, n)
                T.matmul(psE[:, 64:64 + NE], upto[:, :], oh[:, :], start=True, stop=True)
                T.matmul(psE[:, 128:128 + NE], ones[:, :], oh[:, :], start=True, stop=True).then_inc(cum_psum, 1)

            pe.wait_ge(roots_ready, SROUNDS)
            weave(pre(0))
            pe.wait_ge(table_loaded, 16 * TABLE_LOADS)
            carry(0)
            weave(pre(1), later(DENSE_TURN + 1, dense(0)), later(MIX_TURN + 1, mix(0)))
            with pe.Fori(1, NB - 1) as b:
                before = tail(b - 1)
                next(before)
                carry(b)
                weave(pre(b + 1), before, later(DENSE_TURN + 1, dense(b)), later(MIX_TURN + 1, mix(b)))
            before = tail(NB - 2)
            next(before)
            carry(NB - 1)
            weave(before, later(DENSE_TURN + 1, dense(NB - 1)), later(MIX_TURN + 1, mix(NB - 1)))
            weave(tail(NB - 1))

            def transpose_x(e, q):
                pe.wait_ge(x_loaded[q], (e - q) * 8 + 16)
                for j in range(ETILES):
                    o = psA[:, j * P:(j + 1) * P] if j < 4 else psD[:, 0:P]
                    mm = T.transpose(o, ex_in[:, q, j, :], ident[:, :])
                mm.then_inc(exT_psum, 1)

            def first_map(e, q):
                pe.wait_ge(w1_loaded[q], (e - q) * 16 + 32)
                pe.wait_ge(exT_ready, e * 2 + 2)
                for c in range(FC):
                    for a, z in SPLIT:
                        mm = T.matmul((psB, psF)[c][:, a:z], w1[:, q, c * P:(c + 1) * P], ex_T[:, a:z], start=True, stop=True)
                    mm.then_inc(eh_psum, 1)

            def second_map(e, q):
                pe.wait_ge(w2_loaded[q], (e - q) * 16 + 32)
                pe.wait_ge(eh_ready, e * FC + FC)
                for j in range(ETILES):
                    for c in range(FC):
                        mm = T.matmul((psE, psH)[q][:, j * D:(j + 1) * D], ex_h[:, c, j * P:(j + 1) * P], w2[:, q, c, :],
                                      start=(c == 0), stop=(c == FC - 1))
                mm.then_inc(ey_psum, 1)

            transpose_x(0, 0)
            with pe.Fori(0, NE // 2 - 1) as i:
                for q in range(2):
                    e = i * 2 + q
                    first_map(e, q)
                    transpose_x(e + 1, 1 - q)
                    second_map(e, q)
            first_map(NE - 2, 0)
            transpose_x(NE - 1, 1)
            second_map(NE - 2, 0)
            first_map(NE - 1, 1)
            second_map(NE - 1, 1)


_KV = ("L0_ffn_keys_table", "L0_ffn_values_table")


def kernel(**inputs):
    import concourse.bacc as _bacc
    from concourse.bass_utils import run_bass_kernel_spmd as _run

    nc = _bacc.Bacc("TRN2", target_bir_lowering=False, num_devices=1)
    given = {k: np.ascontiguousarray(v) for k, v in inputs.items() if k not in _KV}
    given["kv_table"] = np.concatenate([np.asarray(inputs[k]) for k in _KV], axis=1)
    arrays, aps = {}, {}
    for name, a in given.items():
        arrays[f"in_{name}"] = a
        aps[name] = nc.dram_tensor(f"in_{name}", a.shape, mybir.dt.from_np(a.dtype), kind="ExternalInput").ap()
    out = nc.dram_tensor("out_0", (NB, P, D), F32, kind="ExternalOutput").ap()
    tower(nc, aps, out)
    r = _run(nc, [arrays], core_ids=[0])
    return r.results[0]["out_0"]
```
